# Optimizing a Trainium2 kernel written in Bass

```python
import numpy as np
import jax
import jax.numpy as jnp

def _softmax(x, axis=-1):
    return jax.nn.softmax(x, axis=axis)

def _gelu(x):
    return jax.nn.gelu(x, approximate=True)

def _silu(x):
    return jax.nn.silu(x)

def _sigmoid(x):
    return jax.nn.sigmoid(x)

def _layernorm(x, axis=-1, eps=1e-05):
    m = jnp.mean(x, axis=axis, keepdims=True)
    v = jnp.var(x, axis=axis, keepdims=True)
    return (x - m) / jnp.sqrt(v + eps)

def _scatter_add(tgt, idx, src, axis=0):
    return tgt.at[idx].add(src)

def _segment_sum(src, seg, n):
    return jax.ops.segment_sum(src, seg, n)
kernel_name = 'mk_gnn_preln_d4_gnn_r8_92187a'

def setup_inputs(seed: int=0):
    np.random.seed(seed)
    _w = jnp.asarray

    def _rec_inputs():
        import jax
        import jax.numpy as jnp
        _gk = jax.random.key(seed)
        x = -0.000202 + 1 * jax.random.normal(jax.random.fold_in(_gk, 1), (6250, 64), jnp.float32)
        _s = jax.random.randint(jax.random.fold_in(_gk, 2), (100000,), 0, 6250, jnp.int32)
        _d = jax.random.randint(jax.random.fold_in(_gk, 3), (100000,), 0, 6250, jnp.int32)
        _loop = jnp.arange(6250, dtype=jnp.int32)
        src = jnp.concatenate([_s, _d, _loop])
        dst = jnp.concatenate([_d, _s, _loop])
        _o = jnp.argsort(dst, stable=True)
        src = src[_o]
        dst = dst[_o]
        edge_attr_48 = 5.93493e-05 + 1.00006 * jax.random.normal(jax.random.fold_in(_gk, 12), (206250, 48), jnp.float32)
        edge_type_3 = jax.random.randint(jax.random.fold_in(_gk, 14), (206250,), 0, 3, jnp.int32)
        return (x, src, dst, edge_attr_48, edge_type_3)
    x, src, dst, edge_attr_48, edge_type_3 = _rec_inputs()

    def _L0_gnn_setup():
        import jax, jax.numpy as jnp
        import numpy as np
        N_NODES = 12500
        N_EDGES = 200000
        NODE_IN = 64
        EDGE_OUT = 48
        HIDDEN = 256
        NODE_OUT = 64

        def scatter_mean(src, index, dim_size):
            s = jax.ops.segment_sum(src, index, num_segments=dim_size)
            cnt = jax.ops.segment_sum(jnp.ones((src.shape[0],), src.dtype), index, num_segments=dim_size)
            return s / jnp.maximum(cnt, 1.0)[:, None]
        key = jax.random.key(seed)
        ks = jax.random.split(key, 8)
        x = jax.random.normal(ks[0], (N_NODES, NODE_IN), dtype=jnp.float32)
        edge_index = jax.random.randint(ks[1], (2, N_EDGES), 0, N_NODES, dtype=jnp.int64)
        edge_attr = jax.random.normal(ks[2], (N_EDGES, EDGE_OUT), dtype=jnp.float32)
        u = jax.random.normal(ks[3], (1, 16), dtype=jnp.float32)
        batch = jnp.zeros((N_NODES,), dtype=jnp.int64)
        fan1 = NODE_IN + EDGE_OUT
        W1 = jax.random.uniform(ks[4], (fan1, HIDDEN), minval=-1.0, maxval=1.0) / np.sqrt(fan1)
        b1 = jax.random.uniform(ks[5], (HIDDEN,), minval=-1.0, maxval=1.0) / np.sqrt(fan1)
        W2 = jax.random.uniform(ks[6], (HIDDEN, NODE_OUT), minval=-1.0, maxval=1.0) / np.sqrt(HIDDEN)
        b2 = jax.random.uniform(ks[7], (NODE_OUT,), minval=-1.0, maxval=1.0) / np.sqrt(HIDDEN)
        return {'x': x, 'edge_index': edge_index, 'edge_attr': edge_attr, 'u': u, 'batch': batch, 'W1': W1, 'b1': b1, 'W2': W2, 'b2': b2}
    _L0_gnn_all = _L0_gnn_setup()
    _L0_gnn_in = {k: v for k, v in _L0_gnn_all.items() if k in ('u', 'W1', 'b1', 'W2', 'b2')}
    del _L0_gnn_all

    def _L1_gnn_setup():
        import jax, jax.numpy as jnp
        import numpy as np
        N_NODES = 12500
        key = jax.random.key(seed)
        k1, k2, k3 = jax.random.split(key, 3)
        x = jax.random.normal(k1, (N_NODES, 64), dtype=jnp.float32)
        edge_index = jax.random.randint(k2, (2, 156250), 0, N_NODES, dtype=jnp.int64)
        W = jax.random.normal(k3, (128, 64), dtype=jnp.float32) * (1.0 / np.sqrt(128.0))
        b = jnp.zeros((64,), dtype=jnp.float32)
        return {'x': x, 'edge_index': edge_index, 'W': W, 'b': b}
    _L1_gnn_all = _L1_gnn_setup()
    _L1_gnn_in = {k: v for k, v in _L1_gnn_all.items() if k in ('W', 'b')}
    del _L1_gnn_all

    def _L2_gnn_setup():
        import jax, jax.numpy as jnp
        import numpy as np
        N, E, D, H = (6250, 62500, 64, 8)
        LN_EPS = 1e-05
        SM_EPS = 1e-16
        SLOPE = 0.2

        def layer_norm(x, g, b):
            mu = jnp.mean(x, axis=-1, keepdims=True)
            var = jnp.mean((x - mu) ** 2, axis=-1, keepdims=True)
            return (x - mu) * jax.lax.rsqrt(var + LN_EPS) * g + b
        key = jax.random.key(seed)
        ks = jax.random.split(key, 12)
        glorot = lambda k, shape: jax.random.normal(k, shape, jnp.float32) * np.sqrt(2.0 / (shape[0] + shape[-1]))
        return {'x': jax.random.normal(ks[0], (N, D), jnp.float32), 'edge_index': jax.random.randint(ks[1], (2, E), 0, N, jnp.int64), 'W_att': glorot(ks[2], (D, H * D)), 'att_src': glorot(ks[3], (H, D)), 'att_dst': glorot(ks[4], (H, D)), 'bias_att': jnp.zeros((D,), jnp.float32), 'W1': glorot(ks[5], (D, 2 * D)), 'b1': jnp.zeros((2 * D,), jnp.float32), 'W2': glorot(ks[6], (2 * D, D)), 'b2': jnp.zeros((D,), jnp.float32), 'ln1_g': jnp.ones((D,), jnp.float32), 'ln1_b': jnp.zeros((D,), jnp.float32), 'ln2_g': jnp.ones((D,), jnp.float32), 'ln2_b': jnp.zeros((D,), jnp.float32)}
    _L2_gnn_all = _L2_gnn_setup()
    _L2_gnn_in = {k: v for k, v in _L2_gnn_all.items() if k in ('W_att', 'att_src', 'att_dst', 'bias_att', 'W1', 'b1', 'W2', 'b2', 'ln1_g', 'ln1_b', 'ln2_g', 'ln2_b')}
    del _L2_gnn_all

    def _L3_gnn_setup():
        import jax, jax.numpy as jnp
        import numpy as np
        N_NODES = 12500
        N_EDGES = 125000
        IN_DIM = 64
        OUT_DIM = 64
        NUM_REL = 3
        key = jax.random.key(seed)
        ks = jax.random.split(key, 6)
        x = jax.random.normal(ks[0], (N_NODES, IN_DIM), dtype=jnp.float32)
        edge_index = jax.random.randint(ks[1], (2, N_EDGES), 0, N_NODES, dtype=jnp.int64)
        edge_type = jax.random.randint(ks[2], (N_EDGES,), 0, NUM_REL, dtype=jnp.int64)
        scale = 1.0 / np.sqrt(IN_DIM)
        W_rel = jax.random.uniform(ks[3], (NUM_REL, OUT_DIM, IN_DIM), dtype=jnp.float32, minval=-scale, maxval=scale)
        W_self = jax.random.uniform(ks[4], (OUT_DIM, IN_DIM), dtype=jnp.float32, minval=-scale, maxval=scale)
        b_self = jax.random.uniform(ks[5], (OUT_DIM,), dtype=jnp.float32, minval=-scale, maxval=scale)
        return {'x': x, 'edge_index': edge_index, 'edge_type': edge_type, 'W_rel': W_rel, 'W_self': W_self, 'b_self': b_self}
    _L3_gnn_all = _L3_gnn_setup()
    _L3_gnn_in = {k: v for k, v in _L3_gnn_all.items() if k in ('W_rel', 'W_self', 'b_self')}
    del _L3_gnn_all
    return {'x': x, 'src': src, 'dst': dst, 'edge_attr_48': edge_attr_48, 'edge_type_3': edge_type_3, 'L0_gnn_u': _L0_gnn_in['u'], 'L0_gnn_W1': _L0_gnn_in['W1'], 'L0_gnn_b1': _L0_gnn_in['b1'], 'L0_gnn_W2': _L0_gnn_in['W2'], 'L0_gnn_b2': _L0_gnn_in['b2'], 'L1_gnn_W': _L1_gnn_in['W'], 'L1_gnn_b': _L1_gnn_in['b'], 'L2_gnn_W_att': _L2_gnn_in['W_att'], 'L2_gnn_att_src': _L2_gnn_in['att_src'], 'L2_gnn_att_dst': _L2_gnn_in['att_dst'], 'L2_gnn_bias_att': _L2_gnn_in['bias_att'], 'L2_gnn_W1': _L2_gnn_in['W1'], 'L2_gnn_b1': _L2_gnn_in['b1'], 'L2_gnn_W2': _L2_gnn_in['W2'], 'L2_gnn_b2': _L2_gnn_in['b2'], 'L2_gnn_ln1_g': _L2_gnn_in['ln1_g'], 'L2_gnn_ln1_b': _L2_gnn_in['ln1_b'], 'L2_gnn_ln2_g': _L2_gnn_in['ln2_g'], 'L2_gnn_ln2_b': _L2_gnn_in['ln2_b'], 'L3_gnn_W_rel': _L3_gnn_in['W_rel'], 'L3_gnn_W_self': _L3_gnn_in['W_self'], 'L3_gnn_b_self': _L3_gnn_in['b_self']}

def reference(x, src, dst, edge_attr_48, edge_type_3, L0_gnn_u, L0_gnn_W1, L0_gnn_b1, L0_gnn_W2, L0_gnn_b2, L1_gnn_W, L1_gnn_b, L2_gnn_W_att, L2_gnn_att_src, L2_gnn_att_dst, L2_gnn_bias_att, L2_gnn_W1, L2_gnn_b1, L2_gnn_W2, L2_gnn_b2, L2_gnn_ln1_g, L2_gnn_ln1_b, L2_gnn_ln2_g, L2_gnn_ln2_b, L3_gnn_W_rel, L3_gnn_W_self, L3_gnn_b_self):
    import jax
    import jax.numpy as jnp

    def _L0_gnn_ref(x, edge_index, edge_attr, u, batch, W1, b1, W2, b2):
        import jax, jax.numpy as jnp
        import numpy as np
        N_NODES = 12500
        N_EDGES = 200000
        NODE_IN = 64
        EDGE_OUT = 48
        HIDDEN = 256
        NODE_OUT = 64

        def scatter_mean(src, index, dim_size):
            s = jax.ops.segment_sum(src, index, num_segments=dim_size)
            cnt = jax.ops.segment_sum(jnp.ones((src.shape[0],), src.dtype), index, num_segments=dim_size)
            return s / jnp.maximum(cnt, 1.0)[:, None]
        edge_attr_agg = scatter_mean(edge_attr, edge_index[0], x.shape[0])
        combined = jnp.concatenate([x, edge_attr_agg], axis=1)
        h = jax.nn.relu(combined @ W1 + b1)
        return h @ W2 + b2

    def _L1_gnn_ref(x, edge_index, W, b):
        import jax, jax.numpy as jnp
        import numpy as np
        N_NODES = 12500
        n = x.shape[0]
        row, col = (edge_index[0], edge_index[1])
        neigh = jax.ops.segment_sum(x[row], col, num_segments=n)
        count = jax.ops.segment_sum(jnp.ones_like(col, dtype=x.dtype), col, num_segments=n)
        count = jnp.where(count == 0, jnp.asarray(1.0, x.dtype), count)
        neigh = neigh / count[:, None]
        x_aggr = jnp.concatenate([x, neigh], axis=-1)
        out = x_aggr @ W + b
        return jax.nn.relu(out)

    def _L2_gnn_ref(x, edge_index, W_att, att_src, att_dst, bias_att, W1, b1, W2, b2, ln1_g, ln1_b, ln2_g, ln2_b):
        import jax, jax.numpy as jnp
        import numpy as np
        N, E, D, H = (6250, 62500, 64, 8)
        LN_EPS = 1e-05
        SM_EPS = 1e-16
        SLOPE = 0.2

        def layer_norm(x, g, b):
            mu = jnp.mean(x, axis=-1, keepdims=True)
            var = jnp.mean((x - mu) ** 2, axis=-1, keepdims=True)
            return (x - mu) * jax.lax.rsqrt(var + LN_EPS) * g + b
        n = x.shape[0]
        h = (x @ W_att).reshape(n, H, D)
        a_src = jnp.einsum('nhc,hc->nh', h, att_src)
        a_dst = jnp.einsum('nhc,hc->nh', h, att_dst)
        loops = jnp.arange(n, dtype=edge_index.dtype)
        src = jnp.concatenate([edge_index[0], loops])
        dst = jnp.concatenate([edge_index[1], loops])
        e = a_src[src] + a_dst[dst]
        e = jnp.where(e > 0, e, SLOPE * e)
        m = jax.ops.segment_max(e, dst, num_segments=n)
        e = jnp.exp(e - m[dst])
        s = jax.ops.segment_sum(e, dst, num_segments=n)
        alpha = e / (s[dst] + SM_EPS)
        msg = alpha[:, :, None] * h[src]
        out = jax.ops.segment_sum(msg, dst, num_segments=n)
        att_out = out.mean(axis=1) + bias_att
        x1 = layer_norm(att_out + x, ln1_g, ln1_b)
        ff = jax.nn.relu(x1 @ W1 + b1) @ W2 + b2
        return layer_norm(ff + x1, ln2_g, ln2_b)

    def _L3_gnn_ref(x, edge_index, edge_type, W_rel, W_self, b_self):
        import jax, jax.numpy as jnp
        import numpy as np
        N_NODES = 12500
        N_EDGES = 125000
        IN_DIM = 64
        OUT_DIM = 64
        NUM_REL = 3
        out = x @ W_self.T + b_self
        src = x[edge_index[0]]
        msg = jnp.zeros((src.shape[0], W_rel.shape[1]), dtype=x.dtype)
        for r in range(W_rel.shape[0]):
            msg = msg + jnp.where((edge_type == r)[:, None], src @ W_rel[r].T, 0.0)
        out = out.at[edge_index[1]].add(msg)
        return jax.nn.relu(out)
    edge_index = jnp.stack([src, dst])
    batch0 = jnp.zeros((6250,), jnp.int32)
    h = jnp.maximum(_layernorm(x, axis=-1), 0.0)
    x = x + _L0_gnn_ref(h, edge_index, edge_attr_48, L0_gnn_u, batch0, L0_gnn_W1, L0_gnn_b1, L0_gnn_W2, L0_gnn_b2)
    h = jnp.maximum(_layernorm(x, axis=-1), 0.0)
    x = x + _L1_gnn_ref(h, edge_index, L1_gnn_W, L1_gnn_b)
    h = jnp.maximum(_layernorm(x, axis=-1), 0.0)
    x = x + _L2_gnn_ref(h, edge_index, L2_gnn_W_att, L2_gnn_att_src, L2_gnn_att_dst, L2_gnn_bias_att, L2_gnn_W1, L2_gnn_b1, L2_gnn_W2, L2_gnn_b2, L2_gnn_ln1_g, L2_gnn_ln1_b, L2_gnn_ln2_g, L2_gnn_ln2_b)
    h = jnp.maximum(_layernorm(x, axis=-1), 0.0)
    x = x + _L3_gnn_ref(h, edge_index, edge_type_3, L3_gnn_W_rel, L3_gnn_W_self, L3_gnn_b_self)
    return x

_drawn_inputs = setup_inputs


def setup_inputs(seed=0):
    import zlib

    import numpy as np

    out = dict(_drawn_inputs(seed))
    spreads = {'L1_gnn_b': (0.0, 0.1),
     'L2_gnn_bias_att': (0.0, 0.1),
     'L2_gnn_b1': (0.0, 0.331),
     'L2_gnn_b2': (0.0, 0.1),
     'L2_gnn_ln1_g': (1.0, 0.2),
     'L2_gnn_ln1_b': (0.0, 0.1),
     'L2_gnn_ln2_g': (1.0, 0.2),
     'L2_gnn_ln2_b': (0.0, 0.1)}
    factors = {'edge_attr_48': 3.158,
     'L2_gnn_att_src': 8.0,
     'L2_gnn_att_dst': 8.0,
     'L3_gnn_b_self': 3.989}
    for name, (base, spread) in spreads.items():
        noise = np.random.default_rng([zlib.crc32(name.encode()), seed]).standard_normal(out[name].shape)
        drawn = base * np.exp(spread * noise) if base else spread * noise
        out[name] = jnp.asarray(drawn.astype(out[name].dtype))
    for name, factor in factors.items():
        out[name] = (out[name] * factor).astype(out[name].dtype)
    return out
```

```python
import concourse.bass as bass
from concourse import mybir
from contextlib import ExitStack

f32, i32, bf16 = mybir.dt.float32, mybir.dt.int32, mybir.dt.bfloat16
ALU = mybir.AluOpType
ACT = mybir.ActivationFunctionType
X = mybir.AxisListType.X
P = 128
D = 64
FE = 48
HEADS = 8
HD = HEADS * D
HALF = 26
BHALF = 13
NACC = 4
JB = 7
NCH = 4
BIG = 1e30
LN_EPS = 1e-5


def rows_of(n):
    a = n // 16 * 16
    return [(0, a), (a, n)] if a < n else [(0, n)]


class Chain:

    def __init__(self, nc, ctx, name, loops=0):
        self.sem = {k: ctx.enter_context(nc.semaphore(f"{name}_{k}")) for k in ("c", "hw", "sw")}
        self.pace = ctx.enter_context(nc.semaphore(f"{name}_pace"))
        self.loops, self.steps, self.prev = loops, [], None

    def end(self):
        kind = self.steps[-1][2]
        total = sum(1 if k == "c" else 16 * n for _, _, k, n in self.steps if k == kind)
        return self.sem[kind], total * self.loops + 1 if self.loops else total

    def add(self, engine, fn, kind="c", n=1):
        self.steps.append((engine, fn, kind, n))

    def run(self, engine, eng):
        total = {"c": 0, "hw": 0, "sw": 0}
        for _, _, kind, n in self.steps:
            total[kind] += 1 if kind == "c" else 16 * n
        if not any(s[0] == engine for s in self.steps):
            return
        if self.steps[0][0] == engine and self.prev:
            eng.wait_ge(*self.prev.end())
        if self.loops:
            assert self.steps[-1][2] == "c"
            if self.steps[0][0] == engine:
                eng.sem_inc(self.sem["c"], 1)
            with eng.Fori(0, self.loops) as i:
                self._body(engine, eng, i, total, 1)
        else:
            self._body(engine, eng, 0, total, 0)
            if self.steps[-1][0] == engine and self.steps[-1][2] != "c":
                eng.wait_ge(*self.end())

    def _body(self, engine, eng, i, total, credit):
        count = {"c": credit, "hw": 0, "sw": 0}
        before = "c"
        for e, fn, kind, n in self.steps:
            if e == engine and (count[before] or credit):
                eng.wait_ge(self.sem[before], i * total[before] + count[before])
                if self.loops and engine == "tensor":
                    eng.sem_inc(self.pace, 1)
            if e == engine:
                done = fn(eng, i)
                for d in done if isinstance(done, list) else [done]:
                    d.then_inc(self.sem[kind], 1 if kind == "c" else 16)
            count[kind] += 1 if kind == "c" else 16 * n
            before = kind


def build(nc, x, src, dst, edge_attr, edge_type, w0a, b0a, w0b, b0b, w1, b1, watt, att_s, att_d, batt, wf1, bf1, wf2,
          bf2, g1, be1, g2, be2, w3, b3, out):
    N, E = x.shape[0], src.shape[0]
    T = -(-E // (P * 2 * HALF)) * 2 * HALF
    EP = P * T
    J = -(-(N + 1) // (P * JB)) * JB
    NP = P * J
    HI = NP // P
    TF = E // P
    REST = E - TF * P
    TC = T // NCH
    DUMP = NP
    TAILE = E - (P - 1) * T
    PN, TAILN = N // J, N - N // J * J
    assert TF == T - 1 and 0 < REST < P and 0 < TAILE <= T and HI <= P and PN == P - 1 and 0 < TAILN < J

    def dram(name, shape, dt=f32):
        return nc.dram_tensor(name, shape, dt).ap()

    acc_d = [dram(f"acc{k}", [NP + P, D]) for k in range(NACC)]
    h1_d = dram("h1_table", [NP, D])
    as_d = dram("att_src_table", [NP, HEADS])
    hw_d = dram("att_feature_table", [NP, HD])
    y3_d = dram("relation_table", [3 * NP, D])
    run_d = dram("running_sums", [EP, D])
    run8_d = dram("running_heads", [EP, HEADS])
    spread_d = dram("spread", [EP + NP, 2 * HEADS])
    am_d = dram("node_att_max", [NP, 2 * HEADS])
    cnt_d = dram("degree", [NP])
    end_d = dram("segment_end", [NP])

    def per_node(t):
        return t.rearrange("(p j) f -> p j f", j=J)

    def per_edge(t):
        return t[0:EP, :].rearrange("(p t) f -> p t f", t=T)

    top = ExitStack()
    with top:
        def sb(name, shape, dt=f32, ctx=top):
            return ctx.enter_context(nc.sbuf_tensor(name, shape, dt))

        def sem(name):
            return top.enter_context(nc.semaphore(name))

        ps = [top.enter_context(nc.psum_tensor(f"bank{b}", [P, 512], f32)) for b in range(8)]
        xs = sb("x_nodes", [P, J, D])
        hs = sb("h_nodes", [P, J, D])
        st = sb("node_stat", [P, J])
        st2 = sb("node_stat2", [P, J])
        src_i = sb("src_i", [P, T], i32)
        same = sb("same_dst", [P, T])
        ident = sb("ident", [P, P])
        link = sb("link", [P, J, P])
        last_i = sb("last_edge", [P, J], i32)
        start_i = sb("start_edge", [P, J], i32)
        first_i = sb("first_dst", [P, 1], i32)
        last_f = sb("last_dst_f", [P, 1])
        nonempty = sb("nonempty", [P, J])
        rdeg = sb("one_over_degree", [P, J])
        run = [sb(f"run{h}", [P, HALF, D]) for h in range(2)]
        idx = [sb(f"idx{h}", [P, HALF], i32) for h in range(2)]
        mask = [sb(f"mask{h}", [P, HALF]) for h in range(2)]

        def bc(ap, shape):
            return ap.to_broadcast(shape)

        def normalise(ch, dst_t, src_t, tmp, relu=True, gain=None, shift=None):
            full = [P, J, D]
            s3, q3 = st[:, :].unsqueeze(2), st2[:, :].unsqueeze(2)
            V = "vector"
            ch.add(V, lambda e, i: e.tensor_reduce(st[:, :], src_t[:, :, :], X, ALU.add))
            ch.add(V, lambda e, i: e.tensor_scalar(st[:, :], st[:, :], 1.0 / D, None, ALU.mult))
            ch.add(V, lambda e, i: e.tensor_tensor(dst_t[:, :, :], src_t[:, :, :], bc(s3, full), ALU.subtract))
            ch.add(V, lambda e, i: e.tensor_tensor(tmp[:, :, :], dst_t[:, :, :], dst_t[:, :, :], ALU.mult))
            ch.add(V, lambda e, i: e.tensor_reduce(st2[:, :], tmp[:, :, :], X, ALU.add))
            ch.add(V, lambda e, i: e.tensor_scalar(st2[:, :], st2[:, :], 1.0 / D, LN_EPS, ALU.mult, ALU.add))
            ch.add("scalar", lambda e, i: e.activation(st2[:, :], st2[:, :], ACT.Sqrt))
            ch.add(V, lambda e, i: e.reciprocal(st2[:, :], st2[:, :]))
            ch.add(V, lambda e, i: e.tensor_tensor(dst_t[:, :, :], dst_t[:, :, :], bc(q3, full), ALU.mult))
            if relu:
                ch.add(V, lambda e, i: e.tensor_scalar(dst_t[:, :, :], dst_t[:, :, :], 0.0, None, ALU.max))
            if gain is not None:
                ch.add(V, lambda e, i: e.tensor_tensor(dst_t[:, :, :], dst_t[:, :, :],
                                                       bc(gain[:, :].unsqueeze(1), full), ALU.mult))
                ch.add(V, lambda e, i: e.tensor_tensor(dst_t[:, :, :], dst_t[:, :, :],
                                                       bc(shift[:, :].unsqueeze(1), full), ALU.add))

        def stage(*chains):
            for a, b in zip(chains, chains[1:]):
                b.prev = a
            with nc.Block() as block:
                for name in ("sync", "gpsimd", "scalar", "vector", "tensor"):
                    def body(e, name=name):
                        for ch in chains:
                            ch.run(name, e)
                    getter = {"sync": block.sync, "gpsimd": block.gpsimd, "scalar": block.scalar,
                              "vector": block.vector, "tensor": block.tensor}[name]
                    getter(body)

        def chain(name, loops=0):
            return Chain(nc, top, name, loops)

        l0 = ExitStack()
        src0 = sb("src0", [P, T], i32, l0)
        src0f = sb("src0f", [P, T], f32, l0)
        dlo = sb("dst_lo", [P, T], f32, l0)
        dhi = sb("dst_hi", [P, T], f32, l0)
        hist = sb("hist", [P, P], f32, l0)
        iota = sb("iota_row", [P, P], f32, l0)
        lower = sb("strict_lower", [P, P], f32, l0)
        upper = sb("strict_upper", [P, P], f32, l0)
        dumprow = sb("dump_row", [P, 1], f32, l0)
        ones = sb("ones", [P, 1], f32, l0)
        zero = sb("zero", [P, 1024], f32, l0)
        c0 = ExitStack()
        dst_i = sb("dst_i", [P, T], i32, c0)
        dtmp = sb("dst_tmp", [P, T], i32, c0)
        edge_d = sb("edge_of_runs", [P, 3], i32, c0)
        edge_f = sb("edge_of_runs_f", [P, 3], f32, c0)
        prevf = sb("prev_f", [P, 1], f32, c0)
        linkf = sb("link_dst", [P, 1], f32, c0)

        def load_runs(e, tile, flat):
            body = flat[0:(P - 1) * T].rearrange("(p t) -> p t", t=T)
            d = [e.dma_start(tile[a:b, :], body[a:b, :]) for a, b in rows_of(P - 1)]
            return d + [e.dma_start(tile[P - 1:P, 0:TAILE], flat[(P - 1) * T:E].unsqueeze(0))]

        def node_rows(e, tile, flat, back=False):
            body = flat[0:PN * J, :].rearrange("(p j) f -> p j f", j=J)
            pairs = [(tile[a:b, :, :], body[a:b, :, :]) for a, b in rows_of(PN)]
            pairs.append((tile[PN:PN + 1, 0:TAILN, :], flat[PN * J:N, :].unsqueeze(0)))
            return [e.dma_start(b, a) if back else e.dma_start(a, b) for a, b in pairs]

        ch = chain("setup")

        def clear(e, i):
            e.memset(xs[:, :, :], 0.0)
            e.memset(src_i[:, :], 0)
            e.memset(dst_i[:, :], N)
            e.memset(src0[:, :], N)
            e.memset(zero[:, :], 0.0)
            e.memset(hist[:, :], 0.0)
            e.memset(ones[:, :], 1.0)
            e.memset(lower[:, :], 1.0)
            e.memset(upper[:, :], 1.0)
            e.memset(run[1][:, :, :], 0.0)
            e.memset(edge_d[:, :], -1)
            return e.memset(ident[:, :], 0.0)
        ch.add("vector", clear)

        def loads(e, i):
            a = node_rows(e, xs, x) + load_runs(e, src_i, src) + load_runs(e, dst_i, dst)
            a.append(e.dma_start(src0[:, 0:TF], src[0:P * TF].rearrange("(p t) -> p t", t=TF)))
            col = src.unsqueeze(1)
            dcol = dst.unsqueeze(1)
            with nc.allow_non_contiguous_dma(reason="one column of indices"):
                a.append(e.dma_start(src0[0:REST, TF:T], col[P * TF:E, :]))
            return a
        n_loads = len(rows_of(PN)) + 1 + 2 * (len(rows_of(P - 1)) + 1) + 2
        ch.add("sync", loads, "hw", n_loads)

        def zero_tables(e, i):
            a = []
            for k in range(NACC):
                flat = acc_d[k].rearrange("(p a) f -> p (a f)", p=P)
                w = flat.shape[1]
                for c in range(0, w, 1024):
                    a.append(e.dma_start(flat[:, c:min(c + 1024, w)], zero[:, 0:min(1024, w - c)]))
            flat = spread_d[0:EP, :].rearrange("(p t) f -> p (t f)", p=P)
            w = flat.shape[1]
            for c in range(0, w, 1024):
                a.append(e.dma_start(flat[:, c:min(c + 1024, w)], zero[:, 0:min(1024, w - c)]))
            return a
        n_zero = NACC * -(-((NP + P) * D // P) // 1024) + -(-(T * 2 * HEADS) // 1024)
        ch.add("sync", zero_tables, "hw", n_zero)

        def edges_in(e, i):
            return [e.dma_start(edge_d[:, 1:2], dst_i[:, T - 1:T]), e.dma_start(edge_d[0:P - 1, 2:3], dst_i[1:P, 0:1])]
        ch.add("sync", edges_in, "hw", 2)
        prev_d = sb("prev_d", [P, 1], i32, c0)
        ch.add("vector", lambda e, i: e.memset(prev_d[:, :], -1))
        ch.add("sync", lambda e, i: e.dma_start(prev_d[1:P, :], dst_i[0:P - 1, T - 1:T]), "hw")

        def constants(e, i):
            e.iota(iota[:, :], [[1, P]], base=0, channel_multiplier=0, allow_small_or_imprecise_dtypes=True)
            e.iota(dumprow[:, :], [[0, 1]], base=DUMP, channel_multiplier=1, allow_small_or_imprecise_dtypes=True)
            e.iota(link[:, :, :], [[1, J], [J, P]], base=0, channel_multiplier=0, allow_small_or_imprecise_dtypes=True)
            e.affine_select(out=ident[:, :], in_=ident[:, :], compare_op=ALU.not_equal, fill=1.0, base=0,
                            pattern=[[-1, P]], channel_multiplier=1)
            e.affine_select(out=lower[:, :], in_=lower[:, :], compare_op=ALU.is_gt, fill=0.0, base=0,
                            pattern=[[-1, P]], channel_multiplier=1)
            return e.affine_select(out=upper[:, :], in_=upper[:, :], compare_op=ALU.is_gt, fill=0.0, base=0,
                                   pattern=[[1, P]], channel_multiplier=-1)
        ch.add("gpsimd", constants)
        V = "vector"

        def same_a(e, i):
            e.tensor_tensor(same[:, 1:T], dst_i[:, 1:T], dst_i[:, 0:T - 1], ALU.is_equal)
            e.tensor_tensor(same[:, 0:1], dst_i[:, 0:1], prev_d[:, :], ALU.is_equal)
            e.tensor_copy(edge_f[:, :], edge_d[:, :])
            e.tensor_copy(first_i[:, :], dst_i[:, 0:1])
            e.tensor_copy(last_f[:, :], dst_i[:, T - 1:T])
            e.tensor_copy(src0f[:, :], src0[:, :])
            return e.tensor_scalar(dtmp[:, :], dst_i[:, :], P - 1, None, ALU.bitwise_and)
        ch.add(V, same_a)
        ch.add(V, lambda e, i: e.tensor_copy(dlo[:, :], dtmp[:, :]))
        ch.add(V, lambda e, i: e.tensor_scalar(dtmp[:, :], dst_i[:, :], 7, None, ALU.logical_shift_right))
        ch.add(V, lambda e, i: e.tensor_copy(dhi[:, :], dtmp[:, :]))
        ch.add(V, lambda e, i: e.tensor_tensor(prevf[:, :], edge_f[:, 1:2], edge_f[:, 2:3], ALU.is_equal))
        ch.add(V, lambda e, i: e.scalar_tensor_tensor(linkf[:, :], edge_f[:, 1:2], 1.0, prevf[:, :], ALU.add,
                                                      ALU.mult))
        ch.add(V, lambda e, i: e.tensor_scalar(linkf[:, :], linkf[:, :], -1.0, None, ALU.add))
        ch.add(V, lambda e, i: e.tensor_scalar(link[:, :, :], link[:, :, :], linkf[:, 0:1], None, ALU.is_equal))
        stage(ch)
        c0.close()

        with ExitStack() as ctx:
            attr = [sb(f"attr{h}", [P, HALF, FE], f32, ctx) for h in range(2)]
            val = [sb(f"val{h}", [P, HALF, D], f32, ctx) for h in range(2)]
            eq = [sb(f"eq{k}", [P, P], f32, ctx) for k in range(4)]
            sfs = [sb(f"src_tile{h}", [P, HALF], f32, ctx) for h in range(2)]
            dups = [sb(f"dups{h}", [P, HALF], f32, ctx) for h in range(2)]
            scr = [sb(f"scratch{k}", [P, P], f32, ctx) for k in range(4)]
            tgt = sb("target_f", [P, HALF], f32, ctx)
            ohlo = [sb(f"onehot_lo{h}", [P, HALF, P], bf16, ctx) for h in range(2)]
            ohhi = [sb(f"onehot_hi{h}", [P, HALF, HI], bf16, ctx) for h in range(2)]
            HB = HALF // 2
            s_attr = [sem(f"l0_attr{h}") for h in range(2)]
            s_stage, s_psrc, s_eq, s_sum, s_val, s_hot, s_hist, s_hadd, s_dup, s_tgt, s_vfree, s_acc = (
                sem(f"l0_{n}") for n in ("staged", "src_rows", "equal", "summed", "values", "onehots", "hist",
                                         "hist_added", "dup", "targets", "val_free", "pace"))
            s_add = [sem(f"l0_acc{k}") for k in range(NACC)]
            s_init, s_tail = sem("l0_init"), sem("l0_tail")
            LOOPS = T // (2 * HALF)
            attr_v = edge_attr[0:P * TF, :].rearrange("(p t) f -> p t f", t=TF)

            with nc.Block() as block:
                @block.sync
                def _(e):
                    e.wait_ge(s_init, 1)
                    def load(i, h, last=False):
                        e.wait_ge(s_sum, (i * 2 + h + 1) * HB + 1)
                        t0 = (i * 2 + h) * HALF
                        if last:
                            e.dma_start(attr[h][:, HALF - 1, :], zero[:, 0:FE]).then_inc(s_tail, 16)
                            e.wait_ge(s_tail, 16)
                            e.dma_start(attr[h][0:REST, HALF - 1, :], edge_attr[P * TF:E, :]).then_inc(s_tail, 16)
                            e.wait_ge(s_tail, 32)
                            e.dma_start(attr[h][:, 0:HALF - 1, :], attr_v[:, t0:TF, :]).then_inc(s_attr[h], 16)
                        else:
                            e.dma_start(attr[h][:, :, :], attr_v[:, bass.ds(t0, HALF), :]).then_inc(s_attr[h], 16)
                    if LOOPS > 1:
                        with e.Fori(0, LOOPS - 1) as i:
                            load(i, 0)
                            load(i, 1)
                    load(LOOPS - 1, 0)
                    load(LOOPS - 1, 1, last=True)

                @block.tensor
                def _(e):
                    e.sem_inc(s_sum, 2 * HB + 1)
                    e.wait_ge(s_init, 1)
                    with e.Fori(0, LOOPS) as i:
                        for h in range(2):
                            hh = i * 2 + h
                            e.wait_ge(s_stage, hh + 1)
                            def rows(b):
                                B = hh * HB + b
                                e.wait_ge(s_eq, B + 1)
                                for u in range(2):
                                    last = e.transpose(ps[(h + b) % 2][:, u * P:(u + 1) * P],
                                                       bc(sfs[h][:, 2 * b + u:2 * b + u + 1], [P, P]), ident[:, :])
                                last.then_inc(s_psrc, 1)
                            def sums(b):
                                B = hh * HB + b
                                e.wait_ge(s_eq, B + 3)
                                e.wait_ge(s_val, B + 1)
                                if b == 0:
                                    e.wait_ge(s_attr[h], (i + 1) * 16)
                                for u in range(2):
                                    o = ps[2 + (h + b) % 2][:, u * D:(u + 1) * D]
                                    e.matmul(o[:, 0:FE], eq[2 * ((h + b) % 2) + u][:, :], attr[h][:, 2 * b + u, :],
                                             start=True, stop=True)
                                    last = e.matmul(o[:, FE:FE + 1], eq[2 * ((h + b) % 2) + u][:, :], ones[:, :],
                                                    start=True, stop=True)
                                last.then_inc(s_sum, 1)
                            rows(0)
                            e.wait_ge(s_hot, hh + 1)
                            e.wait_ge(s_hadd, hh + 1)
                            for r in range(HALF):
                                last = e.matmul(ps[4][0:HI, 0:P], ohhi[h][:, r, :], ohlo[h][:, r, :],
                                                start=(r == 0), stop=(r == HALF - 1))
                            last.then_inc(s_hist, 1)
                            for b in range(1, HB):
                                rows(b)
                                sums(b - 1)
                            sums(HB - 1)

                @block.vector
                def _(e):
                    for h in range(2):
                        e.memset(val[h][:, :, :], 0.0)
                        last = e.memset(attr[h][:, :, :], 0.0)
                    last.then_inc(s_init, 1)
                    e.sem_inc(s_eq, 2)
                    e.sem_inc(s_hadd, 1)
                    with e.Fori(0, LOOPS) as i:
                        for h in range(2):
                            hh = i * 2 + h
                            t0 = hh * HALF
                            e.tensor_tensor(ohlo[h][:, :, :], bc(iota[:, :].unsqueeze(1), [P, HALF, P]),
                                            bc(dlo[:, bass.ds(t0, HALF)].unsqueeze(2), [P, HALF, P]), ALU.is_equal)
                            e.tensor_tensor(ohhi[h][:, :, :], bc(iota[:, 0:HI].unsqueeze(1), [P, HALF, HI]),
                                            bc(dhi[:, bass.ds(t0, HALF)].unsqueeze(2), [P, HALF, HI]),
                                            ALU.is_equal).then_inc(s_hot, 1)
                            e.wait_ge(s_stage, hh + 1)
                            for b in range(HB):
                                B = hh * HB + b
                                e.wait_ge(s_psrc, B + 1)
                                e.wait_ge(s_sum, B + 1 + 2 * HB + 1 - 2)
                                e.wait_ge(s_eq, B + 1)
                                for u in range(2):
                                    r = 2 * b + u
                                    row = ps[(h + b) % 2][:, u * P:(u + 1) * P]
                                    k = 2 * ((h + b) % 2) + u
                                    e.scalar_tensor_tensor(scr[k][:, :], row, sfs[h][:, r:r + 1], lower[:, :],
                                                           ALU.is_equal, ALU.mult, accum_out=dups[h][:, r:r + 1])
                                    last = e.tensor_scalar(eq[k][:, :], row, sfs[h][:, r:r + 1], None,
                                                           ALU.is_equal)
                                last.then_inc(s_eq, 1)
                            e.wait_ge(s_eq, (hh + 1) * HB + 2)
                            e.tensor_scalar(dups[h][:, :], dups[h][:, :], 0.0, None, ALU.is_equal).then_inc(s_dup, 1)
                            e.wait_ge(s_dup, hh * 3 + 1)
                            e.scalar_tensor_tensor(tgt[:, :], sfs[h][:, :], dumprow[:, 0:1], dups[h][:, :],
                                                   ALU.subtract, ALU.mult).then_inc(s_dup, 1)
                            e.wait_ge(s_dup, hh * 3 + 2)
                            e.tensor_scalar(tgt[:, :], tgt[:, :], dumprow[:, 0:1], None,
                                            ALU.add).then_inc(s_dup, 1)
                            e.wait_ge(s_dup, hh * 3 + 3)
                            e.wait_ge(s_vfree, hh + 1)
                            e.tensor_copy(idx[h][:, :], tgt[:, :]).then_inc(s_tgt, 1)
                            e.wait_ge(s_hist, hh + 1)
                            e.tensor_tensor(hist[0:HI, :], hist[0:HI, :], ps[4][0:HI, 0:P], ALU.add)\
                             .then_inc(s_hadd, 1)

                @block.scalar
                def _(e):
                    e.wait_ge(s_init, 1)
                    e.sem_inc(s_val, 2)
                    with e.Fori(0, LOOPS) as i:
                        for h in range(2):
                            hh = i * 2 + h
                            e.wait_ge(s_tgt, hh + 1)
                            e.copy(sfs[h][:, :], src0f[:, bass.ds(hh * HALF, HALF)]).then_inc(s_stage, 1)
                            e.wait_ge(s_vfree, hh + 1)
                            for b in range(HB):
                                e.wait_ge(s_sum, hh * HB + b + 1 + 2 * HB + 1)
                                e.copy(val[h][:, 2 * b:2 * b + 2, 0:FE + 1],
                                       ps[2 + (h + b) % 2][:, 0:2 * D].rearrange("p (u f) -> p u f", f=D)[:, :, 0:FE + 1])\
                                 .then_inc(s_val, 1)

                @block.gpsimd
                def _(e):
                    e.sem_inc(s_vfree, 1)
                    e.sem_inc(s_tgt, 2)
                    for k in range(NACC):
                        e.dma_start(acc_d[k][0:1, :], zero[0:1, 0:D]).then_inc(s_add[k], 16)
                    with e.Fori(0, LOOPS) as i:
                        for h in range(2):
                            hh = i * 2 + h
                            e.wait_ge(s_tgt, hh + 3)
                            e.wait_ge(s_val, (hh + 1) * HB + 2)
                            for r in range(HALF):
                                q, k = divmod(h * HALF + r, NACC)
                                e.wait_ge(s_add[k], (i * (2 * HALF // NACC) + q) * 16 + 16)
                                e.sem_inc(s_acc, 1)
                                e.indirect_dma_start(acc_d[k], bass.IndirectOffsetOnAxis(ap=idx[h][:, r:r + 1], axis=0),
                                                     val[h][:, r, :], None, compute_op=ALU.add).then_inc(s_add[k], 16)
                                if r == NACC - 1:
                                    e.sem_inc(s_vfree, 1)
                    for k in range(NACC):
                        e.wait_ge(s_add[k], 16 * (LOOPS * (2 * HALF // NACC) + 1))

        with ExitStack() as ctx:
            cum = sb("cum", [P, P], f32, ctx)
            before = sb("before", [P, 1], f32, ctx)
            endf = sb("end_f", [P, J], f32, ctx)
            degf = sb("deg_f", [P, J], f32, ctx)
            dumpn = sb("dump_n", [P, J], f32, ctx)
            agg = sb("agg", [P, J, D], f32, ctx)
            part = sb("part", [P, J, D], f32, ctx)
            both = sb("both", [P, J, D + FE], f32, ctx)
            bothj = sb("both_step", [P, JB, D + FE], f32, ctx)
            ct = sb("both_t", [D + FE, JB * P], f32, ctx)
            ht = sb("hidden_t", [P, 2, JB * P], f32, ctx)
            w0a_s = sb("w0a", [D + FE, 256], f32, ctx)
            w0b_s = sb("w0b", [P, 2, D], f32, ctx)
            b0a_s = sb("b0a", [P, 2], f32, ctx)
            b0b_s = sb("b0b", [P, D], f32, ctx)
            V = "vector"
            ch = chain("nodes0")
            ch.add("sync", lambda e, i: [
                e.dma_start(agg[:, :, :], per_node(acc_d[0][0:NP, :])), e.dma_start(w0a_s[:, :], w0a),
                e.dma_start(w0b_s[:, :, :], w0b.rearrange("(c p) n -> p c n", p=P)),
                e.dma_start(b0a_s[:, :], b0a), e.dma_start(b0b_s[:, :], b0b.partition_broadcast(P))], "hw", 5)
            ch.add(V, lambda e, i: e.memset(cum[:, :], 1.0))
            ch.add(V, lambda e, i: e.tensor_tensor_scan(cum[0:HI, :], cum[0:HI, :], hist[0:HI, :], 0.0, ALU.mult,
                                                        ALU.add))
            ch.add("tensor", lambda e, i: e.matmul(ps[0][0:HI, 0:1], upper[0:HI, 0:HI], cum[0:HI, P - 1:P],
                                                   start=True, stop=True))
            ch.add(V, lambda e, i: e.tensor_copy(before[0:HI, :], ps[0][0:HI, 0:1]))
            ch.add(V, lambda e, i: e.tensor_scalar(cum[0:HI, :], cum[0:HI, :], before[0:HI, 0:1], None, ALU.add))
            ch.add("sync", lambda e, i: [e.dma_start(end_d.rearrange("(a b) -> a b", b=P), cum[0:HI, :]),
                                         e.dma_start(cnt_d.rearrange("(a b) -> a b", b=P), hist[0:HI, :])], "hw", 2)
            ch.add("sync", lambda e, i: [e.dma_start(endf[:, :], end_d.rearrange("(p j) -> p j", j=J)),
                                         e.dma_start(degf[:, :], cnt_d.rearrange("(p j) -> p j", j=J))], "hw", 2)
            ch.add("gpsimd", lambda e, i: e.iota(dumpn[:, :], [[1, J]], base=EP, channel_multiplier=J,
                                                 allow_small_or_imprecise_dtypes=True))

            def ends(e, i):
                e.tensor_scalar(last_i[:, :], endf[:, :], -1.0, 0.0, ALU.add, ALU.max)
                e.tensor_scalar(rdeg[:, :], degf[:, :], 1.0, None, ALU.max)
                e.tensor_scalar(nonempty[:, :], degf[:, :], 0.0, None, ALU.is_gt)
                return e.tensor_tensor(endf[:, :], endf[:, :], degf[:, :], ALU.subtract)
            ch.add(V, ends)
            ch.add(V, lambda e, i: e.tensor_tensor(endf[:, :], endf[:, :], dumpn[:, :], ALU.subtract))
            ch.add(V, lambda e, i: e.tensor_tensor(endf[:, :], endf[:, :], nonempty[:, :], ALU.mult))
            ch.add(V, lambda e, i: e.tensor_tensor(start_i[:, :], endf[:, :], dumpn[:, :], ALU.add))
            ch.add(V, lambda e, i: e.reciprocal(rdeg[:, :], rdeg[:, :]))
            for k in range(1, NACC):
                ch.add("sync", lambda e, i, k=k: e.dma_start(part[:, :, :], per_node(acc_d[k][0:NP, :])), "hw")
                ch.add(V, lambda e, i: e.tensor_tensor(agg[:, :, :], agg[:, :, :], part[:, :, :], ALU.add))
            ch.add(V, lambda e, i: e.tensor_scalar(st[:, :], agg[:, :, FE], 1.0, None, ALU.max))
            ch.add(V, lambda e, i: e.reciprocal(st[:, :], st[:, :]))
            ch.add(V, lambda e, i: e.tensor_tensor(both[:, :, D:D + FE], agg[:, :, 0:FE],
                                                   bc(st[:, :].unsqueeze(2), [P, J, FE]), ALU.mult))
            normalise(ch, hs, xs, part)
            ch.add(V, lambda e, i: e.tensor_copy(both[:, :, 0:D], hs[:, :, :]))
            ch.add(V, lambda e, i: e.tensor_tensor(xs[:, :, :], xs[:, :, :], bc(b0b_s[:, :].unsqueeze(1), [P, J, D]),
                                                   ALU.add))

            lp = chain("mlp0", J // JB)
            lp.add(V, lambda e, i: e.tensor_copy(bothj[:, :, :], both[:, bass.ds(i * JB, JB), :]))

            def transposes(src_t, width):
                def fn(e, i):
                    for j in range(JB):
                        o = ps[j // 4][0:width, (j % 4) * P:(j % 4 + 1) * P]
                        last = e.transpose(o, src_t[:, j, 0:width], ident[:, :])
                    return last
                return fn

            def untranspose(dst_t, width):
                def fn(e, i):
                    e.copy(dst_t[0:width, 0:512], ps[0][0:width, :])
                    return e.copy(dst_t[0:width, 512:JB * P], ps[1][0:width, 0:JB * P - 512])
                return fn
            lp.add("tensor", transposes(bothj, D + FE))
            lp.add("scalar", untranspose(ct, D + FE))

            def up0(e, i):
                for c in range(2):
                    for b, (lo, hi) in enumerate(((0, 512), (512, JB * P))):
                        last = e.matmul(ps[2 + 2 * c + b][:, 0:hi - lo], w0a_s[:, c * P:(c + 1) * P], ct[:, lo:hi],
                                        start=True, stop=True)
                return last
            lp.add("tensor", up0)

            def relu0(e, i):
                for c in range(2):
                    for b, (lo, hi) in enumerate(((0, 512), (512, JB * P))):
                        last = e.activation(ht[:, c, lo:hi], ps[2 + 2 * c + b][:, 0:hi - lo], ACT.Relu,
                                            bias=b0a_s[:, c:c + 1])
                return last
            lp.add("scalar", relu0)

            def down0(e, i):
                for j in range(JB):
                    for c in range(2):
                        last = e.matmul(ps[6][:, j * D:(j + 1) * D], ht[:, c, j * P:(j + 1) * P], w0b_s[:, c, :],
                                        start=(c == 0), stop=(c == 1))
                return last
            lp.add("tensor", down0)

            def tiles(bank, n=JB, w=D):
                return ps[bank][:, 0:n * w].rearrange("p (j f) -> p j f", f=w)
            lp.add(V, lambda e, i: e.tensor_tensor(xs[:, bass.ds(i * JB, JB), :], xs[:, bass.ds(i * JB, JB), :],
                                                   tiles(6), ALU.add))
            ch2 = chain("norm1")
            normalise(ch2, hs, xs, part)
            ch2.add("sync", lambda e, i: e.dma_start(per_node(h1_d), hs[:, :, :]), "hw")
            stage(ch, lp, ch2)
        l0.close()

        def edge_pass(name, table, index, gbuf, C, alpha=None):
            LP = T // (2 * C)
            s_g = [sem(f"{name}_rows{h}") for h in range(2)]
            s_st = [sem(f"{name}_store{h}") for h in range(2)]
            s_idx, s_use, s_step, s_run, s_mul, s_mix = (
                sem(f"{name}_{n}") for n in ("staged", "used", "step", "run", "scaled", "mixed"))
            wide = alpha is not None
            groups = [(0, 8), (8, C)] if wide else []
            with ExitStack() as ctx, nc.Block() as block:
                astage = [sb(f"{name}_alpha{h}", [P, C, HEADS], f32, ctx) for h in range(2)] if wide else None

                @block.scalar
                def _(e):
                    with e.Fori(0, LP) as i:
                        for h in range(2):
                            hh = i * 2 + h
                            e.wait_ge(s_run, hh + 1)
                            e.copy(idx[h][:, 0:C], index[:, bass.ds(hh * C, C)])
                            if wide:
                                e.copy(astage[h][:, :, :], alpha[:, bass.ds(hh * C, C), :])
                            e.copy(mask[h][:, 0:C], same[:, bass.ds(hh * C, C)]).then_inc(s_idx, 1)

                @block.gpsimd
                def _(e):
                    with e.Fori(0, LP) as i:
                        for h in range(2):
                            hh = i * 2 + h
                            e.wait_ge(s_idx, hh + 1)
                            e.sem_inc(s_use, 1)
                            for r in range(C):
                                e.indirect_dma_start(gbuf[h][:, r, :], None, table,
                                                     bass.IndirectOffsetOnAxis(ap=idx[h][:, r:r + 1], axis=0))\
                                 .then_inc(s_g[h], 16)

                @block.vector
                def _(e):
                    e.sem_inc(s_run, 2)
                    e.memset(run[1][:, C - 1, :], 0.0).then_inc(s_step, 1)
                    with e.Fori(0, LP) as i:
                        for h in range(2):
                            hh = i * 2 + h
                            e.wait_ge(s_g[h], (i + 1) * 16 * C)
                            e.wait_ge(s_idx, hh + 1)
                            if wide:
                                g4 = gbuf[h][:, :, :].rearrange("p r (a f) -> p (r a) f", f=D)
                                a4 = astage[h][:, :, :].rearrange("p r a -> p (r a)").unsqueeze(2)
                                e.tensor_tensor(g4, g4, bc(a4, [P, C * HEADS, D]), ALU.mult).then_inc(s_mul, 1)
                                e.wait_ge(s_mix, hh + 1)
                            e.wait_ge(s_st[h], i * 16 + 16)
                            for r in range(C):
                                before_row = run[h][:, r - 1, :] if r else run[1 - h][:, C - 1, :]
                                row = ps[2 * h + r // 8][:, (r % 8) * D:(r % 8 + 1) * D] if wide else gbuf[h][:, r, :]
                                e.wait_ge(s_step, hh * C + r + 1)
                                last = e.scalar_tensor_tensor(run[h][:, r, :], before_row, mask[h][:, r:r + 1], row,
                                                              ALU.mult, ALU.add).then_inc(s_step, 1)
                            e.wait_ge(s_step, (hh + 1) * C + 1)
                            e.sem_inc(s_run, 1)

                if wide:
                    @block.tensor
                    def _(e):
                        with e.Fori(0, LP) as i:
                            for h in range(2):
                                hh = i * 2 + h
                                e.wait_ge(s_mul, hh + 1)
                                e.wait_ge(s_run, hh + 1)
                                g4 = gbuf[h][:, :, :].rearrange("p r (a f) -> p r a f", f=D)
                                for n, (lo, hi) in enumerate(groups):
                                    for a in range(HEADS):
                                        last = e.matmul(ps[2 * h + n][:, 0:(hi - lo) * D], ident[:, :],
                                                        g4[:, lo:hi, a, :], start=(a == 0), stop=(a == HEADS - 1))
                                last.then_inc(s_mix, 1)

                @block.sync
                def _(e):
                    for h in range(2):
                        e.dma_start(per_edge(run_d)[:, h:h + 1, :], hs[:, 0:1, :]).then_inc(s_st[h], 16)
                    for h in range(2):
                        e.wait_ge(s_st[h], 16)
                    with e.Fori(0, LP) as i:
                        for h in range(2):
                            hh = i * 2 + h
                            e.wait_ge(s_run, hh + 3)
                            e.dma_start(per_edge(run_d)[:, bass.ds(hh * C, C), :], run[h][:, 0:C, :])\
                             .then_inc(s_st[h], 16)
                    for h in range(2):
                        e.wait_ge(s_st[h], 16 * (LP + 1))

        def collect(ch, res, table, tail, w):
            ch.add("gpsimd", lambda e, i: [
                e.indirect_dma_start(res[:, j, :], None, table,
                                     bass.IndirectOffsetOnAxis(ap=last_i[:, j:j + 1], axis=0)) for j in range(J)],
                   "sw", J)
            ch.add("vector", lambda e, i: e.tensor_tensor(res[:, :, :], res[:, :, :],
                                                          bc(nonempty[:, :].unsqueeze(2), [P, J, w]), ALU.mult))
            per = 512 // w

            def carry(e, i):
                for j in range(J):
                    last = e.matmul(ps[j // per][:, (j % per) * w:(j % per + 1) * w], link[:, j, :], tail,
                                    start=True, stop=True)
                return last
            ch.add("tensor", carry)

            def fold(e, i):
                for b in range(-(-J // per)):
                    n = min(per, J - b * per)
                    last = e.tensor_tensor(res[:, b * per:b * per + n, :], res[:, b * per:b * per + n, :],
                                           ps[b][:, 0:n * w].rearrange("p (j f) -> p j f", f=w), ALU.add)
                return last
            ch.add("vector", fold)

        with ExitStack() as ctx:
            g = [sb(f"rows_l1_{h}", [P, HALF, D], f32, ctx) for h in range(2)]
            edge_pass("l1", h1_d, src_i, g, HALF)

        asn = sb("att_src_node", [P, J, HEADS])
        adn = sb("att_dst_node", [P, J, HEADS])
        with ExitStack() as ctx:
            neigh = sb("neigh", [P, J, D], f32, ctx)
            pair = sb("pair", [P, JB, 2 * D], f32, ctx)
            pt = sb("pair_t", [P, JB * P], f32, ctx)
            w1_s = sb("w1", [P, D], f32, ctx)
            b1_s = sb("b1", [P, D], f32, ctx)
            tmp7 = sb("tmp7", [P, JB, D], f32, ctx)
            ch = chain("nodes1")
            ch.add("sync", lambda e, i: [e.dma_start(w1_s[:, :], w1),
                                         e.dma_start(b1_s[:, :], b1.partition_broadcast(P))], "hw", 2)
            collect(ch, neigh, run_d, run[1][:, HALF - 1, :], D)
            ch.add(V, lambda e, i: e.tensor_tensor(neigh[:, :, :], neigh[:, :, :],
                                                   bc(rdeg[:, :].unsqueeze(2), [P, J, D]), ALU.mult))
            lp = chain("dense1", J // JB)

            def join(e, i):
                e.tensor_copy(pair[:, :, 0:D], hs[:, bass.ds(i * JB, JB), :])
                return e.tensor_copy(pair[:, :, D:2 * D], neigh[:, bass.ds(i * JB, JB), :])
            lp.add(V, join)
            lp.add("tensor", transposes(pair, 2 * D))
            lp.add("scalar", untranspose(pt, 2 * D))

            def dense1(e, i):
                for j in range(JB):
                    last = e.matmul(ps[2][:, j * D:(j + 1) * D], pt[:, j * P:(j + 1) * P], w1_s[:, :],
                                    start=True, stop=True)
                return last
            lp.add("tensor", dense1)
            lp.add(V, lambda e, i: e.tensor_tensor(tmp7[:, :, :], tiles(2), bc(b1_s[:, :].unsqueeze(1), [P, JB, D]),
                                                   ALU.add))
            lp.add(V, lambda e, i: e.scalar_tensor_tensor(xs[:, bass.ds(i * JB, JB), :], tmp7[:, :, :], 0.0,
                                                          xs[:, bass.ds(i * JB, JB), :], ALU.max, ALU.add))
            ch2 = chain("norm2")
            normalise(ch2, hs, xs, neigh)
            stage(ch, lp, ch2)

        with ExitStack() as ctx:
            watt_s = sb("watt", [D, HD], f32, ctx)
            attb = sb("att_rows", [D, 2, HD], f32, ctx)
            wlog = sb("logit_weights", [D, 2 * HEADS], f32, ctx)
            step7 = sb("h_step", [P, JB, D], f32, ctx)
            t7 = sb("h_step_t", [D, JB * P], f32, ctx)
            feat = sb("att_features", [P, JB, HD], f32, ctx)
            ch = chain("att_weights")
            ch.add("sync", lambda e, i: [e.dma_start(watt_s[:, :], watt),
                                         e.dma_start(attb[:, 0, :], att_s.rearrange("a f -> (a f)").partition_broadcast(D)),
                                         e.dma_start(attb[:, 1, :], att_d.rearrange("a f -> (a f)").partition_broadcast(D))],
                   "hw", 3)
            for k in range(2):
                ch.add(V, lambda e, i, k=k: e.tensor_tensor(attb[:, k, :], attb[:, k, :], watt_s[:, :], ALU.mult))
                ch.add(V, lambda e, i, k=k: e.tensor_reduce(wlog[:, k * HEADS:(k + 1) * HEADS],
                                                            attb[:, k, :].rearrange("p (a f) -> p a f", f=D), X,
                                                            ALU.add))
            lp = chain("att_features", J // JB)
            lp.add(V, lambda e, i: e.tensor_copy(step7[:, :, :], hs[:, bass.ds(i * JB, JB), :]))
            lp.add("tensor", transposes(step7, D))
            lp.add("scalar", untranspose(t7, D))

            def project(e, i):
                for j in range(JB):
                    last = e.matmul(ps[j][:, :], t7[:, j * P:(j + 1) * P], watt_s[:, :], start=True, stop=True)
                for j in range(JB):
                    last = e.matmul(ps[7][:, j * 16:(j + 1) * 16], t7[:, j * P:(j + 1) * P], wlog[:, :],
                                    start=True, stop=True)
                return last
            lp.add("tensor", project)

            def evac(e, i):
                for j in range(JB):
                    last = e.copy(feat[:, j, :], ps[j][:, :])
                return last
            lp.add("scalar", evac)
            lp.add("sync", lambda e, i: e.dma_start(per_node(hw_d)[:, bass.ds(i * JB, JB), :], feat[:, :, :]), "hw")

            def logits(e, i):
                t = ps[7][:, 0:JB * 16].rearrange("p (j f) -> p j f", f=16)
                e.tensor_copy(asn[:, bass.ds(i * JB, JB), :], t[:, :, 0:HEADS])
                return e.tensor_copy(adn[:, bass.ds(i * JB, JB), :], t[:, :, HEADS:16])
            lp.add(V, logits)
            ch2 = chain("att_tables")
            ch2.add("sync", lambda e, i: e.dma_start(per_node(as_d), asn[:, :, :]), "hw")
            stage(ch, lp, ch2)

        att = ExitStack()
        alpha = sb("alpha", [P, T, HEADS], f32, att)
        selfw = sb("self_weight", [P, J, HEADS], f32, att)
        with ExitStack() as ctx:
            rows8 = [sb(f"logit_rows{h}", [P, HALF, HEADS], f32, ctx) for h in range(2)]
            s_g = [sem(f"l2a_rows{h}") for h in range(2)]
            s_idx, s_use, s_pace = sem("l2a_staged"), sem("l2a_used"), sem("l2a_pace")
            LP = T // (2 * HALF)
            with nc.Block() as block:
                @block.scalar
                def _(e):
                    with e.Fori(0, LP) as i:
                        for h in range(2):
                            hh = i * 2 + h
                            e.wait_ge(s_use, hh + 1)
                            e.copy(idx[h][:, :], src_i[:, bass.ds(hh * HALF, HALF)]).then_inc(s_idx, 1)

                @block.gpsimd
                def _(e):
                    with e.Fori(0, LP) as i:
                        for h in range(2):
                            hh = i * 2 + h
                            e.wait_ge(s_idx, hh + 1)
                            e.sem_inc(s_pace, 1)
                            for r in range(HALF):
                                e.indirect_dma_start(rows8[h][:, r, :], None, as_d,
                                                     bass.IndirectOffsetOnAxis(ap=idx[h][:, r:r + 1], axis=0))\
                                 .then_inc(s_g[h], 16)

                @block.vector
                def _(e):
                    e.sem_inc(s_use, 2)
                    with e.Fori(0, LP) as i:
                        for h in range(2):
                            e.wait_ge(s_g[h], (i + 1) * 16 * HALF)
                            e.tensor_copy(alpha[:, bass.ds((i * 2 + h) * HALF, HALF), :], rows8[h][:, :, :])\
                             .then_inc(s_use, 1)

        with ExitStack() as ctx:
            reset = sb("reset", [P, T], f32, ctx)
            rc = [sb(f"running{k}", [P, TC, HEADS], f32, ctx) for k in range(2)]
            tab = sb("spread_rows", [P, TC, 2 * HEADS], f32, ctx)
            tabl = sb("spread_last", [P, 2 * HEADS], f32, ctx)
            endm = sb("end_max", [P, HEADS], f32, ctx)
            carm = sb("carry_max", [P, HEADS], f32, ctx)
            cmask = sb("carry_mask", [P, P], f32, ctx)
            cm1 = sb("carry_m1", [P, P], f32, ctx)
            fird = sb("first_dst_f", [P, 1], f32, ctx)
            am = sb("att_and_max", [P, J, 2 * HEADS], f32, ctx)
            mx = sb("node_max", [P, J, HEADS], f32, ctx)
            t8 = sb("node_tmp", [P, J, HEADS], f32, ctx)
            ms = sb("mask_stat", [P, J], f32, ctx)
            sx = chain("softmax")

            def chunk(k):
                return slice(k * TC, (k + 1) * TC)

            def scans(data0, data1, outp, init, op0, op1, heads=HEADS, shift=0):
                def fn(e, i):
                    for a in range(heads):
                        last = e.tensor_tensor_scan(outp(a), data0, data1(a), init(a), op0, op1)
                    return last
                return fn
            sx.add(V, lambda e, i: e.tensor_scalar(reset[:, :], same[:, :], 1.0, BIG, ALU.subtract, ALU.mult))
            for rnd in range(2):
                for k in range(NCH):
                    o, b = rc[k % 2], rc[(k + 1) % 2]
                    init = (lambda a, b=b: b[:, TC - 1, a:a + 1]) if k else (
                        (lambda a: carm[:, a:a + 1]) if rnd else (lambda a: -BIG))
                    sx.add(V, scans(reset[:, chunk(k)], lambda a, k=k: alpha[:, chunk(k), a],
                                    lambda a, o=o: o[:, :, a], init, ALU.add, ALU.max))
                    if rnd:
                        sx.add("sync", lambda e, i, k=k, o=o: e.dma_start(per_edge(run8_d)[:, chunk(k), :], o[:, :, :]),
                               "hw")
                if rnd == 0:
                    sx.add(V, lambda e, i: e.tensor_copy(endm[:, :], rc[(NCH - 1) % 2][:, TC - 1, :]))
                    sx.add(V, lambda e, i: e.tensor_copy(fird[:, :], first_i[:, :]))
                    sx.add("tensor", lambda e, i: e.transpose(ps[0][:, 0:P], bc(last_f[:, 0:1], [P, P]), ident[:, :]))
                    sx.add(V, lambda e, i: e.tensor_scalar(cmask[:, :], ps[0][:, 0:P], fird[:, 0:1], None,
                                                           ALU.is_equal))
                    sx.add("gpsimd", lambda e, i: e.affine_select(out=cmask[:, :], in_=cmask[:, :],
                                                                  compare_op=ALU.is_gt, fill=0.0, base=0,
                                                                  pattern=[[-1, P]], channel_multiplier=1))
                    sx.add(V, lambda e, i: e.tensor_scalar(cm1[:, :], cmask[:, :], 1.0, BIG, ALU.subtract, ALU.mult))

                    def spread_ends(e, i):
                        for a in range(HEADS):
                            last = e.transpose(ps[1 + a // 4][:, (a % 4) * P:(a % 4 + 1) * P],
                                               bc(endm[:, a:a + 1], [P, P]), ident[:, :])
                        return last
                    sx.add("tensor", spread_ends)
                    for a in range(HEADS):
                        sx.add(V, lambda e, i, a=a: e.tensor_tensor(
                            cmask[:, :], ps[1 + a // 4][:, (a % 4) * P:(a % 4 + 1) * P], cm1[:, :], ALU.add))
                        sx.add(V, lambda e, i, a=a: e.tensor_reduce(carm[:, a:a + 1], cmask[:, :], X, ALU.max))
            sx.add("gpsimd", lambda e, i: [
                e.indirect_dma_start(mx[:, j, :], None, run8_d,
                                     bass.IndirectOffsetOnAxis(ap=last_i[:, j:j + 1], axis=0)) for j in range(J)],
                   "sw", J)
            ne8 = bc(nonempty[:, :].unsqueeze(2), [P, J, HEADS])
            sx.add(V, lambda e, i: e.tensor_tensor(mx[:, :, :], mx[:, :, :], ne8, ALU.mult))
            sx.add(V, lambda e, i: e.tensor_scalar(ms[:, :], nonempty[:, :], 1.0, BIG, ALU.subtract, ALU.mult))
            sx.add(V, lambda e, i: e.tensor_tensor(mx[:, :, :], mx[:, :, :],
                                                   bc(ms[:, :].unsqueeze(2), [P, J, HEADS]), ALU.add))
            sx.add(V, lambda e, i: e.tensor_tensor(mx[:, :, :], mx[:, :, :], asn[:, :, :], ALU.max))
            sx.add(V, lambda e, i: e.tensor_tensor(mx[:, :, :], mx[:, :, :], adn[:, :, :], ALU.add))

            def leaky(t, u):
                return lambda e, i: e.scalar_tensor_tensor(t, u, 0.2, u, ALU.mult, ALU.max)
            sx.add(V, leaky(am[:, :, HEADS:16], mx[:, :, :]))
            sx.add(V, lambda e, i: e.tensor_copy(am[:, :, 0:HEADS], adn[:, :, :]))
            sx.add(V, lambda e, i: e.tensor_tensor(t8[:, :, :], asn[:, :, :], adn[:, :, :], ALU.add))
            sx.add(V, leaky(selfw[:, :, :], t8[:, :, :]))
            sx.add(V, lambda e, i: e.tensor_tensor(selfw[:, :, :], selfw[:, :, :], am[:, :, HEADS:16], ALU.subtract))
            sx.add("scalar", lambda e, i: e.activation(selfw[:, :, :], selfw[:, :, :], ACT.Exp))

            def spread(values):
                return lambda e, i: [
                    e.indirect_dma_start(spread_d, bass.IndirectOffsetOnAxis(ap=start_i[:, j:j + 1], axis=0),
                                         values[:, j, :], None) for j in range(J)]
            sx.add("gpsimd", spread(am), "sw", J)
            sx.add("sync", lambda e, i: e.dma_start(per_node(am_d), am[:, :, :]), "hw")
            get_first = lambda e, i: [e.indirect_dma_start(tabl[:, :], None, am_d,
                                                           bass.IndirectOffsetOnAxis(ap=first_i[:, 0:1], axis=0))]
            sx.add("gpsimd", get_first, "sw", 1)
            for k in range(NCH):
                o, b = rc[k % 2], rc[(k + 1) % 2]
                sx.add("sync", lambda e, i, k=k: e.dma_start(tab[:, :, :], per_edge(spread_d)[:, chunk(k), :]), "hw")
                sx.add(V, scans(same[:, chunk(k)], lambda a: tab[:, :, a], lambda a: tab[:, :, a],
                                lambda a: tabl[:, a:a + 1], ALU.mult, ALU.add, 2 * HEADS))
                sx.add(V, lambda e, i: e.tensor_copy(tabl[:, :], tab[:, TC - 1, :]))
                al = alpha[:, chunk(k), :]
                sx.add(V, lambda e, i, al=al: e.tensor_tensor(al, al, tab[:, :, 0:HEADS], ALU.add))
                sx.add(V, leaky(al, al))
                sx.add(V, lambda e, i, al=al: e.tensor_tensor(al, al, tab[:, :, HEADS:16], ALU.subtract))
                sx.add("scalar", lambda e, i, al=al: e.activation(al, al, ACT.Exp))
                init = (lambda a, b=b: b[:, TC - 1, a:a + 1]) if k else (lambda a: 0.0)
                sx.add(V, scans(same[:, chunk(k)], lambda a, k=k: alpha[:, chunk(k), a], lambda a, o=o: o[:, :, a],
                                init, ALU.mult, ALU.add))
                sx.add("sync", lambda e, i, k=k, o=o: e.dma_start(per_edge(run8_d)[:, chunk(k), :], o[:, :, :]), "hw")
            collect(sx, mx, run8_d, rc[(NCH - 1) % 2][:, TC - 1, :], HEADS)
            sx.add(V, lambda e, i: e.tensor_tensor(mx[:, :, :], mx[:, :, :], selfw[:, :, :], ALU.add))
            sx.add(V, lambda e, i: e.tensor_scalar(mx[:, :, :], mx[:, :, :], 1e-16, None, ALU.add))
            sx.add(V, lambda e, i: e.reciprocal(mx[:, :, :], mx[:, :, :]))
            sx.add(V, lambda e, i: e.tensor_scalar(am[:, :, 0:HEADS], mx[:, :, :], 1.0 / HEADS, None, ALU.mult))
            sx.add(V, lambda e, i: e.tensor_tensor(selfw[:, :, :], selfw[:, :, :], am[:, :, 0:HEADS], ALU.mult))
            sx.add("gpsimd", spread(am), "sw", J)
            sx.add("sync", lambda e, i: e.dma_start(per_node(am_d), am[:, :, :]), "hw")
            sx.add("gpsimd", get_first, "sw", 1)
            for k in range(NCH):
                sx.add("sync", lambda e, i, k=k: e.dma_start(tab[:, :, :], per_edge(spread_d)[:, chunk(k), :]), "hw")
                sx.add(V, scans(same[:, chunk(k)], lambda a: tab[:, :, a], lambda a: tab[:, :, a],
                                lambda a: tabl[:, a:a + 1], ALU.mult, ALU.add))
                sx.add(V, lambda e, i: e.tensor_copy(tabl[:, 0:HEADS], tab[:, TC - 1, 0:HEADS]))
                al = alpha[:, chunk(k), :]
                sx.add(V, lambda e, i, al=al: e.tensor_tensor(al, al, tab[:, :, 0:HEADS], ALU.mult))
            stage(sx)

        with ExitStack() as ctx:
            g = [sb(f"rows_l2_{h}", [P, BHALF, HD], f32, ctx) for h in range(2)]
            edge_pass("l2", hw_d, src_i, g, BHALF, alpha)

        with ExitStack() as ctx:
            res = sb("att_out", [P, J, D], f32, ctx)
            x1 = sb("x1", [P, J, D], f32, ctx)
            vecs = {n: sb(f"row_{n}", [P, D], f32, ctx) for n in ("batt", "g1", "be1", "g2", "be2", "bf2")}
            wf1_s = sb("wf1", [D, 2 * D], f32, ctx)
            bf1_s = sb("bf1", [P, 1], f32, ctx)
            wf2_s = sb("wf2", [2 * D, D], f32, ctx)
            feat = sb("self_features", [P, JB, HD], f32, ctx)
            sw7 = sb("self_weight_step", [P, JB, HEADS], f32, ctx)
            self7 = sb("self_message", [P, JB, D], f32, ctx)
            step7 = sb("x1_step", [P, JB, D], f32, ctx)
            t7 = sb("x1_step_t", [D, JB * P], f32, ctx)
            hid = sb("hidden2_t", [P, JB * P], f32, ctx)
            ch = chain("nodes2")
            rowsrc = {"batt": batt, "g1": g1, "be1": be1, "g2": g2, "be2": be2, "bf2": bf2}
            ch.add("sync", lambda e, i: [e.dma_start(vecs[n][:, :], rowsrc[n].partition_broadcast(P)) for n in vecs] +
                   [e.dma_start(wf1_s[:, :], wf1), e.dma_start(bf1_s[:, :], bf1), e.dma_start(wf2_s[:, :], wf2)],
                   "hw", 9)
            collect(ch, res, run_d, run[1][:, BHALF - 1, :], D)
            lp = chain("self_edges", J // JB)
            lp.add(V, lambda e, i: e.tensor_copy(sw7[:, :, :], selfw[:, bass.ds(i * JB, JB), :]))
            lp.add("sync", lambda e, i: e.dma_start(feat[:, :, :], per_node(hw_d)[:, bass.ds(i * JB, JB), :]), "hw")
            lp.add(V, lambda e, i: e.tensor_tensor(
                feat[:, :, :].rearrange("p j (a f) -> p (j a) f", f=D),
                feat[:, :, :].rearrange("p j (a f) -> p (j a) f", f=D),
                bc(sw7[:, :, :].rearrange("p j a -> p (j a)").unsqueeze(2), [P, JB * HEADS, D]), ALU.mult))
            lp.add(V, lambda e, i: e.tensor_reduce(self7[:, :, :],
                                                   feat[:, :, :].rearrange("p j (a f) -> p j f a", f=D), X, ALU.add))
            lp.add(V, lambda e, i: e.tensor_tensor(res[:, bass.ds(i * JB, JB), :], res[:, bass.ds(i * JB, JB), :],
                                                   self7[:, :, :], ALU.add))
            full = [P, J, D]
            ch2 = chain("norm_att")
            ch2.add(V, lambda e, i: e.tensor_tensor(res[:, :, :], res[:, :, :], hs[:, :, :], ALU.add))
            ch2.add(V, lambda e, i: e.tensor_tensor(res[:, :, :], res[:, :, :],
                                                    bc(vecs["batt"][:, :].unsqueeze(1), full), ALU.add))
            normalise(ch2, x1, res, hs, relu=False, gain=vecs["g1"], shift=vecs["be1"])
            lp2 = chain("ffn", J // JB)
            lp2.add(V, lambda e, i: e.tensor_copy(step7[:, :, :], x1[:, bass.ds(i * JB, JB), :]))
            lp2.add("tensor", transposes(step7, D))
            lp2.add("scalar", untranspose(t7, D))

            def up2(e, i):
                e.matmul(ps[2][:, :], wf1_s[:, :], t7[:, 0:512], start=True, stop=True)
                return e.matmul(ps[3][:, 0:JB * P - 512], wf1_s[:, :], t7[:, 512:JB * P], start=True, stop=True)
            lp2.add("tensor", up2)

            def relu2(e, i):
                e.activation(hid[:, 0:512], ps[2][:, :], ACT.Relu, bias=bf1_s[:, 0:1])
                return e.activation(hid[:, 512:JB * P], ps[3][:, 0:JB * P - 512], ACT.Relu, bias=bf1_s[:, 0:1])
            lp2.add("scalar", relu2)

            def down2(e, i):
                for j in range(JB):
                    last = e.matmul(ps[4][:, j * D:(j + 1) * D], hid[:, j * P:(j + 1) * P], wf2_s[:, :],
                                    start=True, stop=True)
                return last
            lp2.add("tensor", down2)
            lp2.add(V, lambda e, i: e.tensor_tensor(res[:, bass.ds(i * JB, JB), :], x1[:, bass.ds(i * JB, JB), :],
                                                    tiles(4), ALU.add))
            ch3 = chain("norm_ffn")
            ch3.add(V, lambda e, i: e.tensor_tensor(res[:, :, :], res[:, :, :],
                                                    bc(vecs["bf2"][:, :].unsqueeze(1), full), ALU.add))
            normalise(ch3, x1, res, hs, relu=False, gain=vecs["g2"], shift=vecs["be2"])
            ch3.add(V, lambda e, i: e.tensor_tensor(xs[:, :, :], xs[:, :, :], x1[:, :, :], ALU.add))
            normalise(ch3, hs, xs, res)
            stage(ch, lp, ch2, lp2, ch3)
        att.close()

        own = sb("own", [P, J, D])
        idx3 = sb("relation_index", [P, T], i32)
        with ExitStack() as ctx:
            typ = sb("edge_type", [P, T], i32, ctx)
            tf = sb("edge_type_f", [P, T], f32, ctx)
            w3_s = sb("w3", [D, 4 * D], f32, ctx)
            b3_s = sb("b3", [P, D], f32, ctx)
            step7 = sb("h3_step", [P, JB, D], f32, ctx)
            t7 = sb("h3_step_t", [D, JB * P], f32, ctx)
            rel = sb("relations", [P, 3, JB, D], f32, ctx)
            ch = chain("index3")
            ch.add(V, lambda e, i: e.memset(typ[:, :], 0))
            ch.add("sync", lambda e, i: load_runs(e, typ, edge_type) + [
                e.dma_start(w3_s[:, :], w3), e.dma_start(b3_s[:, :], b3.partition_broadcast(P))], "hw",
                   len(rows_of(P - 1)) + 3)
            ch.add(V, lambda e, i: e.tensor_scalar(tf[:, :], typ[:, :], float(NP), None, ALU.mult))
            ch.add(V, lambda e, i: e.tensor_tensor(idx3[:, :], tf[:, :], src_i[:, :], ALU.add))
            lp = chain("relations", J // JB)
            lp.add(V, lambda e, i: e.tensor_copy(step7[:, :, :], hs[:, bass.ds(i * JB, JB), :]))
            lp.add("tensor", transposes(step7, D))
            lp.add("scalar", untranspose(t7, D))

            def relate(e, i):
                for j in range(JB):
                    last = e.matmul(ps[2 + j // 2][:, (j % 2) * 256:(j % 2 + 1) * 256], t7[:, j * P:(j + 1) * P],
                                    w3_s[:, :], start=True, stop=True)
                return last
            lp.add("tensor", relate)

            def evac3(e, i):
                for j in range(JB):
                    o = ps[2 + j // 2][:, (j % 2) * 256:(j % 2) * 256 + 192].rearrange("p (r f) -> p r f", f=D)
                    last = e.copy(rel[:, :, j, :], o)
                return last
            lp.add("scalar", evac3)
            lp.add("sync", lambda e, i: [
                e.dma_start(per_node(y3_d[r * NP:(r + 1) * NP, :])[:, bass.ds(i * JB, JB), :], rel[:, r, :, :])
                for r in range(3)], "hw", 3)

            def keep(e, i):
                for b in range(4):
                    n = min(2, JB - 2 * b)
                    v = ps[2 + b][:, 0:n * 256].rearrange("p (j f) -> p j f", f=256)[:, :, 192:256]
                    last = e.tensor_tensor(own[:, bass.ds(i * JB + 2 * b, n), :], v,
                                           bc(b3_s[:, :].unsqueeze(1), [P, n, D]), ALU.add)
                return last
            lp.add(V, keep)
            stage(ch, lp)

        with ExitStack() as ctx:
            g = [sb(f"rows_l3_{h}", [P, HALF, D], f32, ctx) for h in range(2)]
            edge_pass("l3", y3_d, idx3, g, HALF)

        with ExitStack() as ctx:
            res = sb("rel_sum", [P, J, D], f32, ctx)
            ch = chain("nodes3")
            collect(ch, res, run_d, run[1][:, HALF - 1, :], D)
            ch.add(V, lambda e, i: e.tensor_tensor(res[:, :, :], res[:, :, :], own[:, :, :], ALU.add))
            ch.add(V, lambda e, i: e.scalar_tensor_tensor(res[:, :, :], res[:, :, :], 0.0, xs[:, :, :], ALU.max,
                                                          ALU.add))
            ch.add("sync", lambda e, i: node_rows(e, res, out, back=True), "hw", len(rows_of(PN)) + 1)
            stage(ch)


def kernel(**inputs):
    import numpy as _np
    import concourse.bacc as _bacc
    from concourse.bass_utils import run_bass_kernel_spmd as _run

    nc = _bacc.Bacc("TRN2", target_bir_lowering=False, num_devices=1)
    g = {k: _np.asarray(v) for k, v in inputs.items()}
    w_rel = g["L3_gnn_W_rel"]
    given = {
        "x": g["x"], "src": g["src"], "dst": g["dst"], "edge_attr": g["edge_attr_48"], "edge_type": g["edge_type_3"],
        "w0a": g["L0_gnn_W1"], "b0a": g["L0_gnn_b1"].reshape(2, 128).T, "w0b": g["L0_gnn_W2"], "b0b": g["L0_gnn_b2"],
        "w1": g["L1_gnn_W"], "b1": g["L1_gnn_b"],
        "watt": g["L2_gnn_W_att"], "att_s": g["L2_gnn_att_src"], "att_d": g["L2_gnn_att_dst"],
        "batt": g["L2_gnn_bias_att"], "wf1": g["L2_gnn_W1"], "bf1": g["L2_gnn_b1"].reshape(128, 1),
        "wf2": g["L2_gnn_W2"], "bf2": g["L2_gnn_b2"], "g1": g["L2_gnn_ln1_g"], "be1": g["L2_gnn_ln1_b"],
        "g2": g["L2_gnn_ln2_g"], "be2": g["L2_gnn_ln2_b"],
        "w3": _np.concatenate([w_rel[0].T, w_rel[1].T, w_rel[2].T, g["L3_gnn_W_self"].T], axis=1),
        "b3": g["L3_gnn_b_self"],
    }
    arrays, args = {}, []
    for name, a in given.items():
        a = _np.ascontiguousarray(a)
        arrays[f"in_{name}"] = a
        args.append(nc.dram_tensor(f"in_{name}", a.shape, mybir.dt.from_np(a.dtype), kind="ExternalInput").ap())
    args.append(nc.dram_tensor("out", g["x"].shape, f32, kind="ExternalOutput").ap())
    build(nc, *args)
    r = _run(nc, [arrays], core_ids=[0])
    return r.results[0]["out"]
```

```python
import concourse.bass as bass
from concourse import mybir
from contextlib import ExitStack

f32, i32, bf16 = mybir.dt.float32, mybir.dt.int32, mybir.dt.bfloat16
ALU = mybir.AluOpType
ACT = mybir.ActivationFunctionType
X = mybir.AxisListType.X
P = 128
D = 64
FE = 48
HEADS = 8
HD = HEADS * D
HALF = 26
NACC = 4
JB = 7
NCH = 4
BIG = 1e30
LN_EPS = 1e-5


def rows_of(n):
    a = n // 16 * 16
    return [(0, a), (a, n)] if a < n else [(0, n)]


class Chain:

    def __init__(self, nc, ctx, name, loops=0):
        self.sem = {k: ctx.enter_context(nc.semaphore(f"{name}_{k}")) for k in ("c", "hw", "sw")}
        self.pace = ctx.enter_context(nc.semaphore(f"{name}_pace"))
        self.loops, self.steps, self.prev = loops, [], None

    def end(self):
        kind = self.steps[-1][2]
        total = sum(1 if k == "c" else 16 * n for _, _, k, n in self.steps if k == kind)
        return self.sem[kind], total * self.loops + 1 if self.loops else total

    def add(self, engine, fn, kind="c", n=1):
        self.steps.append((engine, fn, kind, n))

    def run(self, engine, eng):
        total = {"c": 0, "hw": 0, "sw": 0}
        for _, _, kind, n in self.steps:
            total[kind] += 1 if kind == "c" else 16 * n
        if not any(s[0] == engine for s in self.steps):
            return
        if self.steps[0][0] == engine and self.prev:
            eng.wait_ge(*self.prev.end())
        if self.loops:
            assert self.steps[-1][2] == "c"
            if self.steps[0][0] == engine:
                eng.sem_inc(self.sem["c"], 1)
            with eng.Fori(0, self.loops) as i:
                self._body(engine, eng, i, total, 1)
        else:
            self._body(engine, eng, 0, total, 0)
            if self.steps[-1][0] == engine and self.steps[-1][2] != "c":
                eng.wait_ge(*self.end())

    def _body(self, engine, eng, i, total, credit):
        count = {"c": credit, "hw": 0, "sw": 0}
        before = "c"
        for e, fn, kind, n in self.steps:
            if e == engine and (count[before] or credit):
                eng.wait_ge(self.sem[before], i * total[before] + count[before])
                if self.loops and engine == "tensor":
                    eng.sem_inc(self.pace, 1)
            if e == engine:
                done = fn(eng, i)
                for d in done if isinstance(done, list) else [done]:
                    d.then_inc(self.sem[kind], 1 if kind == "c" else 16)
            count[kind] += 1 if kind == "c" else 16 * n
            before = kind


def build(nc, x, src, dst, edge_attr, edge_type, w0a, b0a, w0b, b0b, w1, b1, watt, att_s, att_d, batt, wf1, bf1, wf2,
          bf2, g1, be1, g2, be2, w3, b3, out):
    N, E = x.shape[0], src.shape[0]
    T = -(-E // (P * 2 * HALF)) * 2 * HALF
    EP = P * T
    J = -(-(N + 1) // (P * JB)) * JB
    NP = P * J
    HI = NP // P
    TF = E // P
    REST = E - TF * P
    TC = T // NCH
    DUMP = NP
    TAILE = E - (P - 1) * T
    PN, TAILN = N // J, N - N // J * J
    assert TF == T - 1 and 0 < REST < P and 0 < TAILE <= T and HI <= P and PN == P - 1 and 0 < TAILN < J

    def dram(name, shape, dt=f32):
        return nc.dram_tensor(name, shape, dt).ap()

    acc_d = [dram(f"acc{k}", [NP + P, D]) for k in range(NACC)]
    h1_d = dram("h1_table", [NP, D])
    as_d = dram("att_src_table", [NP, HEADS])
    hw_d = dram("att_feature_table", [NP, HD])
    y3_d = dram("relation_table", [3 * NP, D])
    run_d = dram("running_sums", [EP, D])
    run8_d = dram("running_heads", [EP, HEADS])
    spread_d = dram("spread", [EP + NP, 2 * HEADS])
    am_d = dram("node_att_max", [NP, 2 * HEADS])
    cnt_d = dram("degree", [NP])
    end_d = dram("segment_end", [NP])

    def per_node(t):
        return t.rearrange("(p j) f -> p j f", j=J)

    def per_edge(t):
        return t[0:EP, :].rearrange("(p t) f -> p t f", t=T)

    top = ExitStack()
    with top:
        def sb(name, shape, dt=f32, ctx=top):
            return ctx.enter_context(nc.sbuf_tensor(name, shape, dt))

        def sem(name):
            return top.enter_context(nc.semaphore(name))

        ps = [top.enter_context(nc.psum_tensor(f"bank{b}", [P, 512], f32)) for b in range(8)]
        xs = sb("x_nodes", [P, J, D])
        hs = sb("h_nodes", [P, J, D])
        st = sb("node_stat", [P, J])
        st2 = sb("node_stat2", [P, J])
        src_i = sb("src_i", [P, T], i32)
        same = sb("same_dst", [P, T])
        ident = sb("ident", [P, P])
        link = sb("link", [P, J, P])
        last_i = sb("last_edge", [P, J], i32)
        start_i = sb("start_edge", [P, J], i32)
        first_i = sb("first_dst", [P, 1], i32)
        last_f = sb("last_dst_f", [P, 1])
        nonempty = sb("nonempty", [P, J])
        rdeg = sb("one_over_degree", [P, J])
        run = [sb(f"run{h}", [P, HALF, D]) for h in range(2)]
        idx = [sb(f"idx{h}", [P, HALF], i32) for h in range(2)]
        mask = [sb(f"mask{h}", [P, HALF]) for h in range(2)]

        def bc(ap, shape):
            return ap.to_broadcast(shape)

        def normalise(ch, dst_t, src_t, tmp, relu=True, gain=None, shift=None):
            full = [P, J, D]
            s3, q3 = st[:, :].unsqueeze(2), st2[:, :].unsqueeze(2)
            V = "vector"
            ch.add(V, lambda e, i: e.tensor_reduce(st[:, :], src_t[:, :, :], X, ALU.add))
            ch.add(V, lambda e, i: e.tensor_scalar(st[:, :], st[:, :], 1.0 / D, None, ALU.mult))
            ch.add(V, lambda e, i: e.tensor_tensor(dst_t[:, :, :], src_t[:, :, :], bc(s3, full), ALU.subtract))
            ch.add(V, lambda e, i: e.tensor_tensor(tmp[:, :, :], dst_t[:, :, :], dst_t[:, :, :], ALU.mult))
            ch.add(V, lambda e, i: e.tensor_reduce(st2[:, :], tmp[:, :, :], X, ALU.add))
            ch.add(V, lambda e, i: e.tensor_scalar(st2[:, :], st2[:, :], 1.0 / D, LN_EPS, ALU.mult, ALU.add))
            ch.add("scalar", lambda e, i: e.activation(st2[:, :], st2[:, :], ACT.Sqrt))
            ch.add(V, lambda e, i: e.reciprocal(st2[:, :], st2[:, :]))
            ch.add(V, lambda e, i: e.tensor_tensor(dst_t[:, :, :], dst_t[:, :, :], bc(q3, full), ALU.mult))
            if relu:
                ch.add(V, lambda e, i: e.tensor_scalar(dst_t[:, :, :], dst_t[:, :, :], 0.0, None, ALU.max))
            if gain is not None:
                ch.add(V, lambda e, i: e.tensor_tensor(dst_t[:, :, :], dst_t[:, :, :],
                                                       bc(gain[:, :].unsqueeze(1), full), ALU.mult))
                ch.add(V, lambda e, i: e.tensor_tensor(dst_t[:, :, :], dst_t[:, :, :],
                                                       bc(shift[:, :].unsqueeze(1), full), ALU.add))

        def stage(*chains):
            for a, b in zip(chains, chains[1:]):
                b.prev = a
            with nc.Block() as block:
                for name in ("sync", "gpsimd", "scalar", "vector", "tensor"):
                    def body(e, name=name):
                        for ch in chains:
                            ch.run(name, e)
                    getter = {"sync": block.sync, "gpsimd": block.gpsimd, "scalar": block.scalar,
                              "vector": block.vector, "tensor": block.tensor}[name]
                    getter(body)

        def chain(name, loops=0):
            return Chain(nc, top, name, loops)

        l0 = ExitStack()
        src0 = sb("src0", [P, T + HALF], i32, l0)
        src0f = sb("src0f", [P, T + HALF], f32, l0)
        dlo = sb("dst_lo", [P, T], f32, l0)
        dhi = sb("dst_hi", [P, T], f32, l0)
        hist = sb("hist", [P, P], f32, l0)
        iota = sb("iota_row", [P, P], f32, l0)
        lower = sb("strict_lower", [P, P], f32, l0)
        upper = sb("strict_upper", [P, P], f32, l0)
        dumprow = sb("dump_row", [P, 1], f32, l0)
        zero = sb("zero", [P, 1024], f32, l0)
        c0 = ExitStack()
        dst_i = sb("dst_i", [P, T], i32, c0)
        dtmp = sb("dst_tmp", [P, T], i32, c0)
        edge_d = sb("edge_of_runs", [P, 3], i32, c0)
        edge_f = sb("edge_of_runs_f", [P, 3], f32, c0)
        prevf = sb("prev_f", [P, 1], f32, c0)
        linkf = sb("link_dst", [P, 1], f32, c0)

        def load_runs(e, tile, flat):
            body = flat[0:(P - 1) * T].rearrange("(p t) -> p t", t=T)
            d = [e.dma_start(tile[a:b, :], body[a:b, :]) for a, b in rows_of(P - 1)]
            return d + [e.dma_start(tile[P - 1:P, 0:TAILE], flat[(P - 1) * T:E].unsqueeze(0))]

        def node_rows(e, tile, flat, back=False):
            body = flat[0:PN * J, :].rearrange("(p j) f -> p j f", j=J)
            pairs = [(tile[a:b, :, :], body[a:b, :, :]) for a, b in rows_of(PN)]
            pairs.append((tile[PN:PN + 1, 0:TAILN, :], flat[PN * J:N, :].unsqueeze(0)))
            return [e.dma_start(b, a) if back else e.dma_start(a, b) for a, b in pairs]

        ch = chain("setup")

        def clear(e, i):
            e.memset(xs[:, :, :], 0.0)
            e.memset(src_i[:, :], 0)
            e.memset(dst_i[:, :], N)
            e.memset(src0[:, :], N)
            e.memset(zero[:, :], 0.0)
            e.memset(hist[:, :], 0.0)
            e.memset(lower[:, :], 1.0)
            e.memset(upper[:, :], 1.0)
            e.memset(run[1][:, :, :], 0.0)
            e.memset(edge_d[:, :], -1)
            return e.memset(ident[:, :], 0.0)
        ch.add("vector", clear)

        def loads(e, i):
            a = node_rows(e, xs, x) + load_runs(e, src_i, src) + load_runs(e, dst_i, dst)
            a.append(e.dma_start(src0[:, 0:TF], src[0:P * TF].rearrange("(p t) -> p t", t=TF)))
            col = src.unsqueeze(1)
            dcol = dst.unsqueeze(1)
            with nc.allow_non_contiguous_dma(reason="one column of indices"):
                a.append(e.dma_start(src0[0:REST, TF:T], col[P * TF:E, :]))
            return a
        n_loads = len(rows_of(PN)) + 1 + 2 * (len(rows_of(P - 1)) + 1) + 2
        ch.add("sync", loads, "hw", n_loads)

        def zero_tables(e, i):
            a = []
            for k in range(NACC):
                flat = acc_d[k].rearrange("(p a) f -> p (a f)", p=P)
                w = flat.shape[1]
                for c in range(0, w, 1024):
                    a.append(e.dma_start(flat[:, c:min(c + 1024, w)], zero[:, 0:min(1024, w - c)]))
            flat = spread_d[0:EP, :].rearrange("(p t) f -> p (t f)", p=P)
            w = flat.shape[1]
            for c in range(0, w, 1024):
                a.append(e.dma_start(flat[:, c:min(c + 1024, w)], zero[:, 0:min(1024, w - c)]))
            return a
        n_zero = NACC * -(-((NP + P) * D // P) // 1024) + -(-(T * 2 * HEADS) // 1024)
        ch.add("sync", zero_tables, "hw", n_zero)

        def edges_in(e, i):
            return [e.dma_start(edge_d[:, 1:2], dst_i[:, T - 1:T]), e.dma_start(edge_d[0:P - 1, 2:3], dst_i[1:P, 0:1])]
        ch.add("sync", edges_in, "hw", 2)
        prev_d = sb("prev_d", [P, 1], i32, c0)
        ch.add("vector", lambda e, i: e.memset(prev_d[:, :], -1))
        ch.add("sync", lambda e, i: e.dma_start(prev_d[1:P, :], dst_i[0:P - 1, T - 1:T]), "hw")

        def constants(e, i):
            e.iota(iota[:, :], [[1, P]], base=0, channel_multiplier=0, allow_small_or_imprecise_dtypes=True)
            e.iota(dumprow[:, :], [[0, 1]], base=DUMP, channel_multiplier=1, allow_small_or_imprecise_dtypes=True)
            e.iota(link[:, :, :], [[1, J], [J, P]], base=0, channel_multiplier=0, allow_small_or_imprecise_dtypes=True)
            e.affine_select(out=ident[:, :], in_=ident[:, :], compare_op=ALU.not_equal, fill=1.0, base=0,
                            pattern=[[-1, P]], channel_multiplier=1)
            e.affine_select(out=lower[:, :], in_=lower[:, :], compare_op=ALU.is_gt, fill=0.0, base=0,
                            pattern=[[-1, P]], channel_multiplier=1)
            return e.affine_select(out=upper[:, :], in_=upper[:, :], compare_op=ALU.is_gt, fill=0.0, base=0,
                                   pattern=[[1, P]], channel_multiplier=-1)
        ch.add("gpsimd", constants)
        V = "vector"

        def same_a(e, i):
            e.tensor_tensor(same[:, 1:T], dst_i[:, 1:T], dst_i[:, 0:T - 1], ALU.is_equal)
            e.tensor_tensor(same[:, 0:1], dst_i[:, 0:1], prev_d[:, :], ALU.is_equal)
            e.tensor_copy(edge_f[:, :], edge_d[:, :])
            e.tensor_copy(first_i[:, :], dst_i[:, 0:1])
            e.tensor_copy(last_f[:, :], dst_i[:, T - 1:T])
            e.tensor_copy(src0f[:, :], src0[:, :])
            return e.tensor_scalar(dtmp[:, :], dst_i[:, :], P - 1, None, ALU.bitwise_and)
        ch.add(V, same_a)
        ch.add(V, lambda e, i: e.tensor_copy(dlo[:, :], dtmp[:, :]))
        ch.add(V, lambda e, i: e.tensor_scalar(dtmp[:, :], dst_i[:, :], 7, None, ALU.logical_shift_right))
        ch.add(V, lambda e, i: e.tensor_copy(dhi[:, :], dtmp[:, :]))
        ch.add(V, lambda e, i: e.tensor_tensor(prevf[:, :], edge_f[:, 1:2], edge_f[:, 2:3], ALU.is_equal))
        ch.add(V, lambda e, i: e.scalar_tensor_tensor(linkf[:, :], edge_f[:, 1:2], 1.0, prevf[:, :], ALU.add,
                                                      ALU.mult))
        ch.add(V, lambda e, i: e.tensor_scalar(linkf[:, :], linkf[:, :], -1.0, None, ALU.add))
        ch.add(V, lambda e, i: e.tensor_scalar(link[:, :, :], link[:, :, :], linkf[:, 0:1], None, ALU.is_equal))
        stage(ch)
        c0.close()

        GROUPS = [(r, min(r + 4, HALF)) for r in range(0, HALF, 4)]
        NG = len(GROUPS)
        assert NG % 2

        with ExitStack() as ctx:
            attr = [sb(f"attr{h}", [P, HALF, FE], f32, ctx) for h in range(2)]
            pack = [sb(f"attr_and_one{h}", [P, HALF, FE + 1], f32, ctx) for h in range(2)]
            val = [sb(f"val{h}", [P, HALF, D], f32, ctx) for h in range(2)]
            eq = [sb(f"eq{k}", [P, 4, P], f32, ctx) for k in range(2)]
            sfs = [sb(f"src_tile{h}", [P, HALF], f32, ctx) for h in range(2)]
            dups = [sb(f"dups{h}", [P, HALF], f32, ctx) for h in range(2)]
            scr = [sb(f"scratch{k}", [P, P], f32, ctx) for k in range(8)]
            tgt = sb("target_f", [P, HALF], f32, ctx)
            ohlo = [sb(f"onehot_lo{h}", [P, HALF, P], bf16, ctx) for h in range(2)]
            ohhi = [sb(f"onehot_hi{h}", [P, HALF, HI], bf16, ctx) for h in range(2)]
            s_attr = [sem(f"l0_attr{h}") for h in range(2)]
            s_stage, s_psrc, s_eq, s_sum, s_val, s_hot, s_hist, s_hadd, s_dup, s_tgt, s_vfree, s_acc = (
                sem(f"l0_{n}") for n in ("staged", "src_rows", "equal", "summed", "values", "onehots", "hist",
                                         "hist_added", "dup", "targets", "val_free", "pace"))
            s_add = [sem(f"l0_acc{k}") for k in range(NACC)]
            s_init, s_tail, s_pack = sem("l0_init"), sem("l0_tail"), sem("l0_packed")
            LOOPS = T // (2 * HALF)
            attr_v = edge_attr[0:P * TF, :].rearrange("(p t) f -> p t f", t=TF)

            with nc.Block() as block:
                @block.sync
                def _(e):
                    e.wait_ge(s_init, 1)
                    def load(i, h, last=False):
                        e.wait_ge(s_pack, i * 2 + h + 1)
                        t0 = (i * 2 + h) * HALF
                        if last:
                            e.dma_start(attr[h][:, HALF - 1, :], zero[:, 0:FE]).then_inc(s_tail, 16)
                            e.wait_ge(s_tail, 16)
                            e.dma_start(attr[h][0:REST, HALF - 1, :], edge_attr[P * TF:E, :]).then_inc(s_tail, 16)
                            e.wait_ge(s_tail, 32)
                            e.dma_start(attr[h][:, 0:HALF - 1, :], attr_v[:, t0:TF, :]).then_inc(s_attr[h], 16)
                        else:
                            e.dma_start(attr[h][:, :, :], attr_v[:, bass.ds(t0, HALF), :]).then_inc(s_attr[h], 16)
                    if LOOPS > 1:
                        with e.Fori(0, LOOPS - 1) as i:
                            load(i, 0)
                            load(i, 1)
                    load(LOOPS - 1, 0)
                    load(LOOPS - 1, 1, last=True)

                @block.tensor
                def _(e):
                    e.sem_inc(s_sum, 2 * NG + 1)
                    e.wait_ge(s_init, 1)
                    with e.Fori(0, LOOPS) as i:
                        for h in range(2):
                            hh = i * 2 + h
                            e.wait_ge(s_stage, hh + 1)

                            def rows(k):
                                lo, hi = GROUPS[k]
                                e.wait_ge(s_eq, hh * NG + k + 1)
                                for r in range(lo, hi):
                                    last = e.transpose(ps[(h + k) % 2][:, (r - lo) * P:(r - lo + 1) * P],
                                                       bc(sfs[h][:, r:r + 1], [P, P]), ident[:, :])
                                last.then_inc(s_psrc, 1)

                            def sums(k):
                                lo, hi = GROUPS[k]
                                e.wait_ge(s_eq, hh * NG + k + 3)
                                e.wait_ge(s_val, hh * NG + k + 1)
                                if k == 0:
                                    e.wait_ge(s_pack, hh + 3)
                                for r in range(lo, hi):
                                    o = ps[2 + (h + k) % 2][:, (r - lo) * D:(r - lo + 1) * D]
                                    same_src = eq[(h + k) % 2][:, r - lo, :]
                                    last = e.matmul(o[:, 0:FE + 1], same_src, pack[h][:, r, :], start=True, stop=True)
                                last.then_inc(s_sum, 1)

                            rows(0)
                            for k in range(1, NG):
                                rows(k)
                                sums(k - 1)
                            sums(NG - 1)
                            e.wait_ge(s_hot, hh + 1)
                            e.wait_ge(s_hadd, hh + 1)
                            for r in range(HALF):
                                last = e.matmul(ps[4][0:HI, 0:P], ohhi[h][:, r, :], ohlo[h][:, r, :],
                                                start=(r == 0), stop=(r == HALF - 1))
                            last.then_inc(s_hist, 1)

                @block.vector
                def _(e):
                    e.memset(ps[4][:, 0:P], 0.0)
                    for h in range(2):
                        e.memset(val[h][:, :, :], 0.0)
                        e.memset(pack[h][:, :, FE:FE + 1], 1.0)
                        last = e.memset(attr[h][:, :, :], 0.0)
                    last.then_inc(s_init, 1)
                    e.sem_inc(s_eq, 2)
                    e.sem_inc(s_hist, 1)
                    e.wait_ge(s_init, 1)
                    with e.Fori(0, LOOPS) as i:
                        for h in range(2):
                            hh = i * 2 + h
                            t0 = hh * HALF
                            e.wait_ge(s_stage, hh + 1)
                            for k, (lo, hi) in enumerate(GROUPS):
                                G, n, m = hh * NG + k, hi - lo, (h + k) % 2
                                e.wait_ge(s_psrc, G + 1)
                                e.wait_ge(s_sum, G + 2 * NG)
                                e.wait_ge(s_eq, G + 1)
                                for r in range(lo, hi):
                                    e.scalar_tensor_tensor(scr[4 * m + r - lo][:, :], ps[m][:, (r - lo) * P:(r - lo + 1) * P],
                                                           sfs[h][:, r:r + 1], lower[:, :], ALU.is_equal, ALU.mult,
                                                           accum_out=dups[h][:, r:r + 1])
                                e.tensor_tensor(eq[m][:, 0:n, :], ps[m][:, 0:n * P].rearrange("p (r j) -> p r j", j=P),
                                                bc(sfs[h][:, lo:hi].unsqueeze(2), [P, n, P]), ALU.is_equal)\
                                 .then_inc(s_eq, 1)
                            e.wait_ge(s_eq, (hh + 1) * NG + 2)
                            e.tensor_scalar(dups[h][:, :], dups[h][:, :], 0.0, None, ALU.is_equal).then_inc(s_dup, 1)
                            e.wait_ge(s_dup, hh * 3 + 1)
                            e.scalar_tensor_tensor(tgt[:, :], sfs[h][:, :], dumprow[:, 0:1], dups[h][:, :],
                                                   ALU.subtract, ALU.mult).then_inc(s_dup, 1)
                            e.wait_ge(s_dup, hh * 3 + 2)
                            e.tensor_scalar(tgt[:, :], tgt[:, :], dumprow[:, 0:1], None, ALU.add).then_inc(s_dup, 1)
                            e.wait_ge(s_dup, hh * 3 + 3)
                            e.wait_ge(s_vfree, hh + 1)
                            e.tensor_copy(idx[h][:, :], tgt[:, :]).then_inc(s_tgt, 1)
                            e.tensor_tensor(ohlo[h][:, :, :], bc(iota[:, :].unsqueeze(1), [P, HALF, P]),
                                            bc(dlo[:, bass.ds(t0, HALF)].unsqueeze(2), [P, HALF, P]), ALU.is_equal)
                            e.tensor_tensor(ohhi[h][:, :, :], bc(iota[:, 0:HI].unsqueeze(1), [P, HALF, HI]),
                                            bc(dhi[:, bass.ds(t0, HALF)].unsqueeze(2), [P, HALF, HI]),
                                            ALU.is_equal).then_inc(s_hot, 1)
                            e.wait_ge(s_hist, hh + 1)
                            e.tensor_tensor(hist[0:HI, :], hist[0:HI, :], ps[4][0:HI, 0:P], ALU.add)\
                             .then_inc(s_hadd, 1)
                    e.wait_ge(s_hist, 2 * LOOPS + 1)
                    e.wait_ge(s_hadd, 2 * LOOPS)
                    e.tensor_tensor(hist[0:HI, :], hist[0:HI, :], ps[4][0:HI, 0:P], ALU.add)

                @block.scalar
                def _(e):
                    e.wait_ge(s_init, 1)
                    e.sem_inc(s_val, 2)
                    e.sem_inc(s_pack, 2)
                    e.copy(sfs[0][:, :], src0f[:, 0:HALF]).then_inc(s_stage, 1)
                    with e.Fori(0, LOOPS) as i:
                        for h in range(2):
                            hh = i * 2 + h
                            e.wait_ge(s_tgt, hh + 2)
                            e.copy(sfs[1 - h][:, :], src0f[:, bass.ds((hh + 1) * HALF, HALF)]).then_inc(s_stage, 1)
                            e.wait_ge(s_attr[h], (i + 1) * 16)
                            e.copy(pack[h][:, :, 0:FE], attr[h][:, :, :]).then_inc(s_pack, 1)
                            e.wait_ge(s_vfree, hh + 1)
                            for k, (lo, hi) in enumerate(GROUPS):
                                n = hi - lo
                                e.wait_ge(s_sum, hh * NG + k + 1 + 2 * NG + 1)
                                e.copy(val[h][:, lo:hi, 0:FE + 1],
                                       ps[2 + (h + k) % 2][:, 0:n * D].rearrange("p (u f) -> p u f", f=D)[:, :, 0:FE + 1])\
                                 .then_inc(s_val, 1)

                @block.gpsimd
                def _(e):
                    e.sem_inc(s_vfree, 1)
                    e.sem_inc(s_tgt, 2)
                    for k in range(NACC):
                        e.dma_start(acc_d[k][0:1, :], zero[0:1, 0:D]).then_inc(s_add[k], 16)
                    with e.Fori(0, LOOPS) as i:
                        for h in range(2):
                            hh = i * 2 + h
                            e.wait_ge(s_tgt, hh + 3)
                            e.wait_ge(s_val, (hh + 1) * NG + 2)
                            for r in range(HALF):
                                q, k = divmod(h * HALF + r, NACC)
                                e.wait_ge(s_add[k], (i * (2 * HALF // NACC) + q) * 16 + 16)
                                e.sem_inc(s_acc, 1)
                                e.indirect_dma_start(acc_d[k], bass.IndirectOffsetOnAxis(ap=idx[h][:, r:r + 1], axis=0),
                                                     val[h][:, r, :], None, compute_op=ALU.add).then_inc(s_add[k], 16)
                                if r == NACC - 1:
                                    e.sem_inc(s_vfree, 1)
                    for k in range(NACC):
                        e.wait_ge(s_add[k], 16 * (LOOPS * (2 * HALF // NACC) + 1))

        with ExitStack() as ctx:
            cum = sb("cum", [P, P], f32, ctx)
            before = sb("before", [P, 1], f32, ctx)
            endf = sb("end_f", [P, J], f32, ctx)
            degf = sb("deg_f", [P, J], f32, ctx)
            dumpn = sb("dump_n", [P, J], f32, ctx)
            agg = sb("agg", [P, J, D], f32, ctx)
            part = sb("part", [P, J, D], f32, ctx)
            both = sb("both", [P, J, D + FE], f32, ctx)
            bothj = sb("both_step", [P, JB, D + FE], f32, ctx)
            ct = sb("both_t", [D + FE, JB * P], f32, ctx)
            ht = sb("hidden_t", [P, 2, JB * P], f32, ctx)
            w0a_s = sb("w0a", [D + FE, 256], f32, ctx)
            w0b_s = sb("w0b", [P, 2, D], f32, ctx)
            b0a_s = sb("b0a", [P, 2], f32, ctx)
            b0b_s = sb("b0b", [P, D], f32, ctx)
            V = "vector"
            ch = chain("nodes0")
            ch.add("sync", lambda e, i: [
                e.dma_start(agg[:, :, :], per_node(acc_d[0][0:NP, :])), e.dma_start(w0a_s[:, :], w0a),
                e.dma_start(w0b_s[:, :, :], w0b.rearrange("(c p) n -> p c n", p=P)),
                e.dma_start(b0a_s[:, :], b0a), e.dma_start(b0b_s[:, :], b0b.partition_broadcast(P))], "hw", 5)
            ch.add(V, lambda e, i: e.memset(cum[:, :], 1.0))
            ch.add(V, lambda e, i: e.tensor_tensor_scan(cum[0:HI, :], cum[0:HI, :], hist[0:HI, :], 0.0, ALU.mult,
                                                        ALU.add))
            ch.add("tensor", lambda e, i: e.matmul(ps[0][0:HI, 0:1], upper[0:HI, 0:HI], cum[0:HI, P - 1:P],
                                                   start=True, stop=True))
            ch.add(V, lambda e, i: e.tensor_copy(before[0:HI, :], ps[0][0:HI, 0:1]))
            ch.add(V, lambda e, i: e.tensor_scalar(cum[0:HI, :], cum[0:HI, :], before[0:HI, 0:1], None, ALU.add))
            ch.add("sync", lambda e, i: [e.dma_start(end_d.rearrange("(a b) -> a b", b=P), cum[0:HI, :]),
                                         e.dma_start(cnt_d.rearrange("(a b) -> a b", b=P), hist[0:HI, :])], "hw", 2)
            ch.add("sync", lambda e, i: [e.dma_start(endf[:, :], end_d.rearrange("(p j) -> p j", j=J)),
                                         e.dma_start(degf[:, :], cnt_d.rearrange("(p j) -> p j", j=J))], "hw", 2)
            ch.add("gpsimd", lambda e, i: e.iota(dumpn[:, :], [[1, J]], base=EP, channel_multiplier=J,
                                                 allow_small_or_imprecise_dtypes=True))

            def ends(e, i):
                e.tensor_scalar(last_i[:, :], endf[:, :], -1.0, 0.0, ALU.add, ALU.max)
                e.tensor_scalar(rdeg[:, :], degf[:, :], 1.0, None, ALU.max)
                e.tensor_scalar(nonempty[:, :], degf[:, :], 0.0, None, ALU.is_gt)
                return e.tensor_tensor(endf[:, :], endf[:, :], degf[:, :], ALU.subtract)
            ch.add(V, ends)
            ch.add(V, lambda e, i: e.tensor_tensor(endf[:, :], endf[:, :], dumpn[:, :], ALU.subtract))
            ch.add(V, lambda e, i: e.tensor_tensor(endf[:, :], endf[:, :], nonempty[:, :], ALU.mult))
            ch.add(V, lambda e, i: e.tensor_tensor(start_i[:, :], endf[:, :], dumpn[:, :], ALU.add))
            ch.add(V, lambda e, i: e.reciprocal(rdeg[:, :], rdeg[:, :]))
            for k in range(1, NACC):
                ch.add("sync", lambda e, i, k=k: e.dma_start(part[:, :, :], per_node(acc_d[k][0:NP, :])), "hw")
                ch.add(V, lambda e, i: e.tensor_tensor(agg[:, :, :], agg[:, :, :], part[:, :, :], ALU.add))
            ch.add(V, lambda e, i: e.tensor_scalar(st[:, :], agg[:, :, FE], 1.0, None, ALU.max))
            ch.add(V, lambda e, i: e.reciprocal(st[:, :], st[:, :]))
            ch.add(V, lambda e, i: e.tensor_tensor(both[:, :, D:D + FE], agg[:, :, 0:FE],
                                                   bc(st[:, :].unsqueeze(2), [P, J, FE]), ALU.mult))
            normalise(ch, hs, xs, part)
            ch.add(V, lambda e, i: e.tensor_copy(both[:, :, 0:D], hs[:, :, :]))
            ch.add(V, lambda e, i: e.tensor_tensor(xs[:, :, :], xs[:, :, :], bc(b0b_s[:, :].unsqueeze(1), [P, J, D]),
                                                   ALU.add))

            lp = chain("mlp0", J // JB)
            lp.add(V, lambda e, i: e.tensor_copy(bothj[:, :, :], both[:, bass.ds(i * JB, JB), :]))

            def transposes(src_t, width):
                def fn(e, i):
                    for j in range(JB):
                        o = ps[j // 4][0:width, (j % 4) * P:(j % 4 + 1) * P]
                        last = e.transpose(o, src_t[:, j, 0:width], ident[:, :])
                    return last
                return fn

            def untranspose(dst_t, width):
                def fn(e, i):
                    e.copy(dst_t[0:width, 0:512], ps[0][0:width, :])
                    return e.copy(dst_t[0:width, 512:JB * P], ps[1][0:width, 0:JB * P - 512])
                return fn
            lp.add("tensor", transposes(bothj, D + FE))
            lp.add("scalar", untranspose(ct, D + FE))

            def up0(e, i):
                for c in range(2):
                    for b, (lo, hi) in enumerate(((0, 512), (512, JB * P))):
                        last = e.matmul(ps[2 + 2 * c + b][:, 0:hi - lo], w0a_s[:, c * P:(c + 1) * P], ct[:, lo:hi],
                                        start=True, stop=True)
                return last
            lp.add("tensor", up0)

            def relu0(e, i):
                for c in range(2):
                    for b, (lo, hi) in enumerate(((0, 512), (512, JB * P))):
                        last = e.activation(ht[:, c, lo:hi], ps[2 + 2 * c + b][:, 0:hi - lo], ACT.Relu,
                                            bias=b0a_s[:, c:c + 1])
                return last
            lp.add("scalar", relu0)

            def down0(e, i):
                for j in range(JB):
                    for c in range(2):
                        last = e.matmul(ps[6][:, j * D:(j + 1) * D], ht[:, c, j * P:(j + 1) * P], w0b_s[:, c, :],
                                        start=(c == 0), stop=(c == 1))
                return last
            lp.add("tensor", down0)

            def tiles(bank, n=JB, w=D):
                return ps[bank][:, 0:n * w].rearrange("p (j f) -> p j f", f=w)
            lp.add(V, lambda e, i: e.tensor_tensor(xs[:, bass.ds(i * JB, JB), :], xs[:, bass.ds(i * JB, JB), :],
                                                   tiles(6), ALU.add))
            ch2 = chain("norm1")
            normalise(ch2, hs, xs, part)
            ch2.add("sync", lambda e, i: e.dma_start(per_node(h1_d), hs[:, :, :]), "hw")
            stage(ch, lp, ch2)
        l0.close()


        def edge_pass(name, table, index, gbuf, alpha=None):
            LP = T // (2 * HALF)
            wide = alpha is not None
            s_rows = [sem(f"{name}_rows{k}") for k in range(NG if wide else 2)]
            s_st = [sem(f"{name}_store{h}") for h in range(2)]
            s_idx, s_pace, s_step, s_run, s_mul, s_mix, s_free = (
                sem(f"{name}_{n}") for n in ("staged", "pace", "step", "run", "scaled", "mixed", "free"))
            with ExitStack() as ctx, nc.Block() as block:
                if wide:
                    astage = [sb(f"{name}_alpha{h}", [P, HALF, HEADS], f32, ctx) for h in range(2)]
                    mixed = sb(f"{name}_mixed", [P, 4, D], f32, ctx)

                @block.scalar
                def _(e):
                    with e.Fori(0, LP) as i:
                        for h in range(2):
                            hh = i * 2 + h
                            e.wait_ge(s_run, hh + 1)
                            e.copy(idx[h][:, :], index[:, bass.ds(hh * HALF, HALF)])
                            if wide:
                                e.copy(astage[h][:, :, :], alpha[:, bass.ds(hh * HALF, HALF), :])
                            e.copy(mask[h][:, :], same[:, bass.ds(hh * HALF, HALF)]).then_inc(s_idx, 1)

                @block.gpsimd
                def _(e):
                    with e.Fori(0, LP) as i:
                        for h in range(2):
                            hh = i * 2 + h
                            e.wait_ge(s_idx, hh + 1)
                            e.sem_inc(s_pace, 1)
                            for k, (lo, hi) in enumerate(GROUPS):
                                if wide:
                                    e.wait_ge(s_free, hh * NG + k + 1)
                                    e.sem_inc(s_pace, 1)
                                for r in range(lo, hi):
                                    to = gbuf[0 if wide else h][:, r, :]
                                    e.indirect_dma_start(to, None, table,
                                                         bass.IndirectOffsetOnAxis(ap=idx[h][:, r:r + 1], axis=0))\
                                     .then_inc(s_rows[k if wide else h], 16)

                @block.vector
                def _(e):
                    e.sem_inc(s_run, 2)
                    if wide:
                        e.sem_inc(s_free, NG)
                    e.memset(run[1][:, HALF - 1, :], 0.0).then_inc(s_step, 1)
                    with e.Fori(0, LP) as i:
                        for h in range(2):
                            hh = i * 2 + h

                            def step(r, row):
                                before_row = run[h][:, r - 1, :] if r else run[1 - h][:, HALF - 1, :]
                                e.wait_ge(s_step, hh * HALF + r + 1)
                                e.scalar_tensor_tensor(run[h][:, r, :], before_row, mask[h][:, r:r + 1], row,
                                                       ALU.mult, ALU.add).then_inc(s_step, 1)

                            def scale(k):
                                lo, hi = GROUPS[k]
                                e.wait_ge(s_rows[k], (hh + 1) * 16 * (hi - lo))
                                g3 = gbuf[0][:, lo:hi, :].rearrange("p r (a f) -> p (r a) f", f=D)
                                a3 = astage[h][:, lo:hi, :].rearrange("p r a -> p (r a)").unsqueeze(2)
                                e.tensor_tensor(g3, g3, bc(a3, [P, (hi - lo) * HEADS, D]), ALU.mult)\
                                 .then_inc(s_mul, 1)

                            def steps(k):
                                lo, hi = GROUPS[k]
                                G = hh * NG + k
                                e.wait_ge(s_mix, G + 1)
                                e.wait_ge(s_step, hh * HALF + lo + 1)
                                g4 = gbuf[0][:, lo:hi, (HEADS - 1) * D:HD]
                                o = ps[(h * NG + k) % 2][:, 0:(hi - lo) * D].rearrange("p (r f) -> p r f", f=D)
                                e.tensor_tensor(mixed[:, 0:hi - lo, :], o, g4, ALU.add).then_inc(s_free, 1)
                                e.wait_ge(s_free, G + NG + 1)
                                for r in range(lo, hi):
                                    step(r, mixed[:, r - lo, :])

                            e.wait_ge(s_idx, hh + 1)
                            e.wait_ge(s_st[h], i * 16 + 16)
                            if wide:
                                scale(0)
                                for k in range(1, NG):
                                    scale(k)
                                    steps(k - 1)
                                steps(NG - 1)
                            else:
                                e.wait_ge(s_rows[h], (i + 1) * 16 * HALF)
                                for r in range(HALF):
                                    step(r, gbuf[h][:, r, :])
                            e.wait_ge(s_step, (hh + 1) * HALF + 1)
                            e.sem_inc(s_run, 1)

                if wide:
                    @block.tensor
                    def _(e):
                        with e.Fori(0, LP) as i:
                            for h in range(2):
                                for k, (lo, hi) in enumerate(GROUPS):
                                    G = (i * 2 + h) * NG + k
                                    e.wait_ge(s_mul, G + 1)
                                    e.wait_ge(s_free, G + NG - 1)
                                    g4 = gbuf[0][:, lo:hi, :].rearrange("p r (a f) -> p r a f", f=D)
                                    for a in range(HEADS - 1):
                                        last = e.matmul(ps[(h * NG + k) % 2][:, 0:(hi - lo) * D], ident[:, :],
                                                        g4[:, :, a, :], start=(a == 0), stop=(a == HEADS - 2))
                                    last.then_inc(s_mix, 1)

                @block.sync
                def _(e):
                    for h in range(2):
                        e.dma_start(per_edge(run_d)[:, h:h + 1, :], hs[:, 0:1, :]).then_inc(s_st[h], 16)
                    for h in range(2):
                        e.wait_ge(s_st[h], 16)
                    with e.Fori(0, LP) as i:
                        for h in range(2):
                            hh = i * 2 + h
                            e.wait_ge(s_run, hh + 3)
                            e.dma_start(per_edge(run_d)[:, bass.ds(hh * HALF, HALF), :], run[h][:, :, :])\
                             .then_inc(s_st[h], 16)
                    for h in range(2):
                        e.wait_ge(s_st[h], 16 * (LP + 1))

        def collect(ch, res, table, tail, w):
            ch.add("gpsimd", lambda e, i: [
                e.indirect_dma_start(res[:, j, :], None, table,
                                     bass.IndirectOffsetOnAxis(ap=last_i[:, j:j + 1], axis=0)) for j in range(J)],
                   "sw", J)
            ch.add("vector", lambda e, i: e.tensor_tensor(res[:, :, :], res[:, :, :],
                                                          bc(nonempty[:, :].unsqueeze(2), [P, J, w]), ALU.mult))
            per = 512 // w

            def carry(e, i):
                for j in range(J):
                    last = e.matmul(ps[j // per][:, (j % per) * w:(j % per + 1) * w], link[:, j, :], tail,
                                    start=True, stop=True)
                return last
            ch.add("tensor", carry)

            def fold(e, i):
                for b in range(-(-J // per)):
                    n = min(per, J - b * per)
                    last = e.tensor_tensor(res[:, b * per:b * per + n, :], res[:, b * per:b * per + n, :],
                                           ps[b][:, 0:n * w].rearrange("p (j f) -> p j f", f=w), ALU.add)
                return last
            ch.add("vector", fold)

        with ExitStack() as ctx:
            g = [sb(f"rows_l1_{h}", [P, HALF, D], f32, ctx) for h in range(2)]
            edge_pass("l1", h1_d, src_i, g)

        asn = sb("att_src_node", [P, J, HEADS])
        adn = sb("att_dst_node", [P, J, HEADS])
        with ExitStack() as ctx:
            neigh = sb("neigh", [P, J, D], f32, ctx)
            pair = sb("pair", [P, JB, 2 * D], f32, ctx)
            pt = sb("pair_t", [P, JB * P], f32, ctx)
            w1_s = sb("w1", [P, D], f32, ctx)
            b1_s = sb("b1", [P, D], f32, ctx)
            tmp7 = sb("tmp7", [P, JB, D], f32, ctx)
            ch = chain("nodes1")
            ch.add("sync", lambda e, i: [e.dma_start(w1_s[:, :], w1),
                                         e.dma_start(b1_s[:, :], b1.partition_broadcast(P))], "hw", 2)
            collect(ch, neigh, run_d, run[1][:, HALF - 1, :], D)
            ch.add(V, lambda e, i: e.tensor_tensor(neigh[:, :, :], neigh[:, :, :],
                                                   bc(rdeg[:, :].unsqueeze(2), [P, J, D]), ALU.mult))
            lp = chain("dense1", J // JB)

            def join(e, i):
                e.tensor_copy(pair[:, :, 0:D], hs[:, bass.ds(i * JB, JB), :])
                return e.tensor_copy(pair[:, :, D:2 * D], neigh[:, bass.ds(i * JB, JB), :])
            lp.add(V, join)
            lp.add("tensor", transposes(pair, 2 * D))
            lp.add("scalar", untranspose(pt, 2 * D))

            def dense1(e, i):
                for j in range(JB):
                    last = e.matmul(ps[2][:, j * D:(j + 1) * D], pt[:, j * P:(j + 1) * P], w1_s[:, :],
                                    start=True, stop=True)
                return last
            lp.add("tensor", dense1)
            lp.add(V, lambda e, i: e.tensor_tensor(tmp7[:, :, :], tiles(2), bc(b1_s[:, :].unsqueeze(1), [P, JB, D]),
                                                   ALU.add))
            lp.add(V, lambda e, i: e.scalar_tensor_tensor(xs[:, bass.ds(i * JB, JB), :], tmp7[:, :, :], 0.0,
                                                          xs[:, bass.ds(i * JB, JB), :], ALU.max, ALU.add))
            ch2 = chain("norm2")
            normalise(ch2, hs, xs, neigh)
            stage(ch, lp, ch2)

        with ExitStack() as ctx:
            watt_s = sb("watt", [D, HD], f32, ctx)
            attb = sb("att_rows", [D, 2, HD], f32, ctx)
            wlog = sb("logit_weights", [D, 2 * HEADS], f32, ctx)
            step7 = sb("h_step", [P, JB, D], f32, ctx)
            t7 = sb("h_step_t", [D, JB * P], f32, ctx)
            feat = sb("att_features", [P, JB, HD], f32, ctx)
            ch = chain("att_weights")
            ch.add("sync", lambda e, i: [e.dma_start(watt_s[:, :], watt),
                                         e.dma_start(attb[:, 0, :], att_s.rearrange("a f -> (a f)").partition_broadcast(D)),
                                         e.dma_start(attb[:, 1, :], att_d.rearrange("a f -> (a f)").partition_broadcast(D))],
                   "hw", 3)
            for k in range(2):
                ch.add(V, lambda e, i, k=k: e.tensor_tensor(attb[:, k, :], attb[:, k, :], watt_s[:, :], ALU.mult))
                ch.add(V, lambda e, i, k=k: e.tensor_reduce(wlog[:, k * HEADS:(k + 1) * HEADS],
                                                            attb[:, k, :].rearrange("p (a f) -> p a f", f=D), X,
                                                            ALU.add))
            lp = chain("att_features", J // JB)
            lp.add(V, lambda e, i: e.tensor_copy(step7[:, :, :], hs[:, bass.ds(i * JB, JB), :]))
            lp.add("tensor", transposes(step7, D))
            lp.add("scalar", untranspose(t7, D))

            def project(e, i):
                for j in range(JB):
                    last = e.matmul(ps[j][:, :], t7[:, j * P:(j + 1) * P], watt_s[:, :], start=True, stop=True)
                for j in range(JB):
                    last = e.matmul(ps[7][:, j * 16:(j + 1) * 16], t7[:, j * P:(j + 1) * P], wlog[:, :],
                                    start=True, stop=True)
                return last
            lp.add("tensor", project)

            def evac(e, i):
                for j in range(JB):
                    last = e.copy(feat[:, j, :], ps[j][:, :])
                return last
            lp.add("scalar", evac)
            lp.add("sync", lambda e, i: e.dma_start(per_node(hw_d)[:, bass.ds(i * JB, JB), :], feat[:, :, :]), "hw")

            def logits(e, i):
                t = ps[7][:, 0:JB * 16].rearrange("p (j f) -> p j f", f=16)
                e.tensor_copy(asn[:, bass.ds(i * JB, JB), :], t[:, :, 0:HEADS])
                return e.tensor_copy(adn[:, bass.ds(i * JB, JB), :], t[:, :, HEADS:16])
            lp.add(V, logits)
            ch2 = chain("att_tables")
            ch2.add("sync", lambda e, i: e.dma_start(per_node(as_d), asn[:, :, :]), "hw")
            stage(ch, lp, ch2)

        att = ExitStack()
        alpha = sb("alpha", [P, T, HEADS], f32, att)
        selfw = sb("self_weight", [P, J, HEADS], f32, att)
        with ExitStack() as ctx:
            rows8 = [sb(f"logit_rows{h}", [P, HALF, HEADS], f32, ctx) for h in range(2)]
            s_g = [sem(f"l2a_rows{h}") for h in range(2)]
            s_idx, s_use, s_pace = sem("l2a_staged"), sem("l2a_used"), sem("l2a_pace")
            LP = T // (2 * HALF)
            with nc.Block() as block:
                @block.scalar
                def _(e):
                    with e.Fori(0, LP) as i:
                        for h in range(2):
                            hh = i * 2 + h
                            e.wait_ge(s_use, hh + 1)
                            e.copy(idx[h][:, :], src_i[:, bass.ds(hh * HALF, HALF)]).then_inc(s_idx, 1)

                @block.gpsimd
                def _(e):
                    with e.Fori(0, LP) as i:
                        for h in range(2):
                            hh = i * 2 + h
                            e.wait_ge(s_idx, hh + 1)
                            e.sem_inc(s_pace, 1)
                            for r in range(HALF):
                                e.indirect_dma_start(rows8[h][:, r, :], None, as_d,
                                                     bass.IndirectOffsetOnAxis(ap=idx[h][:, r:r + 1], axis=0))\
                                 .then_inc(s_g[h], 16)

                @block.vector
                def _(e):
                    e.sem_inc(s_use, 2)
                    with e.Fori(0, LP) as i:
                        for h in range(2):
                            e.wait_ge(s_g[h], (i + 1) * 16 * HALF)
                            e.tensor_copy(alpha[:, bass.ds((i * 2 + h) * HALF, HALF), :], rows8[h][:, :, :])\
                             .then_inc(s_use, 1)

        with ExitStack() as ctx:
            reset = sb("reset", [P, T], f32, ctx)
            rc = [sb(f"running{k}", [P, TC, HEADS], f32, ctx) for k in range(2)]
            tab = sb("spread_rows", [P, TC, 2 * HEADS], f32, ctx)
            tabl = sb("spread_last", [P, 2 * HEADS], f32, ctx)
            endm = sb("end_max", [P, HEADS], f32, ctx)
            carm = sb("carry_max", [P, HEADS], f32, ctx)
            cmask = sb("carry_mask", [P, P], f32, ctx)
            cm1 = sb("carry_m1", [P, P], f32, ctx)
            fird = sb("first_dst_f", [P, 1], f32, ctx)
            am = sb("att_and_max", [P, J, 2 * HEADS], f32, ctx)
            mx = sb("node_max", [P, J, HEADS], f32, ctx)
            t8 = sb("node_tmp", [P, J, HEADS], f32, ctx)
            ms = sb("mask_stat", [P, J], f32, ctx)
            sx = chain("softmax")

            def chunk(k):
                return slice(k * TC, (k + 1) * TC)

            def scans(data0, data1, outp, init, op0, op1, heads=HEADS, shift=0):
                def fn(e, i):
                    for a in range(heads):
                        last = e.tensor_tensor_scan(outp(a), data0, data1(a), init(a), op0, op1)
                    return last
                return fn
            sx.add(V, lambda e, i: e.tensor_scalar(reset[:, :], same[:, :], 1.0, BIG, ALU.subtract, ALU.mult))
            for rnd in range(2):
                for k in range(NCH):
                    o, b = rc[k % 2], rc[(k + 1) % 2]
                    init = (lambda a, b=b: b[:, TC - 1, a:a + 1]) if k else (
                        (lambda a: carm[:, a:a + 1]) if rnd else (lambda a: -BIG))
                    sx.add(V, scans(reset[:, chunk(k)], lambda a, k=k: alpha[:, chunk(k), a],
                                    lambda a, o=o: o[:, :, a], init, ALU.add, ALU.max))
                    if rnd:
                        sx.add("sync", lambda e, i, k=k, o=o: e.dma_start(per_edge(run8_d)[:, chunk(k), :], o[:, :, :]),
                               "hw")
                if rnd == 0:
                    sx.add(V, lambda e, i: e.tensor_copy(endm[:, :], rc[(NCH - 1) % 2][:, TC - 1, :]))
                    sx.add(V, lambda e, i: e.tensor_copy(fird[:, :], first_i[:, :]))
                    sx.add("tensor", lambda e, i: e.transpose(ps[0][:, 0:P], bc(last_f[:, 0:1], [P, P]), ident[:, :]))
                    sx.add(V, lambda e, i: e.tensor_scalar(cmask[:, :], ps[0][:, 0:P], fird[:, 0:1], None,
                                                           ALU.is_equal))
                    sx.add("gpsimd", lambda e, i: e.affine_select(out=cmask[:, :], in_=cmask[:, :],
                                                                  compare_op=ALU.is_gt, fill=0.0, base=0,
                                                                  pattern=[[-1, P]], channel_multiplier=1))
                    sx.add(V, lambda e, i: e.tensor_scalar(cm1[:, :], cmask[:, :], 1.0, BIG, ALU.subtract, ALU.mult))

                    def spread_ends(e, i):
                        for a in range(HEADS):
                            last = e.transpose(ps[1 + a // 4][:, (a % 4) * P:(a % 4 + 1) * P],
                                               bc(endm[:, a:a + 1], [P, P]), ident[:, :])
                        return last
                    sx.add("tensor", spread_ends)
                    for a in range(HEADS):
                        sx.add(V, lambda e, i, a=a: e.tensor_tensor(
                            cmask[:, :], ps[1 + a // 4][:, (a % 4) * P:(a % 4 + 1) * P], cm1[:, :], ALU.add))
                        sx.add(V, lambda e, i, a=a: e.tensor_reduce(carm[:, a:a + 1], cmask[:, :], X, ALU.max))
            sx.add("gpsimd", lambda e, i: [
                e.indirect_dma_start(mx[:, j, :], None, run8_d,
                                     bass.IndirectOffsetOnAxis(ap=last_i[:, j:j + 1], axis=0)) for j in range(J)],
                   "sw", J)
            ne8 = bc(nonempty[:, :].unsqueeze(2), [P, J, HEADS])
            sx.add(V, lambda e, i: e.tensor_tensor(mx[:, :, :], mx[:, :, :], ne8, ALU.mult))
            sx.add(V, lambda e, i: e.tensor_scalar(ms[:, :], nonempty[:, :], 1.0, BIG, ALU.subtract, ALU.mult))
            sx.add(V, lambda e, i: e.tensor_tensor(mx[:, :, :], mx[:, :, :],
                                                   bc(ms[:, :].unsqueeze(2), [P, J, HEADS]), ALU.add))
            sx.add(V, lambda e, i: e.tensor_tensor(mx[:, :, :], mx[:, :, :], asn[:, :, :], ALU.max))
            sx.add(V, lambda e, i: e.tensor_tensor(mx[:, :, :], mx[:, :, :], adn[:, :, :], ALU.add))

            def leaky(t, u):
                return lambda e, i: e.scalar_tensor_tensor(t, u, 0.2, u, ALU.mult, ALU.max)
            sx.add(V, leaky(am[:, :, HEADS:16], mx[:, :, :]))
            sx.add(V, lambda e, i: e.tensor_copy(am[:, :, 0:HEADS], adn[:, :, :]))
            sx.add(V, lambda e, i: e.tensor_tensor(t8[:, :, :], asn[:, :, :], adn[:, :, :], ALU.add))
            sx.add(V, leaky(selfw[:, :, :], t8[:, :, :]))
            sx.add(V, lambda e, i: e.tensor_tensor(selfw[:, :, :], selfw[:, :, :], am[:, :, HEADS:16], ALU.subtract))
            sx.add("scalar", lambda e, i: e.activation(selfw[:, :, :], selfw[:, :, :], ACT.Exp))

            def spread(values):
                return lambda e, i: [
                    e.indirect_dma_start(spread_d, bass.IndirectOffsetOnAxis(ap=start_i[:, j:j + 1], axis=0),
                                         values[:, j, :], None) for j in range(J)]
            sx.add("gpsimd", spread(am), "sw", J)
            sx.add("sync", lambda e, i: e.dma_start(per_node(am_d), am[:, :, :]), "hw")
            get_first = lambda e, i: [e.indirect_dma_start(tabl[:, :], None, am_d,
                                                           bass.IndirectOffsetOnAxis(ap=first_i[:, 0:1], axis=0))]
            sx.add("gpsimd", get_first, "sw", 1)
            for k in range(NCH):
                o, b = rc[k % 2], rc[(k + 1) % 2]
                sx.add("sync", lambda e, i, k=k: e.dma_start(tab[:, :, :], per_edge(spread_d)[:, chunk(k), :]), "hw")
                sx.add(V, scans(same[:, chunk(k)], lambda a: tab[:, :, a], lambda a: tab[:, :, a],
                                lambda a: tabl[:, a:a + 1], ALU.mult, ALU.add, 2 * HEADS))
                sx.add(V, lambda e, i: e.tensor_copy(tabl[:, :], tab[:, TC - 1, :]))
                al = alpha[:, chunk(k), :]
                sx.add(V, lambda e, i, al=al: e.tensor_tensor(al, al, tab[:, :, 0:HEADS], ALU.add))
                sx.add(V, leaky(al, al))
                sx.add(V, lambda e, i, al=al: e.tensor_tensor(al, al, tab[:, :, HEADS:16], ALU.subtract))
                sx.add("scalar", lambda e, i, al=al: e.activation(al, al, ACT.Exp))
                init = (lambda a, b=b: b[:, TC - 1, a:a + 1]) if k else (lambda a: 0.0)
                sx.add(V, scans(same[:, chunk(k)], lambda a, k=k: alpha[:, chunk(k), a], lambda a, o=o: o[:, :, a],
                                init, ALU.mult, ALU.add))
                sx.add("sync", lambda e, i, k=k, o=o: e.dma_start(per_edge(run8_d)[:, chunk(k), :], o[:, :, :]), "hw")
            collect(sx, mx, run8_d, rc[(NCH - 1) % 2][:, TC - 1, :], HEADS)
            sx.add(V, lambda e, i: e.tensor_tensor(mx[:, :, :], mx[:, :, :], selfw[:, :, :], ALU.add))
            sx.add(V, lambda e, i: e.tensor_scalar(mx[:, :, :], mx[:, :, :], 1e-16, None, ALU.add))
            sx.add(V, lambda e, i: e.reciprocal(mx[:, :, :], mx[:, :, :]))
            sx.add(V, lambda e, i: e.tensor_scalar(am[:, :, 0:HEADS], mx[:, :, :], 1.0 / HEADS, None, ALU.mult))
            sx.add(V, lambda e, i: e.tensor_tensor(selfw[:, :, :], selfw[:, :, :], am[:, :, 0:HEADS], ALU.mult))
            sx.add("gpsimd", spread(am), "sw", J)
            sx.add("sync", lambda e, i: e.dma_start(per_node(am_d), am[:, :, :]), "hw")
            sx.add("gpsimd", get_first, "sw", 1)
            for k in range(NCH):
                sx.add("sync", lambda e, i, k=k: e.dma_start(tab[:, :, :], per_edge(spread_d)[:, chunk(k), :]), "hw")
                sx.add(V, scans(same[:, chunk(k)], lambda a: tab[:, :, a], lambda a: tab[:, :, a],
                                lambda a: tabl[:, a:a + 1], ALU.mult, ALU.add))
                sx.add(V, lambda e, i: e.tensor_copy(tabl[:, 0:HEADS], tab[:, TC - 1, 0:HEADS]))
                al = alpha[:, chunk(k), :]
                sx.add(V, lambda e, i, al=al: e.tensor_tensor(al, al, tab[:, :, 0:HEADS], ALU.mult))
            stage(sx)

        with ExitStack() as ctx:
            g = [sb("rows_l2", [P, HALF, HD], f32, ctx)]
            edge_pass("l2", hw_d, src_i, g, alpha)

        with ExitStack() as ctx:
            res = sb("att_out", [P, J, D], f32, ctx)
            x1 = sb("x1", [P, J, D], f32, ctx)
            vecs = {n: sb(f"row_{n}", [P, D], f32, ctx) for n in ("batt", "g1", "be1", "g2", "be2", "bf2")}
            wf1_s = sb("wf1", [D, 2 * D], f32, ctx)
            bf1_s = sb("bf1", [P, 1], f32, ctx)
            wf2_s = sb("wf2", [2 * D, D], f32, ctx)
            feat = sb("self_features", [P, JB, HD], f32, ctx)
            sw7 = sb("self_weight_step", [P, JB, HEADS], f32, ctx)
            self7 = sb("self_message", [P, JB, D], f32, ctx)
            step7 = sb("x1_step", [P, JB, D], f32, ctx)
            t7 = sb("x1_step_t", [D, JB * P], f32, ctx)
            hid = sb("hidden2_t", [P, JB * P], f32, ctx)
            ch = chain("nodes2")
            rowsrc = {"batt": batt, "g1": g1, "be1": be1, "g2": g2, "be2": be2, "bf2": bf2}
            ch.add("sync", lambda e, i: [e.dma_start(vecs[n][:, :], rowsrc[n].partition_broadcast(P)) for n in vecs] +
                   [e.dma_start(wf1_s[:, :], wf1), e.dma_start(bf1_s[:, :], bf1), e.dma_start(wf2_s[:, :], wf2)],
                   "hw", 9)
            collect(ch, res, run_d, run[1][:, HALF - 1, :], D)
            lp = chain("self_edges", J // JB)
            lp.add(V, lambda e, i: e.tensor_copy(sw7[:, :, :], selfw[:, bass.ds(i * JB, JB), :]))
            lp.add("sync", lambda e, i: e.dma_start(feat[:, :, :], per_node(hw_d)[:, bass.ds(i * JB, JB), :]), "hw")
            lp.add(V, lambda e, i: e.tensor_tensor(
                feat[:, :, :].rearrange("p j (a f) -> p (j a) f", f=D),
                feat[:, :, :].rearrange("p j (a f) -> p (j a) f", f=D),
                bc(sw7[:, :, :].rearrange("p j a -> p (j a)").unsqueeze(2), [P, JB * HEADS, D]), ALU.mult))
            lp.add(V, lambda e, i: e.tensor_reduce(self7[:, :, :],
                                                   feat[:, :, :].rearrange("p j (a f) -> p j f a", f=D), X, ALU.add))
            lp.add(V, lambda e, i: e.tensor_tensor(res[:, bass.ds(i * JB, JB), :], res[:, bass.ds(i * JB, JB), :],
                                                   self7[:, :, :], ALU.add))
            full = [P, J, D]
            ch2 = chain("norm_att")
            ch2.add(V, lambda e, i: e.tensor_tensor(res[:, :, :], res[:, :, :], hs[:, :, :], ALU.add))
            ch2.add(V, lambda e, i: e.tensor_tensor(res[:, :, :], res[:, :, :],
                                                    bc(vecs["batt"][:, :].unsqueeze(1), full), ALU.add))
            normalise(ch2, x1, res, hs, relu=False, gain=vecs["g1"], shift=vecs["be1"])
            lp2 = chain("ffn", J // JB)
            lp2.add(V, lambda e, i: e.tensor_copy(step7[:, :, :], x1[:, bass.ds(i * JB, JB), :]))
            lp2.add("tensor", transposes(step7, D))
            lp2.add("scalar", untranspose(t7, D))

            def up2(e, i):
                e.matmul(ps[2][:, :], wf1_s[:, :], t7[:, 0:512], start=True, stop=True)
                return e.matmul(ps[3][:, 0:JB * P - 512], wf1_s[:, :], t7[:, 512:JB * P], start=True, stop=True)
            lp2.add("tensor", up2)

            def relu2(e, i):
                e.activation(hid[:, 0:512], ps[2][:, :], ACT.Relu, bias=bf1_s[:, 0:1])
                return e.activation(hid[:, 512:JB * P], ps[3][:, 0:JB * P - 512], ACT.Relu, bias=bf1_s[:, 0:1])
            lp2.add("scalar", relu2)

            def down2(e, i):
                for j in range(JB):
                    last = e.matmul(ps[4][:, j * D:(j + 1) * D], hid[:, j * P:(j + 1) * P], wf2_s[:, :],
                                    start=True, stop=True)
                return last
            lp2.add("tensor", down2)
            lp2.add(V, lambda e, i: e.tensor_tensor(res[:, bass.ds(i * JB, JB), :], x1[:, bass.ds(i * JB, JB), :],
                                                    tiles(4), ALU.add))
            ch3 = chain("norm_ffn")
            ch3.add(V, lambda e, i: e.tensor_tensor(res[:, :, :], res[:, :, :],
                                                    bc(vecs["bf2"][:, :].unsqueeze(1), full), ALU.add))
            normalise(ch3, x1, res, hs, relu=False, gain=vecs["g2"], shift=vecs["be2"])
            ch3.add(V, lambda e, i: e.tensor_tensor(xs[:, :, :], xs[:, :, :], x1[:, :, :], ALU.add))
            normalise(ch3, hs, xs, res)
            stage(ch, lp, ch2, lp2, ch3)
        att.close()

        own = sb("own", [P, J, D])
        idx3 = sb("relation_index", [P, T], i32)
        with ExitStack() as ctx:
            typ = sb("edge_type", [P, T], i32, ctx)
            tf = sb("edge_type_f", [P, T], f32, ctx)
            w3_s = sb("w3", [D, 4 * D], f32, ctx)
            b3_s = sb("b3", [P, D], f32, ctx)
            step7 = sb("h3_step", [P, JB, D], f32, ctx)
            t7 = sb("h3_step_t", [D, JB * P], f32, ctx)
            rel = sb("relations", [P, 3, JB, D], f32, ctx)
            ch = chain("index3")
            ch.add(V, lambda e, i: e.memset(typ[:, :], 0))
            ch.add("sync", lambda e, i: load_runs(e, typ, edge_type) + [
                e.dma_start(w3_s[:, :], w3), e.dma_start(b3_s[:, :], b3.partition_broadcast(P))], "hw",
                   len(rows_of(P - 1)) + 3)
            ch.add(V, lambda e, i: e.tensor_scalar(tf[:, :], typ[:, :], float(NP), None, ALU.mult))
            ch.add(V, lambda e, i: e.tensor_tensor(idx3[:, :], tf[:, :], src_i[:, :], ALU.add))
            lp = chain("relations", J // JB)
            lp.add(V, lambda e, i: e.tensor_copy(step7[:, :, :], hs[:, bass.ds(i * JB, JB), :]))
            lp.add("tensor", transposes(step7, D))
            lp.add("scalar", untranspose(t7, D))

            def relate(e, i):
                for j in range(JB):
                    last = e.matmul(ps[2 + j // 2][:, (j % 2) * 256:(j % 2 + 1) * 256], t7[:, j * P:(j + 1) * P],
                                    w3_s[:, :], start=True, stop=True)
                return last
            lp.add("tensor", relate)

            def evac3(e, i):
                for j in range(JB):
                    o = ps[2 + j // 2][:, (j % 2) * 256:(j % 2) * 256 + 192].rearrange("p (r f) -> p r f", f=D)
                    last = e.copy(rel[:, :, j, :], o)
                return last
            lp.add("scalar", evac3)
            lp.add("sync", lambda e, i: [
                e.dma_start(per_node(y3_d[r * NP:(r + 1) * NP, :])[:, bass.ds(i * JB, JB), :], rel[:, r, :, :])
                for r in range(3)], "hw", 3)

            def keep(e, i):
                for b in range(4):
                    n = min(2, JB - 2 * b)
                    v = ps[2 + b][:, 0:n * 256].rearrange("p (j f) -> p j f", f=256)[:, :, 192:256]
                    last = e.tensor_tensor(own[:, bass.ds(i * JB + 2 * b, n), :], v,
                                           bc(b3_s[:, :].unsqueeze(1), [P, n, D]), ALU.add)
                return last
            lp.add(V, keep)
            stage(ch, lp)

        with ExitStack() as ctx:
            g = [sb(f"rows_l3_{h}", [P, HALF, D], f32, ctx) for h in range(2)]
            edge_pass("l3", y3_d, idx3, g)

        with ExitStack() as ctx:
            res = sb("rel_sum", [P, J, D], f32, ctx)
            ch = chain("nodes3")
            collect(ch, res, run_d, run[1][:, HALF - 1, :], D)
            ch.add(V, lambda e, i: e.tensor_tensor(res[:, :, :], res[:, :, :], own[:, :, :], ALU.add))
            ch.add(V, lambda e, i: e.scalar_tensor_tensor(res[:, :, :], res[:, :, :], 0.0, xs[:, :, :], ALU.max,
                                                          ALU.add))
            ch.add("sync", lambda e, i: node_rows(e, res, out, back=True), "hw", len(rows_of(PN)) + 1)
            stage(ch)


def kernel(**inputs):
    import numpy as _np
    import concourse.bacc as _bacc
    from concourse.bass_utils import run_bass_kernel_spmd as _run

    nc = _bacc.Bacc("TRN2", target_bir_lowering=False, num_devices=1)
    g = {k: _np.asarray(v) for k, v in inputs.items()}
    w_rel = g["L3_gnn_W_rel"]
    given = {
        "x": g["x"], "src": g["src"], "dst": g["dst"], "edge_attr": g["edge_attr_48"], "edge_type": g["edge_type_3"],
        "w0a": g["L0_gnn_W1"], "b0a": g["L0_gnn_b1"].reshape(2, 128).T, "w0b": g["L0_gnn_W2"], "b0b": g["L0_gnn_b2"],
        "w1": g["L1_gnn_W"], "b1": g["L1_gnn_b"],
        "watt": g["L2_gnn_W_att"], "att_s": g["L2_gnn_att_src"], "att_d": g["L2_gnn_att_dst"],
        "batt": g["L2_gnn_bias_att"], "wf1": g["L2_gnn_W1"], "bf1": g["L2_gnn_b1"].reshape(128, 1),
        "wf2": g["L2_gnn_W2"], "bf2": g["L2_gnn_b2"], "g1": g["L2_gnn_ln1_g"], "be1": g["L2_gnn_ln1_b"],
        "g2": g["L2_gnn_ln2_g"], "be2": g["L2_gnn_ln2_b"],
        "w3": _np.concatenate([w_rel[0].T, w_rel[1].T, w_rel[2].T, g["L3_gnn_W_self"].T], axis=1),
        "b3": g["L3_gnn_b_self"],
    }
    arrays, args = {}, []
    for name, a in given.items():
        a = _np.ascontiguousarray(a)
        arrays[f"in_{name}"] = a
        args.append(nc.dram_tensor(f"in_{name}", a.shape, mybir.dt.from_np(a.dtype), kind="ExternalInput").ap())
    args.append(nc.dram_tensor("out", g["x"].shape, f32, kind="ExternalOutput").ap())
    build(nc, *args)
    r = _run(nc, [arrays], core_ids=[0])
    return r.results[0]["out"]
```

```python
import concourse.bass as bass
from concourse import mybir
from contextlib import ExitStack

f32, i32, bf16 = mybir.dt.float32, mybir.dt.int32, mybir.dt.bfloat16
ALU = mybir.AluOpType
ACT = mybir.ActivationFunctionType
X = mybir.AxisListType.X
P = 128
D = 64
FE = 48
HEADS = 8
HD = HEADS * D
HALF = 26
NACC = 4
JB = 7
OWN = 3
NCH = 4
BIG = 1e30
LN_EPS = 1e-5


def rows_of(n):
    a = n // 16 * 16
    return [(0, a), (a, n)] if a < n else [(0, n)]


class Chain:
    KINDS = ("c", "hw", "sw") + tuple(f"side{n}{t}" for n in range(4) for t in ("", "hw"))
    UNIT = {k: 1 if k == "c" or k[-1].isdigit() else 16 for k in KINDS}

    def __init__(self, nc, ctx, name, loops=0):
        self.nc, self.ctx, self.name = nc, ctx, name
        self.loops, self.steps, self.prev = loops, [], None

    def prepare(self):
        used = {s[2] for s in self.steps} | ({"c", "pace"} if self.loops else set())
        self.sem = {k: self.ctx.enter_context(self.nc.semaphore(f"{self.name}_{k}")) for k in sorted(used)}

    def total(self):
        return {k: sum(self.UNIT[k] * n for _, _, kind, n, _ in self.steps if kind == k) for k in self.KINDS}

    def end(self):
        kind = self.steps[-1][2]
        n = self.total()[kind]
        return self.sem[kind], n * self.loops + 1 if self.loops else n

    def add(self, engine, fn, kind="c", n=1, join=False):
        self.steps.append((engine, fn, kind, n, join))

    def beside(self, engine, fn, dma=0, lane=0, join=False):
        assert not self.loops
        self.steps.append((engine, fn, f"side{lane}hw" if dma else f"side{lane}", dma or 1, join))

    def run(self, engine, eng):
        run_lanes([self], engine, eng)

    def emit(self, engine, eng, i):
        total, count = self.total(), dict.fromkeys(self.KINDS, 0)
        count["c"] = 1 if self.loops else 0
        before = "c"
        for n_step, (e, fn, kind, n, join) in enumerate(self.steps):
            if e == engine:
                if count[before]:
                    eng.wait_ge(self.sem[before], i * total[before] + count[before])
                elif n_step and self.prev:
                    for c in self.prev:
                        eng.wait_ge(*c.end())
                if self.loops and engine == "tensor":
                    eng.sem_inc(self.sem["pace"], 1)
                lanes = range(4) if join is True else join or (kind[4:5] if kind.startswith("side") else ())
                for k in self.KINDS[3:]:
                    if count[k] and int(k[4]) in [int(n) for n in lanes]:
                        eng.wait_ge(self.sem[k], count[k])
                done = fn(eng, i)
                if done is None:
                    eng.sem_inc(self.sem[kind], n)
                else:
                    for d in done if isinstance(done, list) else [done]:
                        d.then_inc(self.sem[kind], self.UNIT[kind])
            count[kind] += self.UNIT[kind] * n
            if not kind.startswith("side"):
                before = kind
            yield


def run_lanes(chains, engine, eng):
    first = chains[0]
    if not any(s[0] == engine for s in first.steps):
        return
    starts = first.steps[0][0] == engine
    if starts and first.prev:
        for c in first.prev:
            eng.wait_ge(*c.end())
    if first.loops:
        if starts:
            for c in chains:
                eng.sem_inc(c.sem["c"], 1)
        with eng.Fori(0, first.loops) as i:
            for _ in zip(*(c.emit(engine, eng, i) for c in chains)):
                pass
    else:
        for _ in zip(*(c.emit(engine, eng, 0) for c in chains)):
            pass
        if first.steps[-1][0] == engine and first.steps[-1][2] != "c":
            eng.wait_ge(*first.end())


def build(nc, x, src, dst, edge_attr, edge_type, w0a, b0a, w0b, b0b, w1, b1, watt, att_s, att_d, batt, wf1, bf1, wf2,
          bf2, g1, be1, g2, be2, w3, b3, out):
    N, E = x.shape[0], src.shape[0]
    T = -(-E // (P * 2 * HALF)) * 2 * HALF
    EP = P * T
    J = -(-(N + 1) // (P * JB)) * JB
    NP = P * J
    HI = NP // P
    TF = E // P
    REST = E - TF * P
    TC = T // NCH
    DUMP = NP
    TAILE = E - (P - 1) * T
    PN, TAILN = N // J, N - N // J * J
    assert TF == T - 1 and 0 < REST < P and 0 < TAILE <= T and HI <= P and PN == P - 1 and 0 < TAILN < J

    def dram(name, shape, dt=f32):
        return nc.dram_tensor(name, shape, dt).ap()

    acc_d = [dram(f"acc{k}", [NP + P, D]) for k in range(NACC)]
    h1_d = dram("h1_table", [NP, D])
    as_d = dram("att_src_table", [NP, HEADS])
    hw_d = dram("att_feature_table", [NP, HD])
    y3_d = dram("relation_table", [3 * NP, D])
    run_d = dram("running_sums", [EP, D])
    run8_d = dram("running_heads", [EP, HEADS])
    spread_d = dram("spread", [EP + NP, 2 * HEADS])
    spread8_d = dram("spread_heads", [EP + NP, HEADS])
    am_d = dram("node_att_max", [NP, 2 * HEADS])
    cnt_d = dram("degree", [NP])
    end_d = dram("segment_end", [NP])

    def per_node(t):
        return t.rearrange("(p j) f -> p j f", j=J)

    def per_edge(t):
        return t[0:EP, :].rearrange("(p t) f -> p t f", t=T)

    top = ExitStack()
    with top:
        def sb(name, shape, dt=f32, ctx=top):
            return ctx.enter_context(nc.sbuf_tensor(name, shape, dt))

        def sem(name):
            return top.enter_context(nc.semaphore(name))

        banks = top.enter_context(nc.psum_tensor("banks", [P, 8, 512], f32))
        ps = [banks[:, b, :] for b in range(8)]
        xs = sb("x_nodes", [P, J, D])
        hs = sb("h_nodes", [P, J, D])
        st = sb("node_stat", [P, J])
        st2 = sb("node_stat2", [P, J])
        src_i = sb("src_i", [P, T], i32)
        same = sb("same_dst", [P, T])
        ident = sb("ident", [P, P])
        iota = sb("iota_row", [P, P])
        part_no = sb("partition_number", [P, 1])
        link = sb("link", [P, J, P])
        last_i = sb("last_edge", [P, J], i32)
        start_i = sb("start_edge", [P, J], i32)
        first_i = sb("first_dst", [P, 1], i32)
        last_f = sb("last_dst_f", [P, 1])
        nonempty = sb("nonempty", [P, J])
        rdeg = sb("one_over_degree", [P, J])
        run = [sb(f"run{h}", [P, HALF, D]) for h in range(2)]
        idx = [sb(f"idx{h}", [P, HALF], i32) for h in range(2)]
        mask = [sb(f"mask{h}", [P, HALF]) for h in range(2)]

        def bc(ap, shape):
            return ap.to_broadcast(shape)

        def normalise(ch, dst_t, src_t, tmp, relu=True, gain=None, shift=None):
            full = [P, J, D]
            s3, q3 = st[:, :].unsqueeze(2), st2[:, :].unsqueeze(2)
            V = "vector"
            ch.add(V, lambda e, i: e.tensor_reduce(st[:, :], src_t[:, :, :], X, ALU.add))
            ch.add(V, lambda e, i: e.tensor_scalar(st[:, :], st[:, :], 1.0 / D, None, ALU.mult))
            ch.add(V, lambda e, i: e.tensor_tensor(dst_t[:, :, :], src_t[:, :, :], bc(s3, full), ALU.subtract))
            ch.add(V, lambda e, i: e.tensor_tensor(tmp[:, :, :], dst_t[:, :, :], dst_t[:, :, :], ALU.mult))
            ch.add(V, lambda e, i: e.tensor_reduce(st2[:, :], tmp[:, :, :], X, ALU.add))
            ch.add(V, lambda e, i: e.tensor_scalar(st2[:, :], st2[:, :], 1.0 / D, LN_EPS, ALU.mult, ALU.add))
            ch.add("scalar", lambda e, i: e.activation(st2[:, :], st2[:, :], ACT.Sqrt))
            ch.add(V, lambda e, i: e.reciprocal(st2[:, :], st2[:, :]))
            if relu:
                ch.add(V, lambda e, i: e.scalar_tensor_tensor(dst_t[:, :, :], dst_t[:, :, :], 0.0, bc(q3, full),
                                                              ALU.max, ALU.mult))
            else:
                ch.add(V, lambda e, i: e.tensor_tensor(dst_t[:, :, :], dst_t[:, :, :], bc(q3, full), ALU.mult))
            if gain is not None:
                ch.add(V, lambda e, i: e.tensor_tensor(dst_t[:, :, :], dst_t[:, :, :],
                                                       bc(gain[:, :].unsqueeze(1), full), ALU.mult))
                ch.add(V, lambda e, i: e.tensor_tensor(dst_t[:, :, :], dst_t[:, :, :],
                                                       bc(shift[:, :].unsqueeze(1), full), ALU.add))

        def stage(*parts):
            parts = [p if isinstance(p, tuple) else (p,) for p in parts]
            for a, b in zip([None] + parts, parts):
                for c in b:
                    c.prev = a
                    c.prepare()
            with nc.Block() as block:
                for name in ("sync", "gpsimd", "scalar", "vector", "tensor"):
                    def body(e, name=name):
                        for part in parts:
                            run_lanes(part, name, e)
                    getter = {"sync": block.sync, "gpsimd": block.gpsimd, "scalar": block.scalar,
                              "vector": block.vector, "tensor": block.tensor}[name]
                    getter(body)

        def two_lanes(name, make):
            out = []
            for k, (lo, n) in enumerate(((0, 4), (4, JB - 4))):
                ch = chain(f"{name}{k}", J // JB)
                make(ch, k, lo, n, ps[4 * k:4 * k + 4])
                out.append(ch)
            return tuple(out)

        def transposes(src_t, width, n, bank):
            def fn(e, i):
                for j in range(n):
                    last = e.transpose(bank[0:width, j * P:(j + 1) * P], src_t[:, j, 0:width], ident[:, :])
                return last
            return fn

        def tiles(bank, n, w=D):
            return bank[:, 0:n * w].rearrange("p (j f) -> p j f", f=w)

        def chain(name, loops=0):
            return Chain(nc, top, name, loops)

        l0 = ExitStack()
        src0 = sb("src0", [P, T + HALF], i32, l0)
        src0f = sb("src0f", [P, T + HALF], f32, l0)
        dlo = sb("dst_lo", [P, T], f32, l0)
        dhi = sb("dst_hi", [P, T], f32, l0)
        hist = sb("hist", [P, P], f32, l0)
        lower = sb("strict_lower", [P, P], f32, l0)
        upper = sb("strict_upper", [P, P], f32, l0)
        dumpn = sb("dump_n", [P, J], f32, l0)
        dumprow = sb("dump_row", [P, 1], f32, l0)
        zero = sb("zero", [P, 1024], f32, l0)
        c0 = ExitStack()
        dst_i = sb("dst_i", [P, T], i32, c0)
        dtmp = sb("dst_tmp", [P, T], i32, c0)
        edge_d = sb("edge_of_runs", [P, 3], i32, c0)
        edge_f = sb("edge_of_runs_f", [P, 3], f32, c0)
        prevf = sb("prev_f", [P, 1], f32, c0)
        linkf = sb("link_dst", [P, 1], f32, c0)

        def load_runs(e, tile, flat):
            body = flat[0:(P - 1) * T].rearrange("(p t) -> p t", t=T)
            d = [e.dma_start(tile[a:b, :], body[a:b, :]) for a, b in rows_of(P - 1)]
            return d + [e.dma_start(tile[P - 1:P, 0:TAILE], flat[(P - 1) * T:E].unsqueeze(0))]

        def node_rows(e, tile, flat, back=False):
            body = flat[0:PN * J, :].rearrange("(p j) f -> p j f", j=J)
            pairs = [(tile[a:b, :, :], body[a:b, :, :]) for a, b in rows_of(PN)]
            pairs.append((tile[PN:PN + 1, 0:TAILN, :], flat[PN * J:N, :].unsqueeze(0)))
            return [e.dma_start(b, a) if back else e.dma_start(a, b) for a, b in pairs]

        ch = chain("setup")

        def clear(e, i):
            e.memset(xs[:, :, :], 0.0)
            e.memset(src_i[:, :], 0)
            e.memset(dst_i[:, :], N)
            e.memset(src0[:, :], N)
            e.memset(zero[:, :], 0.0)
            e.memset(hist[:, :], 0.0)
            e.memset(lower[:, :], 1.0)
            e.memset(upper[:, :], 1.0)
            e.memset(run[1][:, :, :], 0.0)
            e.memset(edge_d[:, :], -1)
            return e.memset(ident[:, :], 0.0)
        ch.add("vector", clear)

        def zero_table(e, flat):
            w = flat.shape[1]
            return [e.dma_start(flat[:, c:min(c + 1024, w)], zero[:, 0:min(1024, w - c)]) for c in range(0, w, 1024)]

        def zero_accumulators(e, i):
            return sum((zero_table(e, acc_d[k].rearrange("(p a) f -> p (a f)", p=P)) for k in range(NACC)), [])
        ch.beside("scalar", zero_accumulators, NACC * -(-((NP + P) * D // P) // 1024))

        def loads(e, i):
            a = node_rows(e, xs, x) + load_runs(e, src_i, src) + load_runs(e, dst_i, dst)
            a.append(e.dma_start(src0[:, 0:TF], src[0:P * TF].rearrange("(p t) -> p t", t=TF)))
            col = src.unsqueeze(1)
            with nc.allow_non_contiguous_dma(reason="one column of indices"):
                a.append(e.dma_start(src0[0:REST, TF:T], col[P * TF:E, :]))
            return a
        n_loads = len(rows_of(PN)) + 1 + 2 * (len(rows_of(P - 1)) + 1) + 2
        ch.add("sync", loads, "hw", n_loads)

        def edges_in(e, i):
            return [e.dma_start(edge_d[:, 1:2], dst_i[:, T - 1:T]), e.dma_start(edge_d[0:P - 1, 2:3], dst_i[1:P, 0:1])]
        ch.add("sync", edges_in, "hw", 2)
        prev_d = sb("prev_d", [P, 1], i32, c0)
        ch.add("vector", lambda e, i: e.memset(prev_d[:, :], -1))
        ch.add("sync", lambda e, i: e.dma_start(prev_d[1:P, :], dst_i[0:P - 1, T - 1:T]), "hw")

        def constants(e, i):
            e.iota(iota[:, :], [[1, P]], base=0, channel_multiplier=0, allow_small_or_imprecise_dtypes=True)
            e.iota(part_no[:, :], [[0, 1]], base=0, channel_multiplier=1, allow_small_or_imprecise_dtypes=True)
            e.iota(dumpn[:, :], [[1, J]], base=EP, channel_multiplier=J, allow_small_or_imprecise_dtypes=True)
            e.iota(dumprow[:, :], [[0, 1]], base=DUMP, channel_multiplier=1, allow_small_or_imprecise_dtypes=True)
            e.iota(link[:, :, :], [[1, J], [J, P]], base=0, channel_multiplier=0, allow_small_or_imprecise_dtypes=True)
            e.affine_select(out=ident[:, :], in_=ident[:, :], compare_op=ALU.not_equal, fill=1.0, base=0,
                            pattern=[[-1, P]], channel_multiplier=1)
            e.affine_select(out=lower[:, :], in_=lower[:, :], compare_op=ALU.is_gt, fill=0.0, base=0,
                            pattern=[[-1, P]], channel_multiplier=1)
            return e.affine_select(out=upper[:, :], in_=upper[:, :], compare_op=ALU.is_gt, fill=0.0, base=0,
                                   pattern=[[1, P]], channel_multiplier=-1)
        ch.add("gpsimd", constants)
        V = "vector"

        def same_a(e, i):
            e.tensor_tensor(same[:, 1:T], dst_i[:, 1:T], dst_i[:, 0:T - 1], ALU.is_equal)
            e.tensor_tensor(same[:, 0:1], dst_i[:, 0:1], prev_d[:, :], ALU.is_equal)
            e.tensor_copy(edge_f[:, :], edge_d[:, :])
            e.tensor_copy(first_i[:, :], dst_i[:, 0:1])
            e.tensor_copy(last_f[:, :], dst_i[:, T - 1:T])
            e.tensor_copy(src0f[:, :], src0[:, :])
            return e.tensor_scalar(dtmp[:, :], dst_i[:, :], P - 1, None, ALU.bitwise_and)
        ch.add(V, same_a)
        ch.add(V, lambda e, i: e.tensor_copy(dlo[:, :], dtmp[:, :]))
        ch.add(V, lambda e, i: e.tensor_scalar(dtmp[:, :], dst_i[:, :], 7, None, ALU.logical_shift_right))
        ch.add(V, lambda e, i: e.tensor_copy(dhi[:, :], dtmp[:, :]))
        ch.add(V, lambda e, i: e.tensor_tensor(prevf[:, :], edge_f[:, 1:2], edge_f[:, 2:3], ALU.is_equal))
        ch.add(V, lambda e, i: e.scalar_tensor_tensor(linkf[:, :], edge_f[:, 1:2], 1.0, prevf[:, :], ALU.add,
                                                      ALU.mult))
        ch.add(V, lambda e, i: e.tensor_scalar(linkf[:, :], linkf[:, :], -1.0, None, ALU.add))
        ch.add(V, lambda e, i: e.tensor_scalar(link[:, :, :], link[:, :, :], linkf[:, 0:1], None, ALU.is_equal),
               join=True)
        stage(ch)
        c0.close()

        GROUPS = [(r, min(r + 4, HALF)) for r in range(0, HALF, 4)]
        NG = len(GROUPS)
        assert NG % 2

        nd = ExitStack()
        both = sb("both", [P, J, D + FE], f32, nd)
        part = sb("part", [P, J, D], f32, nd)
        cum = sb("cum", [P, P], f32, nd)
        before = sb("before", [P, 1], f32, nd)
        endf = sb("end_f", [P, J], f32, nd)
        degf = sb("deg_f", [P, J], f32, nd)
        tail0 = chain("nodes0_early")
        tail0.add(V, lambda e, i: e.memset(cum[:, :], 1.0))
        tail0.add(V, lambda e, i: e.tensor_tensor_scan(cum[0:HI, :], cum[0:HI, :], hist[0:HI, :], 0.0, ALU.mult,
                                                       ALU.add))
        tail0.add("tensor", lambda e, i: e.matmul(ps[5][0:HI, 0:1], upper[0:HI, 0:HI], cum[0:HI, P - 1:P],
                                                  start=True, stop=True))
        tail0.add(V, lambda e, i: e.tensor_copy(before[0:HI, :], ps[5][0:HI, 0:1]))
        tail0.add(V, lambda e, i: e.tensor_scalar(cum[0:HI, :], cum[0:HI, :], before[0:HI, 0:1], None, ALU.add))
        tail0.add("sync", lambda e, i: [e.dma_start(end_d.rearrange("(a b) -> a b", b=P), cum[0:HI, :]),
                                        e.dma_start(cnt_d.rearrange("(a b) -> a b", b=P), hist[0:HI, :])], "hw", 2)
        tail0.add("sync", lambda e, i: [e.dma_start(endf[:, :], end_d.rearrange("(p j) -> p j", j=J)),
                                        e.dma_start(degf[:, :], cnt_d.rearrange("(p j) -> p j", j=J))], "hw", 2)

        def ends(e, i):
            e.tensor_scalar(last_i[:, :], endf[:, :], -1.0, 0.0, ALU.add, ALU.max)
            e.tensor_scalar(rdeg[:, :], degf[:, :], 1.0, None, ALU.max)
            e.tensor_scalar(nonempty[:, :], degf[:, :], 0.0, None, ALU.is_gt)
            return e.tensor_tensor(endf[:, :], endf[:, :], degf[:, :], ALU.subtract)
        tail0.add(V, ends)
        tail0.add(V, lambda e, i: e.tensor_tensor(endf[:, :], endf[:, :], dumpn[:, :], ALU.subtract))
        tail0.add(V, lambda e, i: e.tensor_tensor(endf[:, :], endf[:, :], nonempty[:, :], ALU.mult))
        tail0.add(V, lambda e, i: e.tensor_tensor(start_i[:, :], endf[:, :], dumpn[:, :], ALU.add))
        tail0.add(V, lambda e, i: e.reciprocal(rdeg[:, :], rdeg[:, :]))
        normalise(tail0, hs, xs, part)
        tail0.add(V, lambda e, i: e.tensor_copy(both[:, :, 0:D], hs[:, :, :]))
        tail0.prepare()

        with ExitStack() as ctx:
            attr = [sb(f"attr{h}", [P, HALF, FE], f32, ctx) for h in range(2)]
            pack = [sb(f"attr_and_one{h}", [P, HALF, FE + 1], f32, ctx) for h in range(2)]
            val = [sb(f"val{h}", [P, HALF, D], f32, ctx) for h in range(2)]
            eq = [sb(f"eq{k}", [P, 4, P], f32, ctx) for k in range(2)]
            sfs = [sb(f"src_tile{h}", [P, HALF], f32, ctx) for h in range(2)]
            dups = [sb(f"dups{h}", [P, HALF], f32, ctx) for h in range(2)]
            scr = [sb(f"scratch{k}", [P, P], f32, ctx) for k in range(8)]
            tgt = sb("target_f", [P, HALF], f32, ctx)
            ohlo = [sb(f"onehot_lo{h}", [P, HALF, P], bf16, ctx) for h in range(2)]
            ohhi = [sb(f"onehot_hi{h}", [P, HALF, HI], bf16, ctx) for h in range(2)]
            s_attr = [sem(f"l0_attr{h}") for h in range(2)]
            s_stage, s_psrc, s_eq, s_sum, s_val, s_hot, s_hist, s_hadd, s_dup, s_tgt, s_vfree, s_acc = (
                sem(f"l0_{n}") for n in ("staged", "src_rows", "equal", "summed", "values", "onehots", "hist",
                                         "hist_added", "dup", "targets", "val_free", "pace"))
            s_add = [sem(f"l0_acc{k}") for k in range(NACC)]
            s_init, s_tail, s_pack, s_zero = sem("l0_init"), sem("l0_tail"), sem("l0_packed"), sem("l0_zeroed")
            LOOPS = T // (2 * HALF)
            attr_v = edge_attr[0:P * TF, :].rearrange("(p t) f -> p t f", t=TF)

            with nc.Block() as block:
                @block.sync
                def _(e):

                    def zeros(i):
                        for table in (spread_d, spread8_d):
                            w = 2 * HALF * table.shape[1]
                            e.dma_start(table[0:EP, :].rearrange("(p t) f -> p (t f)", p=P)[:, bass.ds(i * w, w)],
                                        zero[:, 0:w]).then_inc(s_zero, 16)

                    def load(i, h, last=False):
                        e.wait_ge(s_pack, i * 2 + h + 1)
                        t0 = (i * 2 + h) * HALF
                        if last:
                            e.dma_start(attr[h][:, HALF - 1, :], zero[:, 0:FE]).then_inc(s_tail, 16)
                            e.wait_ge(s_tail, 16)
                            e.dma_start(attr[h][0:REST, HALF - 1, :], edge_attr[P * TF:E, :]).then_inc(s_tail, 16)
                            e.wait_ge(s_tail, 32)
                            e.dma_start(attr[h][:, 0:HALF - 1, :], attr_v[:, t0:TF, :]).then_inc(s_attr[h], 16)
                        else:
                            e.dma_start(attr[h][:, :, :], attr_v[:, bass.ds(t0, HALF), :]).then_inc(s_attr[h], 16)
                    if LOOPS > 1:
                        with e.Fori(0, LOOPS - 1) as i:
                            load(i, 0)
                            load(i, 1)
                            zeros(i)
                    load(LOOPS - 1, 0)
                    load(LOOPS - 1, 1, last=True)
                    zeros(LOOPS - 1)
                    e.wait_ge(s_zero, 16 * 2 * LOOPS)
                    tail0.run("sync", e)

                @block.tensor
                def _(e):
                    e.sem_inc(s_sum, 2 * NG + 1)
                    e.wait_ge(s_init, 1)
                    with e.Fori(0, LOOPS) as i:
                        for h in range(2):
                            hh = i * 2 + h
                            e.wait_ge(s_stage, hh + 1)

                            def rows(k):
                                lo, hi = GROUPS[k]
                                e.wait_ge(s_eq, hh * NG + k + 1)
                                for r in range(lo, hi):
                                    last = e.transpose(ps[(h + k) % 2][:, (r - lo) * P:(r - lo + 1) * P],
                                                       bc(sfs[h][:, r:r + 1], [P, P]), ident[:, :])
                                last.then_inc(s_psrc, 1)

                            def sums(k):
                                lo, hi = GROUPS[k]
                                e.wait_ge(s_eq, hh * NG + k + 3)
                                e.wait_ge(s_val, hh * NG + k + 1)
                                if k == 0:
                                    e.wait_ge(s_pack, hh + 3)
                                for r in range(lo, hi):
                                    o = ps[2 + (h + k) % 2][:, (r - lo) * D:(r - lo + 1) * D]
                                    same_src = eq[(h + k) % 2][:, r - lo, :]
                                    last = e.matmul(o[:, 0:FE + 1], same_src, pack[h][:, r, :], start=True, stop=True)
                                last.then_inc(s_sum, 1)

                            rows(0)
                            for k in range(1, NG):
                                rows(k)
                                sums(k - 1)
                            sums(NG - 1)
                            e.wait_ge(s_hot, hh + 1)
                            e.wait_ge(s_hadd, hh + 1)
                            for r in range(HALF):
                                last = e.matmul(ps[4][0:HI, 0:P], ohhi[h][:, r, :], ohlo[h][:, r, :],
                                                start=(r == 0), stop=(r == HALF - 1))
                            last.then_inc(s_hist, 1)
                    tail0.run("tensor", e)

                @block.vector
                def _(e):
                    e.memset(ps[4][:, 0:P], 0.0)
                    for h in range(2):
                        e.memset(val[h][:, :, FE + 1:D], 0.0)
                        last = e.memset(pack[h][:, :, FE:FE + 1], 1.0)
                    last.then_inc(s_init, 1)
                    e.sem_inc(s_eq, 2)
                    e.sem_inc(s_hist, 1)
                    e.wait_ge(s_init, 1)
                    with e.Fori(0, LOOPS) as i:
                        for h in range(2):
                            hh = i * 2 + h
                            t0 = hh * HALF
                            e.wait_ge(s_stage, hh + 1)
                            for k, (lo, hi) in enumerate(GROUPS):
                                G, n, m = hh * NG + k, hi - lo, (h + k) % 2
                                e.wait_ge(s_psrc, G + 1)
                                e.wait_ge(s_sum, G + 2 * NG)
                                e.wait_ge(s_eq, G + 1)
                                for r in range(lo, hi):
                                    e.scalar_tensor_tensor(scr[4 * m + r - lo][:, :], ps[m][:, (r - lo) * P:(r - lo + 1) * P],
                                                           sfs[h][:, r:r + 1], lower[:, :], ALU.is_equal, ALU.mult,
                                                           accum_out=dups[h][:, r:r + 1])
                                e.tensor_tensor(eq[m][:, 0:n, :], ps[m][:, 0:n * P].rearrange("p (r j) -> p r j", j=P),
                                                bc(sfs[h][:, lo:hi].unsqueeze(2), [P, n, P]), ALU.is_equal)\
                                 .then_inc(s_eq, 1)
                            e.wait_ge(s_eq, (hh + 1) * NG + 2)
                            e.tensor_scalar(dups[h][:, :], dups[h][:, :], 0.0, None, ALU.is_equal).then_inc(s_dup, 1)
                            e.wait_ge(s_dup, hh * 3 + 1)
                            e.scalar_tensor_tensor(tgt[:, :], sfs[h][:, :], dumprow[:, 0:1], dups[h][:, :],
                                                   ALU.subtract, ALU.mult).then_inc(s_dup, 1)
                            e.wait_ge(s_dup, hh * 3 + 2)
                            e.tensor_scalar(tgt[:, :], tgt[:, :], dumprow[:, 0:1], None, ALU.add).then_inc(s_dup, 1)
                            e.wait_ge(s_dup, hh * 3 + 3)
                            e.wait_ge(s_vfree, hh + 1)
                            e.tensor_copy(idx[h][:, :], tgt[:, :]).then_inc(s_tgt, 1)
                            e.tensor_tensor(ohlo[h][:, :, :], bc(iota[:, :].unsqueeze(1), [P, HALF, P]),
                                            bc(dlo[:, bass.ds(t0, HALF)].unsqueeze(2), [P, HALF, P]), ALU.is_equal)
                            e.tensor_tensor(ohhi[h][:, :, :], bc(iota[:, 0:HI].unsqueeze(1), [P, HALF, HI]),
                                            bc(dhi[:, bass.ds(t0, HALF)].unsqueeze(2), [P, HALF, HI]),
                                            ALU.is_equal).then_inc(s_hot, 1)
                            e.wait_ge(s_hist, hh + 1)
                            e.tensor_tensor(hist[0:HI, :], hist[0:HI, :], ps[4][0:HI, 0:P], ALU.add)\
                             .then_inc(s_hadd, 1)
                    e.wait_ge(s_hist, 2 * LOOPS + 1)
                    e.wait_ge(s_hadd, 2 * LOOPS)
                    e.tensor_tensor(hist[0:HI, :], hist[0:HI, :], ps[4][0:HI, 0:P], ALU.add).then_inc(s_hadd, 1)
                    e.wait_ge(s_hadd, 2 * LOOPS + 1)
                    tail0.run("vector", e)

                @block.scalar
                def _(e):
                    e.wait_ge(s_init, 1)
                    e.sem_inc(s_val, 2)
                    e.sem_inc(s_pack, 2)
                    e.copy(sfs[0][:, :], src0f[:, 0:HALF]).then_inc(s_stage, 1)
                    with e.Fori(0, LOOPS) as i:
                        for h in range(2):
                            hh = i * 2 + h
                            e.wait_ge(s_tgt, hh + 2)
                            e.copy(sfs[1 - h][:, :], src0f[:, bass.ds((hh + 1) * HALF, HALF)]).then_inc(s_stage, 1)
                            e.wait_ge(s_attr[h], (i + 1) * 16)
                            e.copy(pack[h][:, :, 0:FE], attr[h][:, :, :]).then_inc(s_pack, 1)
                            e.wait_ge(s_vfree, hh + 1)
                            for k, (lo, hi) in enumerate(GROUPS):
                                n = hi - lo
                                e.wait_ge(s_sum, hh * NG + k + 1 + 2 * NG + 1)
                                e.copy(val[h][:, lo:hi, 0:FE + 1],
                                       ps[2 + (h + k) % 2][:, 0:n * D].rearrange("p (u f) -> p u f", f=D)[:, :, 0:FE + 1])\
                                 .then_inc(s_val, 1)
                    tail0.run("scalar", e)

                @block.gpsimd
                def _(e):
                    e.sem_inc(s_vfree, 1)
                    e.sem_inc(s_tgt, 2)
                    for k in range(NACC):
                        e.dma_start(acc_d[k][0:1, :], zero[0:1, 0:D]).then_inc(s_add[k], 16)
                    with e.Fori(0, LOOPS) as i:
                        for h in range(2):
                            hh = i * 2 + h
                            e.wait_ge(s_tgt, hh + 3)
                            e.wait_ge(s_val, (hh + 1) * NG + 2)
                            for r in range(HALF):
                                q, k = divmod(h * HALF + r, NACC)
                                e.wait_ge(s_add[k], (i * (2 * HALF // NACC) + q) * 16 + 16)
                                e.sem_inc(s_acc, 1)
                                e.indirect_dma_start(acc_d[k], bass.IndirectOffsetOnAxis(ap=idx[h][:, r:r + 1], axis=0),
                                                     val[h][:, r, :], None, compute_op=ALU.add).then_inc(s_add[k], 16)
                                if r == NACC - 1:
                                    e.sem_inc(s_vfree, 1)
                    for k in range(NACC):
                        e.wait_ge(s_add[k], 16 * (LOOPS * (2 * HALF // NACC) + 1))

        with ExitStack() as ctx:
            agg = sb("agg", [P, J, D], f32, ctx)
            w0a_s = sb("w0a", [D + FE, 256], f32, ctx)
            w0b_s = sb("w0b", [P, 2, D], f32, ctx)
            b0a_s = sb("b0a", [P, 2], f32, ctx)
            b0b_s = sb("b0b", [P, D], f32, ctx)
            V = "vector"
            ch = chain("nodes0")
            more = [part] + [sb(f"accumulator{k}", [P, J, D], f32, ctx) for k in range(2, NACC)]
            ch.add("sync", lambda e, i: [
                e.dma_start(t[:, :, :], per_node(acc_d[k][0:NP, :])) for k, t in enumerate([agg] + more)] + [
                e.dma_start(w0a_s[:, :], w0a),
                e.dma_start(w0b_s[:, :, :], w0b.rearrange("(c p) n -> p c n", p=P)),
                e.dma_start(b0a_s[:, :], b0a), e.dma_start(b0b_s[:, :], b0b.partition_broadcast(P))], "hw", NACC + 4)
            for t in more:
                ch.add(V, lambda e, i, t=t: e.tensor_tensor(agg[:, :, :], agg[:, :, :], t[:, :, :], ALU.add))
            ch.add(V, lambda e, i: e.tensor_scalar(st[:, :], agg[:, :, FE], 1.0, None, ALU.max))
            ch.add(V, lambda e, i: e.reciprocal(st[:, :], st[:, :]))
            ch.add(V, lambda e, i: e.tensor_tensor(both[:, :, D:D + FE], agg[:, :, 0:FE],
                                                   bc(st[:, :].unsqueeze(2), [P, J, FE]), ALU.mult))
            ch.add(V, lambda e, i: e.tensor_tensor(xs[:, :, :], xs[:, :, :], bc(b0b_s[:, :].unsqueeze(1), [P, J, D]),
                                                   ALU.add))

            def mlp0(lp, k, lo, n, pb):
                step = sb(f"both_step{k}", [P, n, D + FE], f32, ctx)
                ct = sb(f"both_t{k}", [D + FE, n * P], f32, ctx)
                ht = sb(f"hidden_t{k}", [P, 2, n * P], f32, ctx)
                lp.add(V, lambda e, i: e.tensor_copy(step[:, :, :], both[:, bass.ds(i * JB + lo, n), :]))
                lp.add("tensor", transposes(step, D + FE, n, pb[0]))
                lp.add("scalar", lambda e, i: e.copy(ct[:, :], pb[0][0:D + FE, 0:n * P]))

                def up(e, i):
                    for c in range(2):
                        last = e.matmul(pb[1 + c][:, 0:n * P], w0a_s[:, c * P:(c + 1) * P], ct[:, :], start=True,
                                        stop=True)
                    return last
                lp.add("tensor", up)

                def relu(e, i):
                    for c in range(2):
                        last = e.activation(ht[:, c, :], pb[1 + c][:, 0:n * P], ACT.Relu, bias=b0a_s[:, c:c + 1])
                    return last
                lp.add("scalar", relu)

                def down(e, i):
                    for j in range(n):
                        for c in range(2):
                            last = e.matmul(pb[3][:, j * D:(j + 1) * D], ht[:, c, j * P:(j + 1) * P], w0b_s[:, c, :],
                                            start=(c == 0), stop=(c == 1))
                    return last
                lp.add("tensor", down)
                at = lambda i: bass.ds(i * JB + lo, n)
                lp.add(V, lambda e, i: e.tensor_tensor(xs[:, at(i), :], xs[:, at(i), :], tiles(pb[3], n), ALU.add))
            lp = two_lanes("mlp0", mlp0)
            ch2 = chain("norm1")
            normalise(ch2, hs, xs, part)
            ch2.add("sync", lambda e, i: e.dma_start(per_node(h1_d), hs[:, :, :]), "hw")
            stage(ch, lp, ch2)
        nd.close()
        l0.close()


        def edge_pass(name, table, index, gbuf, alpha=None):
            LP = T // (2 * HALF)
            wide = alpha is not None
            s_rows = [sem(f"{name}_rows{k}") for k in range(NG if wide else 2)]
            s_st = [sem(f"{name}_store{h}") for h in range(2)]
            s_idx, s_pace, s_step, s_run, s_mul, s_mix, s_free = (
                sem(f"{name}_{n}") for n in ("staged", "pace", "step", "run", "scaled", "mixed", "free"))
            with ExitStack() as ctx, nc.Block() as block:
                if wide:
                    astage = [sb(f"{name}_alpha{h}", [P, HALF, HEADS], f32, ctx) for h in range(2)]
                    mixed = sb(f"{name}_mixed", [P, 4, D], f32, ctx)

                @block.scalar
                def _(e):
                    with e.Fori(0, LP) as i:
                        for h in range(2):
                            hh = i * 2 + h
                            e.wait_ge(s_run, hh + 1)
                            e.copy(idx[h][:, :], index[:, bass.ds(hh * HALF, HALF)])
                            if wide:
                                e.copy(astage[h][:, :, :], alpha[:, bass.ds(hh * HALF, HALF), :])
                            e.copy(mask[h][:, :], same[:, bass.ds(hh * HALF, HALF)]).then_inc(s_idx, 1)

                @block.gpsimd
                def _(e):
                    with e.Fori(0, LP) as i:
                        for h in range(2):
                            hh = i * 2 + h
                            e.wait_ge(s_idx, hh + 1)
                            e.sem_inc(s_pace, 1)
                            for k, (lo, hi) in enumerate(GROUPS):
                                if wide:
                                    e.wait_ge(s_free, hh * NG + k + 1)
                                    e.sem_inc(s_pace, 1)
                                for r in range(lo, hi):
                                    to = gbuf[0 if wide else h][:, r, :]
                                    e.indirect_dma_start(to, None, table,
                                                         bass.IndirectOffsetOnAxis(ap=idx[h][:, r:r + 1], axis=0))\
                                     .then_inc(s_rows[k if wide else h], 16)

                @block.vector
                def _(e):
                    e.sem_inc(s_run, 2)
                    if wide:
                        e.sem_inc(s_free, NG)
                    e.memset(run[1][:, HALF - 1, :], 0.0).then_inc(s_step, 1)
                    def step(i, h, r, row):
                        before_row = run[h][:, r - 1, :] if r else run[1 - h][:, HALF - 1, :]
                        e.wait_ge(s_step, (i * 2 + h) * HALF + r + 1)
                        e.scalar_tensor_tensor(run[h][:, r, :], before_row, mask[h][:, r:r + 1], row,
                                               ALU.mult, ALU.add).then_inc(s_step, 1)

                    def scale(i, h, k):
                        lo, hi = GROUPS[k]
                        if k == 0:
                            e.wait_ge(s_idx, i * 2 + h + 1)
                        e.wait_ge(s_rows[k], (i * 2 + h + 1) * 16 * (hi - lo))
                        g3 = gbuf[0][:, lo:hi, :].rearrange("p r (a f) -> p (r a) f", f=D)
                        a3 = astage[h][:, lo:hi, :].rearrange("p r a -> p (r a)").unsqueeze(2)
                        e.tensor_tensor(g3, g3, bc(a3, [P, (hi - lo) * HEADS, D]), ALU.mult).then_inc(s_mul, 1)

                    def steps(i, h, k):
                        lo, hi = GROUPS[k]
                        hh = i * 2 + h
                        G = hh * NG + k
                        if k == 0:
                            e.wait_ge(s_st[h], i * 16 + 16)
                        e.wait_ge(s_mix, G + 1)
                        e.wait_ge(s_step, hh * HALF + lo + 1)
                        g4 = gbuf[0][:, lo:hi, (HEADS - 1) * D:HD]
                        o = ps[(h * NG + k) % 2][:, 0:(hi - lo) * D].rearrange("p (r f) -> p r f", f=D)
                        e.tensor_tensor(mixed[:, 0:hi - lo, :], o, g4, ALU.add).then_inc(s_free, 1)
                        e.wait_ge(s_free, G + NG + 1)
                        for r in range(lo, hi):
                            step(i, h, r, mixed[:, r - lo, :])
                        if k == NG - 1:
                            e.wait_ge(s_step, (hh + 1) * HALF + 1)
                            e.sem_inc(s_run, 1)

                    if wide:
                        order = [(h, k) for h in range(2) for k in range(NG)]
                        scale(0, *order[0])

                        def round_of(i, last=False):
                            for now, then in zip(order, order[1:]):
                                scale(i, *then)
                                steps(i, *now)
                            if not last:
                                scale(i + 1, *order[0])
                            steps(i, *order[-1])
                        if LP > 1:
                            with e.Fori(0, LP - 1) as i:
                                round_of(i)
                        round_of(LP - 1, last=True)
                    else:
                        with e.Fori(0, LP) as i:
                            for h in range(2):
                                hh = i * 2 + h
                                e.wait_ge(s_idx, hh + 1)
                                e.wait_ge(s_st[h], i * 16 + 16)
                                e.wait_ge(s_rows[h], (i + 1) * 16 * HALF)
                                for r in range(HALF):
                                    step(i, h, r, gbuf[h][:, r, :])
                                e.wait_ge(s_step, (hh + 1) * HALF + 1)
                                e.sem_inc(s_run, 1)

                if wide:
                    @block.tensor
                    def _(e):
                        with e.Fori(0, LP) as i:
                            for h in range(2):
                                for k, (lo, hi) in enumerate(GROUPS):
                                    G = (i * 2 + h) * NG + k
                                    e.wait_ge(s_mul, G + 1)
                                    e.wait_ge(s_free, G + NG - 1)
                                    g4 = gbuf[0][:, lo:hi, :].rearrange("p r (a f) -> p r a f", f=D)
                                    for a in range(HEADS - 1):
                                        last = e.matmul(ps[(h * NG + k) % 2][:, 0:(hi - lo) * D], ident[:, :],
                                                        g4[:, :, a, :], start=(a == 0), stop=(a == HEADS - 2))
                                    last.then_inc(s_mix, 1)

                @block.sync
                def _(e):
                    for h in range(2):
                        e.dma_start(per_edge(run_d)[:, h:h + 1, :], hs[:, 0:1, :]).then_inc(s_st[h], 16)
                    for h in range(2):
                        e.wait_ge(s_st[h], 16)
                    with e.Fori(0, LP) as i:
                        for h in range(2):
                            hh = i * 2 + h
                            e.wait_ge(s_run, hh + 3)
                            e.dma_start(per_edge(run_d)[:, bass.ds(hh * HALF, HALF), :], run[h][:, :, :])\
                             .then_inc(s_st[h], 16)
                    for h in range(2):
                        e.wait_ge(s_st[h], 16 * (LP + 1))

        def collect(ch, res, table, tail, w, stores=()):
            per = 512 // w

            def carry(e, i):
                for j in range(J):
                    last = e.matmul(ps[j // per][:, (j % per) * w:(j % per + 1) * w], link[:, j, :], tail,
                                    start=True, stop=True)
                return last
            ch.beside("tensor", carry)
            ch.add("gpsimd", lambda e, i: [
                e.indirect_dma_start(res[:, j, :], None, table,
                                     bass.IndirectOffsetOnAxis(ap=last_i[:, j:j + 1], axis=0)) for j in range(J)],
                   "sw", J, join=stores)
            ch.add("vector", lambda e, i: e.tensor_tensor(res[:, :, :], res[:, :, :],
                                                          bc(nonempty[:, :].unsqueeze(2), [P, J, w]), ALU.mult))
            def fold(e, i):
                for b in range(-(-J // per)):
                    n = min(per, J - b * per)
                    last = e.tensor_tensor(res[:, b * per:b * per + n, :], res[:, b * per:b * per + n, :],
                                           ps[b][:, 0:n * w].rearrange("p (j f) -> p j f", f=w), ALU.add)
                return last
            ch.add("vector", fold, join=True)

        with ExitStack() as ctx:
            g = [sb(f"rows_l1_{h}", [P, HALF, D], f32, ctx) for h in range(2)]
            edge_pass("l1", h1_d, src_i, g)

        asn = sb("att_src_node", [P, J, HEADS])
        adn = sb("att_dst_node", [P, J, HEADS])
        with ExitStack() as ctx:
            neigh = sb("neigh", [P, J, D], f32, ctx)
            w1_s = sb("w1", [P, D], f32, ctx)
            b1_s = sb("b1", [P, D], f32, ctx)
            ch = chain("nodes1")
            ch.beside("sync", lambda e, i: [e.dma_start(w1_s[:, :], w1),
                                            e.dma_start(b1_s[:, :], b1.partition_broadcast(P))], 2)
            collect(ch, neigh, run_d, run[1][:, HALF - 1, :], D)
            ch.add(V, lambda e, i: e.tensor_tensor(neigh[:, :, :], neigh[:, :, :],
                                                   bc(rdeg[:, :].unsqueeze(2), [P, J, D]), ALU.mult))
            def dense1(lp, k, lo, n, pb):
                pair = sb(f"pair{k}", [P, n, 2 * D], f32, ctx)
                pt = sb(f"pair_t{k}", [P, n * P], f32, ctx)
                pre = sb(f"before_relu{k}", [P, n, D], f32, ctx)
                at = lambda i: bass.ds(i * JB + lo, n)

                def join(e, i):
                    e.tensor_copy(pair[:, :, 0:D], hs[:, at(i), :])
                    return e.tensor_copy(pair[:, :, D:2 * D], neigh[:, at(i), :])
                lp.add(V, join)
                lp.add("tensor", transposes(pair, 2 * D, n, pb[0]))
                lp.add("scalar", lambda e, i: e.copy(pt[:, :], pb[0][:, 0:n * P]))

                def product(e, i):
                    for j in range(n):
                        last = e.matmul(pb[1][:, j * D:(j + 1) * D], pt[:, j * P:(j + 1) * P], w1_s[:, :],
                                        start=True, stop=True)
                    return last
                lp.add("tensor", product)
                lp.add(V, lambda e, i: e.tensor_tensor(pre[:, :, :], tiles(pb[1], n),
                                                       bc(b1_s[:, :].unsqueeze(1), [P, n, D]), ALU.add))
                lp.add(V, lambda e, i: e.scalar_tensor_tensor(xs[:, at(i), :], pre[:, :, :], 0.0, xs[:, at(i), :],
                                                              ALU.max, ALU.add))
            lp = two_lanes("dense1_", dense1)
            ch2 = chain("norm2")
            normalise(ch2, hs, xs, neigh)
            stage(ch, lp, ch2)

        s_feat = [sem(f"features_stored{k}") for k in range(2)]
        s_rel = [sem(f"relations_stored{k}") for k in range(2)]

        def start_stores(e, sems, n):
            for s in sems:
                e.sem_inc(s, 16 * n)

        att = ExitStack()
        alpha = sb("alpha", [P, T, HEADS], f32, att)
        selfw = sb("self_weight", [P, J, HEADS], f32, att)
        look = ExitStack()
        split = [sb(f"logit_part{k}", [P, HI * HEADS], bf16, look) for k in range(3)]
        src_lo = sb("src_lo", [P, T], f32, look)
        src_hi = sb("src_hi", [P, T], f32, look)
        with ExitStack() as ctx:
            tmp_i = sb("src_tmp", [P, T], i32, ctx)
            whole = sb("logit_table", [P, HI * HEADS], f32, ctx)
            watt_s = sb("watt", [D, HD], f32, ctx)
            attb = sb("att_rows", [D, 2, HD], f32, ctx)
            wlog = sb("logit_weights", [D, 2 * HEADS], f32, ctx)
            ch = chain("att_weights")
            ch.add("sync", lambda e, i: start_stores(e, s_feat, 1) or [
                                         e.dma_start(watt_s[:, :], watt),
                                         e.dma_start(attb[:, 0, :], att_s.rearrange("a f -> (a f)").partition_broadcast(D)),
                                         e.dma_start(attb[:, 1, :], att_d.rearrange("a f -> (a f)").partition_broadcast(D))],
                   "hw", 3)
            for k in range(2):
                ch.add(V, lambda e, i, k=k: e.tensor_tensor(attb[:, k, :], attb[:, k, :], watt_s[:, :], ALU.mult))
                ch.add(V, lambda e, i, k=k: e.tensor_reduce(wlog[:, k * HEADS:(k + 1) * HEADS],
                                                            attb[:, k, :].rearrange("p (a f) -> p a f", f=D), X,
                                                            ALU.add))
            def features(lp, k, lo, n, pb):
                step = sb(f"h_step{k}", [P, n, D], f32, ctx)
                ht = sb(f"h_step_t{k}", [D, n * P], f32, ctx)
                feat = sb(f"att_features{k}", [P, n, HD], f32, ctx)
                at = lambda i: bass.ds(i * JB + lo, n)
                lp.add(V, lambda e, i: e.tensor_copy(step[:, :, :], hs[:, at(i), :]))
                lp.add("tensor", transposes(step, D, n, pb[0]))
                lp.add("scalar", lambda e, i: e.copy(ht[:, :], pb[0][0:D, 0:n * P]))
                for two in ((0, 2), (2, n)):
                    def project(e, i, two=two):
                        for j in range(*two):
                            last = e.matmul(pb[1 + j % 2][:, :], ht[:, j * P:(j + 1) * P], watt_s[:, :], start=True,
                                            stop=True)
                        if two[0]:
                            for j in range(n):
                                last = e.matmul(pb[3][:, j * 16:(j + 1) * 16], ht[:, j * P:(j + 1) * P], wlog[:, :],
                                                start=True, stop=True)
                        return last
                    lp.add("tensor", project)

                    def evacuate(e, i, two=two):
                        if two[0] == 0:
                            e.wait_ge(s_feat[k], i * 16 + 16)
                        for j in range(*two):
                            last = e.copy(feat[:, j, :], pb[1 + j % 2][:, :])
                        return last
                    lp.add("scalar", evacuate)

                def store(e, i):
                    e.dma_start(per_node(hw_d)[:, at(i), :], feat[:, :, :]).then_inc(s_feat[k], 16)
                lp.add("sync", store)

                def logits(e, i):
                    t = tiles(pb[3], n, 16)
                    e.tensor_copy(asn[:, at(i), :], t[:, :, 0:HEADS])
                    return e.tensor_copy(adn[:, at(i), :], t[:, :, HEADS:16])
                lp.add(V, logits)
            lp = two_lanes("features", features)
            ch2 = chain("att_tables")
            for part, op, n in ((src_lo, ALU.bitwise_and, P - 1), (src_hi, ALU.logical_shift_right, 7)):
                ch2.beside(V, lambda e, i, op=op, n=n: e.tensor_scalar(tmp_i[:, :], src_i[:, :], n, None, op))
                ch2.beside(V, lambda e, i, part=part: e.tensor_copy(part[:, :], tmp_i[:, :]))
            ch2.add("sync", lambda e, i: e.dma_start(per_node(as_d), asn[:, :, :]), "hw")

            def stored(e, sems, n):
                for s in sems:
                    e.wait_ge(s, 16 * n * (J // JB + 1))
            ch2.add("sync", lambda e, i: stored(e, s_feat, 1) or e.dma_start(
                whole[:, :].rearrange("p (h f) -> p h f", f=HEADS), as_d.rearrange("(h p) f -> p h f", p=P)), "hw")
            for k in range(3):
                ch2.add(V, lambda e, i, k=k: e.tensor_copy(split[k][:, :], whole[:, :]), join=(k == 0))
                if k < 2:
                    ch2.add(V, lambda e, i, k=k: e.tensor_tensor(whole[:, :], whole[:, :], split[k][:, :],
                                                                 ALU.subtract))
            stage(ch, lp, ch2)

        with ExitStack() as ctx:
            LG, LN = 4, 3
            BY_ROW = HALF - LG * LN
            W = HI * HEADS
            ORDER = [(h, k) for h in range(2) for k in range(LG)]
            rows8 = [sb(f"logit_rows{h}", [P, BY_ROW, HEADS], f32, ctx) for h in range(2)]
            lo_s = [sb(f"lo_step{h}", [P, LG * LN], f32, ctx) for h in range(2)]
            hi_s = [sb(f"hi_step{h}", [P, LG * LN], f32, ctx) for h in range(2)]
            onhi = [sb(f"onehot_hi_src{h}", [P, LG * LN, HI], f32, ctx) for h in range(2)]
            onlo = [sb(f"onehot_lo_src{k}", [P, LN * P], bf16, ctx) for k in range(2)]
            picked = [sb(f"picked{k}", [P, LN, W], f32, ctx) for k in range(2)]
            s_g = [sem(f"l2a_rows{h}") for h in range(2)]
            s_idx, s_use, s_pace, s_lo, s_on, s_look, s_pick, s_red, s_hi = (
                sem(f"l2a_{n}") for n in ("staged", "used", "pace", "lo_rows", "onehots", "looked_up", "picked",
                                          "reduced", "hi_onehots"))
            LP = T // (2 * HALF)
            with nc.Block() as block:
                @block.scalar
                def _(e):
                    with e.Fori(0, LP) as i:
                        for h in range(2):
                            hh = i * 2 + h
                            t0 = hh * HALF
                            e.wait_ge(s_use, hh + 1)
                            e.copy(idx[h][:, 0:BY_ROW], src_i[:, bass.ds(t0, BY_ROW)])
                            e.copy(hi_s[h][:, :], src_hi[:, bass.ds(t0 + BY_ROW, LG * LN)])
                            e.copy(lo_s[h][:, :], src_lo[:, bass.ds(t0 + BY_ROW, LG * LN)]).then_inc(s_idx, 1)

                @block.gpsimd
                def _(e):
                    with e.Fori(0, LP) as i:
                        for h in range(2):
                            e.wait_ge(s_idx, i * 2 + h + 1)
                            e.sem_inc(s_pace, 1)
                            for r in range(BY_ROW):
                                e.indirect_dma_start(rows8[h][:, r, :], None, as_d,
                                                     bass.IndirectOffsetOnAxis(ap=idx[h][:, r:r + 1], axis=0))\
                                 .then_inc(s_g[h], 16)

                @block.tensor
                def _(e):
                    def rows(i, h, k):
                        if k == 0:
                            e.wait_ge(s_idx, i * 2 + h + 1)
                        e.wait_ge(s_on, (i * 2 + h) * LG + k + 1)
                        for r in range(LN):
                            last = e.transpose(ps[k % 2][:, r * P:(r + 1) * P],
                                               bc(lo_s[h][:, k * LN + r:k * LN + r + 1], [P, P]), ident[:, :])
                        last.then_inc(s_lo, 1)

                    def products(i, h, k):
                        G = (i * 2 + h) * LG + k
                        e.wait_ge(s_on, G + 3)
                        e.wait_ge(s_pick, G + 1)
                        for r in range(LN):
                            for n in range(3):
                                last = e.matmul(ps[2 + LN * (k % 2) + r][:, 0:W],
                                                onlo[k % 2][:, r * P:(r + 1) * P], split[n][:, :],
                                                start=(n == 0), stop=(n == 2))
                        last.then_inc(s_look, 1)

                    rows(0, *ORDER[0])

                    def round_of(i, last=False):
                        for now, then in zip(ORDER, ORDER[1:]):
                            rows(i, *then)
                            products(i, *now)
                        if not last:
                            rows(i + 1, *ORDER[0])
                        products(i, *ORDER[-1])
                    if LP > 1:
                        with e.Fori(0, LP - 1) as i:
                            round_of(i)
                    round_of(LP - 1, last=True)

                @block.vector
                def _(e):
                    e.sem_inc(s_use, 2)
                    e.sem_inc(s_on, 2)
                    e.sem_inc(s_pick, 2)
                    e.sem_inc(s_red, 2)

                    def compare(i, h, k):
                        hh = i * 2 + h
                        if k == 0:
                            e.wait_ge(s_idx, hh + 1)
                            e.tensor_tensor(onhi[h][:, :, :], bc(iota[:, 0:HI].unsqueeze(1), [P, LG * LN, HI]),
                                            bc(hi_s[h][:, :].unsqueeze(2), [P, LG * LN, HI]), ALU.is_equal)\
                             .then_inc(s_hi, 1)
                        e.wait_ge(s_lo, hh * LG + k + 1)
                        e.tensor_scalar(onlo[k % 2][:, :], ps[k % 2][:, 0:LN * P], part_no[:, 0:1], None,
                                        ALU.is_equal).then_inc(s_on, 1)

                    def pick(i, h, k):
                        G = (i * 2 + h) * LG + k
                        e.wait_ge(s_red, G + 1)
                        e.wait_ge(s_look, G + 1)
                        if k == 0:
                            e.wait_ge(s_hi, i * 2 + h + 1)
                        b = 2 + LN * (k % 2)
                        e.tensor_tensor(
                            picked[k % 2][:, :, :].rearrange("p r (h f) -> p r h f", f=HEADS),
                            banks[:, b:b + LN, 0:W].rearrange("p r (h f) -> p r h f", f=HEADS),
                            bc(onhi[h][:, k * LN:(k + 1) * LN, :].unsqueeze(3), [P, LN, HI, HEADS]),
                            ALU.mult).then_inc(s_pick, 1)

                    def reduce(i, h, k):
                        hh = i * 2 + h
                        e.wait_ge(s_pick, hh * LG + k + 3)
                        e.tensor_reduce(alpha[:, bass.ds(hh * HALF + BY_ROW + k * LN, LN), :],
                                        picked[k % 2][:, :, :].rearrange("p r (h f) -> p r f h", f=HEADS),
                                        X, ALU.add).then_inc(s_red, 1)
                        if k == LG - 1:
                            e.wait_ge(s_g[h], (i + 1) * 16 * BY_ROW)
                            e.wait_ge(s_red, (hh + 1) * LG + 2)
                            e.tensor_copy(alpha[:, bass.ds(hh * HALF, BY_ROW), :], rows8[h][:, :, :])\
                             .then_inc(s_use, 1)

                    compare(0, *ORDER[0])

                    def round_of(i, last=False):
                        for n, now in enumerate(ORDER):
                            if n + 1 < len(ORDER):
                                compare(i, *ORDER[n + 1])
                            elif not last:
                                compare(i + 1, *ORDER[0])
                            pick(i, *now)
                            if n:
                                reduce(i, *ORDER[n - 1])
                        reduce(i, *ORDER[-1])
                    if LP > 1:
                        with e.Fori(0, LP - 1) as i:
                            round_of(i)
                    round_of(LP - 1, last=True)
        look.close()

        with ExitStack() as ctx:
            reset = run[0][:, :, :].rearrange("p r f -> p (r f)")[:, 0:T]
            masks = run[1][:, :, :].rearrange("p r f -> p (r f)")
            cmask, cm1, batt_s = masks[:, 0:P], masks[:, P:2 * P], masks[:, 2 * P:2 * P + D]
            tab = [sb(f"spread_rows{k}", [P, TC, 2 * HEADS], f32, ctx) for k in range(2)]
            halves = [t.rearrange("p t f -> p (t f)")[:, n * TC * HEADS:(n + 1) * TC * HEADS]
                      .rearrange("p (t f) -> p t f", f=HEADS) for t in (tab[0][:, :, :], tab[1][:, :, :])
                      for n in range(2)]
            tabl = sb("spread_last", [P, 2 * HEADS], f32, ctx)
            endm = sb("end_max", [P, HEADS], f32, ctx)
            carm = sb("carry_max", [P, HEADS], f32, ctx)
            fird = sb("first_dst_f", [P, 1], f32, ctx)
            am = sb("att_and_max", [P, J, 2 * HEADS], f32, ctx)
            mx = sb("node_max", [P, J, HEADS], f32, ctx)
            t8 = sb("node_tmp", [P, J, HEADS], f32, ctx)
            ms = sb("mask_stat", [P, J], f32, ctx)
            msg = [sb(f"self_message{k}", [P, OWN, D], f32, ctx) for k in range(2)]
            sx = chain("softmax")
            sx.beside("sync", lambda e, i: [e.dma_start(batt_s, batt.partition_broadcast(P))], 1)

            def chunk(k):
                return slice(k * TC, (k + 1) * TC)

            def scans(data0, data1, outp, init, op0, op1, heads=HEADS, shift=0):
                def fn(e, i):
                    for a in range(heads):
                        last = e.tensor_tensor_scan(outp(a), data0, data1(a), init(a), op0, op1)
                    return last
                return fn
            sx.add(V, lambda e, i: e.tensor_scalar(reset, same[:, :], 1.0, BIG, ALU.subtract, ALU.mult))
            assert len(halves) == NCH
            for rnd in range(2):
                for k in range(NCH):
                    o, b = halves[k], halves[k - 1]
                    init = (lambda a, b=b: b[:, TC - 1, a:a + 1]) if k else (
                        (lambda a: carm[:, a:a + 1]) if rnd else (lambda a: -BIG))
                    sx.add(V, scans(reset[:, chunk(k)], lambda a, k=k: alpha[:, chunk(k), a],
                                    lambda a, o=o: o[:, :, a], init, ALU.add, ALU.max))
                    if rnd:
                        sx.beside("sync", lambda e, i, k=k, o=o: [
                            e.dma_start(per_edge(run8_d)[:, chunk(k), :], o[:, :, :])], 1, lane=k % 2)
                if rnd == 0:
                    sx.add(V, lambda e, i: e.tensor_copy(endm[:, :], halves[NCH - 1][:, TC - 1, :]))
                    sx.add(V, lambda e, i: e.tensor_copy(fird[:, :], first_i[:, :]))
                    sx.add("tensor", lambda e, i: e.transpose(ps[0][:, 0:P], bc(last_f[:, 0:1], [P, P]), ident[:, :]))
                    sx.add(V, lambda e, i: e.tensor_scalar(cmask, ps[0][:, 0:P], fird[:, 0:1], None,
                                                           ALU.is_equal))
                    sx.add("gpsimd", lambda e, i: e.affine_select(out=cmask, in_=cmask,
                                                                  compare_op=ALU.is_gt, fill=0.0, base=0,
                                                                  pattern=[[-1, P]], channel_multiplier=1))
                    sx.add(V, lambda e, i: e.tensor_scalar(cm1, cmask, 1.0, BIG, ALU.subtract, ALU.mult))

                    def spread_ends(e, i):
                        for a in range(HEADS):
                            last = e.transpose(ps[1 + a // 4][:, (a % 4) * P:(a % 4 + 1) * P],
                                               bc(endm[:, a:a + 1], [P, P]), ident[:, :])
                        return last
                    sx.add("tensor", spread_ends)
                    for a in range(HEADS):
                        sx.add(V, lambda e, i, a=a: e.tensor_tensor(
                            cmask, ps[1 + a // 4][:, (a % 4) * P:(a % 4 + 1) * P], cm1, ALU.add))
                        sx.add(V, lambda e, i, a=a: e.tensor_reduce(carm[:, a:a + 1], cmask, X, ALU.max))
            sx.add("gpsimd", lambda e, i: [
                e.indirect_dma_start(mx[:, j, :], None, run8_d,
                                     bass.IndirectOffsetOnAxis(ap=last_i[:, j:j + 1], axis=0)) for j in range(J)],
                   "sw", J, join=True)
            ne8 = bc(nonempty[:, :].unsqueeze(2), [P, J, HEADS])
            sx.add(V, lambda e, i: e.tensor_tensor(mx[:, :, :], mx[:, :, :], ne8, ALU.mult))
            sx.add(V, lambda e, i: e.tensor_scalar(ms[:, :], nonempty[:, :], 1.0, BIG, ALU.subtract, ALU.mult))
            sx.add(V, lambda e, i: e.tensor_tensor(mx[:, :, :], mx[:, :, :],
                                                   bc(ms[:, :].unsqueeze(2), [P, J, HEADS]), ALU.add))
            sx.add(V, lambda e, i: e.tensor_tensor(mx[:, :, :], mx[:, :, :], asn[:, :, :], ALU.max))
            sx.add(V, lambda e, i: e.tensor_tensor(mx[:, :, :], mx[:, :, :], adn[:, :, :], ALU.add))

            def leaky(t, u):
                return lambda e, i: e.scalar_tensor_tensor(t, u, 0.2, u, ALU.mult, ALU.max)
            sx.add(V, leaky(am[:, :, HEADS:16], mx[:, :, :]))
            sx.add(V, lambda e, i: e.tensor_copy(am[:, :, 0:HEADS], adn[:, :, :]))
            sx.beside(V, lambda e, i: e.tensor_tensor(t8[:, :, :], asn[:, :, :], adn[:, :, :], ALU.add), lane=0)
            sx.beside(V, leaky(selfw[:, :, :], t8[:, :, :]), lane=0)
            sx.beside(V, lambda e, i: e.tensor_tensor(selfw[:, :, :], selfw[:, :, :], am[:, :, HEADS:16],
                                                      ALU.subtract), lane=0)
            sx.beside("scalar", lambda e, i: e.activation(selfw[:, :, :], selfw[:, :, :], ACT.Exp), lane=0)
            sx.beside("sync", lambda e, i: [e.dma_start(per_node(am_d), am[:, :, :])], 1, lane=3)

            def spread(table, w):
                return lambda e, i: [
                    e.indirect_dma_start(table, bass.IndirectOffsetOnAxis(ap=start_i[:, j:j + 1], axis=0),
                                         am[:, j, 0:w], None) for j in range(J)]

            def load(k):
                if k < NCH:
                    sx.beside("sync", lambda e, i: [
                        e.dma_start(tab[k % 2][:, :, :], per_edge(spread_d)[:, chunk(k), :])], 1, lane=2, join=(2, 3))
            sx.add("gpsimd", spread(spread_d, 2 * HEADS), "sw", J)
            load(0)
            get_first = lambda e, i: [e.indirect_dma_start(tabl[:, :], None, am_d,
                                                           bass.IndirectOffsetOnAxis(ap=first_i[:, 0:1], axis=0))]
            sx.add("gpsimd", get_first, "sw", 1, join=(3,))
            for k in range(NCH):
                t, o = tab[k % 2], halves[2 * (k % 2)]
                sx.add(V, scans(same[:, chunk(k)], lambda a, t=t: t[:, :, a], lambda a, t=t: t[:, :, a],
                                lambda a: tabl[:, a:a + 1], ALU.mult, ALU.add, 2 * HEADS), join=(2,))
                load(k + 1)
                sx.add(V, lambda e, i, t=t: e.tensor_copy(tabl[:, :], t[:, TC - 1, :]))
                al = alpha[:, chunk(k), :]
                sx.add(V, lambda e, i, al=al, t=t: e.tensor_tensor(al, al, t[:, :, 0:HEADS], ALU.add))
                sx.add(V, leaky(al, al))
                sx.add(V, lambda e, i, al=al, t=t: e.tensor_tensor(al, al, t[:, :, HEADS:16], ALU.subtract))
                sx.add("scalar", lambda e, i, al=al: e.activation(al, al, ACT.Exp))
                init = (lambda a: endm[:, a:a + 1]) if k else (lambda a: 0.0)
                sx.add(V, scans(same[:, chunk(k)], lambda a, k=k: alpha[:, chunk(k), a], lambda a, o=o: o[:, :, a],
                                init, ALU.mult, ALU.add))
                sx.add(V, lambda e, i, o=o: e.tensor_copy(endm[:, :], o[:, TC - 1, :]))
                sx.beside("sync", lambda e, i, k=k, o=o: [
                    e.dma_start(per_edge(run8_d)[:, chunk(k), :], o[:, :, :])], 1, lane=3)
            collect(sx, mx, run8_d, endm[:, :], HEADS, stores=(3,))
            sx.add(V, lambda e, i: e.tensor_tensor(mx[:, :, :], mx[:, :, :], selfw[:, :, :], ALU.add))
            sx.add(V, lambda e, i: e.tensor_scalar(mx[:, :, :], mx[:, :, :], 1e-16, None, ALU.add))
            sx.add(V, lambda e, i: e.reciprocal(mx[:, :, :], mx[:, :, :]))
            sx.add(V, lambda e, i: e.tensor_scalar(am[:, :, 0:HEADS], mx[:, :, :], 1.0 / HEADS, None, ALU.mult))
            sx.add(V, lambda e, i: e.tensor_tensor(selfw[:, :, :], selfw[:, :, :], am[:, :, 0:HEADS], ALU.mult))
            sx.beside("sync", lambda e, i: [e.dma_start(per_node(am_d), am[:, :, :])], 1, lane=3)
            sx.add(V, lambda e, i: e.tensor_tensor(hs[:, :, :], hs[:, :, :],
                                                   bc(batt_s.unsqueeze(1), [P, J, D]), ALU.add), join=(0, 1))
            for n, j in enumerate(range(0, J, OWN)):
                w = min(OWN, J - j)
                f3 = run[n % 2][:, 0:w * HEADS, :]
                sx.beside("sync", lambda e, i, f3=f3, j=j, w=w: [e.dma_start(
                    f3.rearrange("p (j a) f -> p j (a f)", a=HEADS), per_node(hw_d)[:, j:j + w, :])], 1, lane=n % 2)
                sx.beside(V, lambda e, i, f3=f3, j=j, w=w: e.tensor_tensor(
                    f3, f3, bc(selfw[:, j:j + w, :].rearrange("p j a -> p (j a)").unsqueeze(2),
                               [P, w * HEADS, D]), ALU.mult), lane=n % 2)
                sx.beside(V, lambda e, i, f3=f3, m=msg[n % 2], w=w: e.tensor_reduce(
                    m[:, 0:w, :], f3.rearrange("p (j a) f -> p j f a", a=HEADS), X, ALU.add), lane=n % 2)
                sx.beside(V, lambda e, i, j=j, m=msg[n % 2], w=w: e.tensor_tensor(
                    hs[:, j:j + w, :], hs[:, j:j + w, :], m[:, 0:w, :], ALU.add), lane=n % 2)
            sx.add("gpsimd", spread(spread8_d, HEADS), "sw", J)
            def load8(k):
                sx.beside("sync", lambda e, i: [
                    e.dma_start(halves[k][:, :, :], per_edge(spread8_d)[:, chunk(k), :])], 1, lane=2 + k % 2)
            load8(0)
            sx.add("gpsimd", get_first, "sw", 1, join=(3,))
            load8(1)
            for k in range(NCH):
                t = halves[k]
                sx.add(V, scans(same[:, chunk(k)], lambda a, t=t: t[:, :, a], lambda a, t=t: t[:, :, a],
                                lambda a: tabl[:, a:a + 1], ALU.mult, ALU.add), join=(2 + k % 2,))
                if k + 2 < NCH:
                    load8(k + 2)
                sx.add(V, lambda e, i, t=t: e.tensor_copy(tabl[:, 0:HEADS], t[:, TC - 1, :]))
                al = alpha[:, chunk(k), :]
                sx.add(V, lambda e, i, al=al, t=t: e.tensor_tensor(al, al, t[:, :, :], ALU.mult))
            stage(sx)

        with ExitStack() as ctx:
            g = [sb("rows_l2", [P, HALF, HD], f32, ctx)]
            edge_pass("l2", hw_d, src_i, g, alpha)

        with ExitStack() as ctx:
            res = sb("att_out", [P, J, D], f32, ctx)
            x1 = sb("x1", [P, J, D], f32, ctx)
            vecs = {n: sb(f"row_{n}", [P, D], f32, ctx) for n in ("g1", "be1", "g2", "be2", "bf2")}
            wf1_s = sb("wf1", [D, 2 * D], f32, ctx)
            bf1_s = sb("bf1", [P, 1], f32, ctx)
            wf2_s = sb("wf2", [2 * D, D], f32, ctx)
            ch = chain("nodes2")
            typ = sb("edge_type", [P, T], i32, ctx)
            ch.beside(V, lambda e, i: e.memset(typ[:, :], 0))
            ch.beside("sync", lambda e, i: load_runs(e, typ, edge_type), len(rows_of(P - 1)) + 1)
            ch.beside(V, lambda e, i: e.scalar_tensor_tensor(src_i[:, :], typ[:, :], float(NP), src_i[:, :], ALU.mult,
                                                             ALU.add))
            rowsrc = {"g1": g1, "be1": be1, "g2": g2, "be2": be2, "bf2": bf2}
            ch.beside("sync", lambda e, i: [e.dma_start(vecs[n][:, :], rowsrc[n].partition_broadcast(P))
                                            for n in vecs] + [
                e.dma_start(wf1_s[:, :], wf1), e.dma_start(bf1_s[:, :], bf1), e.dma_start(wf2_s[:, :], wf2)], 8)
            collect(ch, res, run_d, run[1][:, HALF - 1, :], D)
            full = [P, J, D]
            ch2 = chain("norm_att")
            ch2.add(V, lambda e, i: e.tensor_tensor(res[:, :, :], res[:, :, :], hs[:, :, :], ALU.add))
            normalise(ch2, x1, res, hs, relu=False, gain=vecs["g1"], shift=vecs["be1"])
            def ffn(lp, k, lo, n, pb):
                step = sb(f"x1_step{k}", [P, n, D], f32, ctx)
                xt = sb(f"x1_step_t{k}", [D, n * P], f32, ctx)
                hid = sb(f"hidden2_t{k}", [P, n * P], f32, ctx)
                at = lambda i: bass.ds(i * JB + lo, n)
                lp.add(V, lambda e, i: e.tensor_copy(step[:, :, :], x1[:, at(i), :]))
                lp.add("tensor", transposes(step, D, n, pb[0]))
                lp.add("scalar", lambda e, i: e.copy(xt[:, :], pb[0][0:D, 0:n * P]))
                lp.add("tensor", lambda e, i: e.matmul(pb[1][:, 0:n * P], wf1_s[:, :], xt[:, :], start=True, stop=True))
                lp.add("scalar", lambda e, i: e.activation(hid[:, :], pb[1][:, 0:n * P], ACT.Relu, bias=bf1_s[:, 0:1]))

                def down(e, i):
                    for j in range(n):
                        last = e.matmul(pb[2][:, j * D:(j + 1) * D], hid[:, j * P:(j + 1) * P], wf2_s[:, :],
                                        start=True, stop=True)
                    return last
                lp.add("tensor", down)
                lp.add(V, lambda e, i: e.tensor_tensor(res[:, at(i), :], x1[:, at(i), :], tiles(pb[2], n), ALU.add))
            lp2 = two_lanes("ffn", ffn)
            ch3 = chain("norm_ffn")
            ch3.add(V, lambda e, i: e.tensor_tensor(res[:, :, :], res[:, :, :],
                                                    bc(vecs["bf2"][:, :].unsqueeze(1), full), ALU.add))
            normalise(ch3, x1, res, hs, relu=False, gain=vecs["g2"], shift=vecs["be2"])
            ch3.add(V, lambda e, i: e.tensor_tensor(xs[:, :, :], xs[:, :, :], x1[:, :, :], ALU.add))
            normalise(ch3, hs, xs, res)
            stage(ch, ch2, lp2, ch3)
        att.close()

        own = sb("own", [P, J, D])
        with ExitStack() as ctx:
            w3_s = sb("w3", [D, 4 * D], f32, ctx)
            b3_s = sb("b3", [P, D], f32, ctx)
            ch = chain("index3")
            ch.add("sync", lambda e, i: start_stores(e, s_rel, 3) or [
                                         e.dma_start(w3_s[:, :], w3),
                                         e.dma_start(b3_s[:, :], b3.partition_broadcast(P))], "hw", 2)
            def relations(lp, k, lo, n, pb):
                step = sb(f"h3_step{k}", [P, n, D], f32, ctx)
                ht = sb(f"h3_step_t{k}", [D, n * P], f32, ctx)
                rel = sb(f"relations{k}", [P, 3, n, D], f32, ctx)
                lp.add(V, lambda e, i: e.tensor_copy(step[:, :, :], hs[:, bass.ds(i * JB + lo, n), :]))
                lp.add("tensor", transposes(step, D, n, pb[0]))
                lp.add("scalar", lambda e, i: e.copy(ht[:, :], pb[0][0:D, 0:n * P]))

                def relate(e, i):
                    for j in range(n):
                        last = e.matmul(pb[1 + j // 2][:, (j % 2) * 256:(j % 2 + 1) * 256], ht[:, j * P:(j + 1) * P],
                                        w3_s[:, :], start=True, stop=True)
                    return last
                lp.add("tensor", relate)

                def evacuate(e, i):
                    e.wait_ge(s_rel[k], i * 48 + 48)
                    for j in range(n):
                        o = pb[1 + j // 2][:, (j % 2) * 256:(j % 2) * 256 + 192].rearrange("p (r f) -> p r f", f=D)
                        last = e.copy(rel[:, :, j, :], o)
                    return last
                lp.add("scalar", evacuate)

                def store(e, i):
                    for r in range(3):
                        e.dma_start(per_node(y3_d[r * NP:(r + 1) * NP, :])[:, bass.ds(i * JB + lo, n), :],
                                    rel[:, r, :, :]).then_inc(s_rel[k], 16)
                lp.add("sync", store)

                def keep(e, i):
                    for b in range(2):
                        m = min(2, n - 2 * b)
                        v = tiles(pb[1 + b], m, 256)[:, :, 192:256]
                        last = e.tensor_tensor(own[:, bass.ds(i * JB + lo + 2 * b, m), :], v,
                                               bc(b3_s[:, :].unsqueeze(1), [P, m, D]), ALU.add)
                    return last
                lp.add(V, keep)
            lp = two_lanes("relations", relations)
            ch2 = chain("relations_end")
            ch2.add("sync", lambda e, i: stored(e, s_rel, 3))
            stage(ch, lp, ch2)

        with ExitStack() as ctx:
            g = [sb(f"rows_l3_{h}", [P, HALF, D], f32, ctx) for h in range(2)]
            edge_pass("l3", y3_d, src_i, g)

        with ExitStack() as ctx:
            res = sb("rel_sum", [P, J, D], f32, ctx)
            ch = chain("nodes3")
            collect(ch, res, run_d, run[1][:, HALF - 1, :], D)
            ch.add(V, lambda e, i: e.tensor_tensor(res[:, :, :], res[:, :, :], own[:, :, :], ALU.add))
            ch.add(V, lambda e, i: e.scalar_tensor_tensor(res[:, :, :], res[:, :, :], 0.0, xs[:, :, :], ALU.max,
                                                          ALU.add))
            ch.add("sync", lambda e, i: node_rows(e, res, out, back=True), "hw", len(rows_of(PN)) + 1)
            stage(ch)


def kernel(**inputs):
    import numpy as _np
    import concourse.bacc as _bacc
    from concourse.bass_utils import run_bass_kernel_spmd as _run

    nc = _bacc.Bacc("TRN2", target_bir_lowering=False, num_devices=1)
    g = {k: _np.asarray(v) for k, v in inputs.items()}
    w_rel = g["L3_gnn_W_rel"]
    given = {
        "x": g["x"], "src": g["src"], "dst": g["dst"], "edge_attr": g["edge_attr_48"], "edge_type": g["edge_type_3"],
        "w0a": g["L0_gnn_W1"], "b0a": g["L0_gnn_b1"].reshape(2, 128).T, "w0b": g["L0_gnn_W2"], "b0b": g["L0_gnn_b2"],
        "w1": g["L1_gnn_W"], "b1": g["L1_gnn_b"],
        "watt": g["L2_gnn_W_att"], "att_s": g["L2_gnn_att_src"], "att_d": g["L2_gnn_att_dst"],
        "batt": g["L2_gnn_bias_att"], "wf1": g["L2_gnn_W1"], "bf1": g["L2_gnn_b1"].reshape(128, 1),
        "wf2": g["L2_gnn_W2"], "bf2": g["L2_gnn_b2"], "g1": g["L2_gnn_ln1_g"], "be1": g["L2_gnn_ln1_b"],
        "g2": g["L2_gnn_ln2_g"], "be2": g["L2_gnn_ln2_b"],
        "w3": _np.concatenate([w_rel[0].T, w_rel[1].T, w_rel[2].T, g["L3_gnn_W_self"].T], axis=1),
        "b3": g["L3_gnn_b_self"],
    }
    arrays, args = {}, []
    for name, a in given.items():
        a = _np.ascontiguousarray(a)
        arrays[f"in_{name}"] = a
        args.append(nc.dram_tensor(f"in_{name}", a.shape, mybir.dt.from_np(a.dtype), kind="ExternalInput").ap())
    args.append(nc.dram_tensor("out", g["x"].shape, f32, kind="ExternalOutput").ap())
    build(nc, *args)
    r = _run(nc, [arrays], core_ids=[0])
    return r.results[0]["out"]
```
